# Optimizing a Trainium2 kernel written in Bass

```python
import numpy as np
import jax
import jax.numpy as jnp

def _softmax(x, axis=-1):
    return jax.nn.softmax(x, axis=axis)

def _gelu(x):
    return jax.nn.gelu(x, approximate=True)

def _silu(x):
    return jax.nn.silu(x)

def _sigmoid(x):
    return jax.nn.sigmoid(x)

def _layernorm(x, axis=-1, eps=1e-05):
    m = jnp.mean(x, axis=axis, keepdims=True)
    v = jnp.var(x, axis=axis, keepdims=True)
    return (x - m) / jnp.sqrt(v + eps)

def _scatter_add(tgt, idx, src, axis=0):
    return tgt.at[idx].add(src)

def _segment_sum(src, seg, n):
    return jax.ops.segment_sum(src, seg, n)
kernel_name = 'mk_adaln_d1_jaxref_r4_c6e9b8'

def setup_inputs(seed: int=0):
    np.random.seed(seed)
    _w = jnp.asarray

    def _L0_attn_setup():
        import jax, jax.numpy as jnp
        import numpy as np
        N_HEADS = 16
        SEG = 64
        EPS = 1e-06

        def _sigma(x):
            return jax.nn.elu(x) + 1.0

        def _infini_attention(x, W_q, W_k, W_v, W_o, beta_param):
            B, T, D = x.shape
            H = N_HEADS
            dk = D // H
            assert T % SEG == 0
            S = T // SEG

            def proj(W):
                y = (x @ W.T).reshape(B, T, H, dk).transpose(0, 2, 1, 3)
                return y.reshape(B, H, S, SEG, dk).transpose(2, 0, 1, 3, 4)
            Qs, Ks, Vs = (proj(W_q), proj(W_k), proj(W_v))
            beta = jax.nn.sigmoid(beta_param).reshape(1, H, 1, 1)
            causal = jnp.triu(jnp.ones((SEG, SEG), dtype=bool), k=1)
            inv_sqrt_dk = 1.0 / jnp.sqrt(jnp.asarray(dk, x.dtype))
            M0 = jnp.zeros((B, H, dk, dk), dtype=x.dtype)
            z0 = jnp.zeros((B, H, dk), dtype=x.dtype)

            def step(carry, qkv):
                M, z = carry
                q, k, v = qkv
                sq = _sigma(q)
                denom_q = jnp.sum(sq * z[:, :, None, :], axis=-1, keepdims=True) + EPS
                A_mem = jnp.matmul(sq, M) / denom_q
                scores = jnp.matmul(q, jnp.swapaxes(k, -2, -1)) * inv_sqrt_dk
                scores = jnp.where(causal, -jnp.inf, scores)
                A_dot = jnp.matmul(jax.nn.softmax(scores, axis=-1), v)
                A_s = beta * A_mem + (1.0 - beta) * A_dot
                sk = _sigma(k)
                denom_k = jnp.sum(sk * z[:, :, None, :], axis=-1, keepdims=True) + EPS
                V_prev = jnp.matmul(sk, M) / denom_k
                M_new = M + jnp.einsum('bhtk,bhtv->bhkv', sk, v - V_prev)
                z_new = z + jnp.sum(sk, axis=-2)
                return ((M_new, z_new), A_s)
            (M, z), outs = jax.lax.scan(step, (M0, z0), (Qs, Ks, Vs))
            out = outs.transpose(1, 3, 0, 2, 4).reshape(B, S * SEG, H, dk)
            out = outs.transpose(1, 2, 0, 3, 4).reshape(B, H, T, dk)
            out = out.transpose(0, 2, 1, 3).reshape(B, T, D)
            out = out @ W_o.T
            return (out, M.mean(0), z.mean(0))

        def _reference_tuple_inner(x, W_q, W_k, W_v, W_o, beta_param):
            return _infini_attention(x, W_q, W_k, W_v, W_o, beta_param)
        key = jax.random.key(seed)
        kx, kq, kk, kv, ko = jax.random.split(key, 5)
        B, T, D = (4, 1024, 256)
        scale = D ** (-0.5)
        return {'x': jax.random.normal(kx, (B, T, D), dtype=jnp.float32), 'W_q': jax.random.normal(kq, (D, D), dtype=jnp.float32) * scale, 'W_k': jax.random.normal(kk, (D, D), dtype=jnp.float32) * scale, 'W_v': jax.random.normal(kv, (D, D), dtype=jnp.float32) * scale, 'W_o': jax.random.normal(ko, (D, D), dtype=jnp.float32) * scale, 'beta_param': jnp.zeros((N_HEADS,), dtype=jnp.float32)}
    _L0_attn_in = _L0_attn_setup()

    def _L0_ffn_setup():
        import jax, jax.numpy as jnp
        import numpy as np
        E, H, I, K = (8, 256, 512, 2)
        B, S = (4, 512)
        key = jax.random.key(seed)
        k1, k2, k3, k4 = jax.random.split(key, 4)
        x = jax.random.normal(k1, (B, S, H), dtype=jnp.float32)
        router_w = jax.random.uniform(k2, (E, H), dtype=jnp.float32, minval=-1.0, maxval=1.0) / np.sqrt(H).astype(np.float32)
        w13 = jax.random.normal(k3, (E, H, 2 * I), dtype=jnp.float32) * 0.02
        w2 = jax.random.normal(k4, (E, I, H), dtype=jnp.float32) * 0.02
        return {'x': x, 'router_w': router_w, 'w13': w13, 'w2': w2}
    _L0_ffn_in = _L0_ffn_setup()
    _L0_c = _w((lambda *s: np.random.randn(*s).astype(np.float32) * 0.05)(8, 256))
    _L0_wmod = _w((lambda *s: np.random.randn(*s).astype(np.float32) * 0.05)(256, 6 * 256) * 256 ** (-0.5))
    _d = {'L0_attn_x': _L0_attn_in['x'], 'L0_attn_W_q': _L0_attn_in['W_q'], 'L0_attn_W_k': _L0_attn_in['W_k'], 'L0_attn_W_v': _L0_attn_in['W_v'], 'L0_attn_W_o': _L0_attn_in['W_o'], 'L0_attn_beta_param': _L0_attn_in['beta_param'], 'L0_ffn_router_w': _L0_ffn_in['router_w'], 'L0_ffn_w13': _L0_ffn_in['w13'], 'L0_ffn_w2': _L0_ffn_in['w2'], 'L0_c': _L0_c, 'L0_wmod': _L0_wmod}
    _x0 = _d['L0_attn_x']
    _d['L0_attn_x'] = jax.random.normal(jax.random.fold_in(jax.random.key(seed), 1), (8, 1024, 256), dtype=_x0.dtype)
    del _x0
    return _d

def reference(L0_attn_x, L0_attn_W_q, L0_attn_W_k, L0_attn_W_v, L0_attn_W_o, L0_attn_beta_param, L0_ffn_router_w, L0_ffn_w13, L0_ffn_w2, L0_c, L0_wmod):

    def _L0_attn_ref(x, W_q, W_k, W_v, W_o, beta_param):
        import jax, jax.numpy as jnp
        import numpy as np
        N_HEADS = 16
        SEG = 64
        EPS = 1e-06

        def _sigma(x):
            return jax.nn.elu(x) + 1.0

        def _infini_attention(x, W_q, W_k, W_v, W_o, beta_param):
            B, T, D = x.shape
            H = N_HEADS
            dk = D // H
            assert T % SEG == 0
            S = T // SEG

            def proj(W):
                y = (x @ W.T).reshape(B, T, H, dk).transpose(0, 2, 1, 3)
                return y.reshape(B, H, S, SEG, dk).transpose(2, 0, 1, 3, 4)
            Qs, Ks, Vs = (proj(W_q), proj(W_k), proj(W_v))
            beta = jax.nn.sigmoid(beta_param).reshape(1, H, 1, 1)
            causal = jnp.triu(jnp.ones((SEG, SEG), dtype=bool), k=1)
            inv_sqrt_dk = 1.0 / jnp.sqrt(jnp.asarray(dk, x.dtype))
            M0 = jnp.zeros((B, H, dk, dk), dtype=x.dtype)
            z0 = jnp.zeros((B, H, dk), dtype=x.dtype)

            def step(carry, qkv):
                M, z = carry
                q, k, v = qkv
                sq = _sigma(q)
                denom_q = jnp.sum(sq * z[:, :, None, :], axis=-1, keepdims=True) + EPS
                A_mem = jnp.matmul(sq, M) / denom_q
                scores = jnp.matmul(q, jnp.swapaxes(k, -2, -1)) * inv_sqrt_dk
                scores = jnp.where(causal, -jnp.inf, scores)
                A_dot = jnp.matmul(jax.nn.softmax(scores, axis=-1), v)
                A_s = beta * A_mem + (1.0 - beta) * A_dot
                sk = _sigma(k)
                denom_k = jnp.sum(sk * z[:, :, None, :], axis=-1, keepdims=True) + EPS
                V_prev = jnp.matmul(sk, M) / denom_k
                M_new = M + jnp.einsum('bhtk,bhtv->bhkv', sk, v - V_prev)
                z_new = z + jnp.sum(sk, axis=-2)
                return ((M_new, z_new), A_s)
            (M, z), outs = jax.lax.scan(step, (M0, z0), (Qs, Ks, Vs))
            out = outs.transpose(1, 3, 0, 2, 4).reshape(B, S * SEG, H, dk)
            out = outs.transpose(1, 2, 0, 3, 4).reshape(B, H, T, dk)
            out = out.transpose(0, 2, 1, 3).reshape(B, T, D)
            out = out @ W_o.T
            return (out, M.mean(0), z.mean(0))

        def _reference_tuple_inner(x, W_q, W_k, W_v, W_o, beta_param):
            return _infini_attention(x, W_q, W_k, W_v, W_o, beta_param)
        return _reference_tuple_inner(x, W_q, W_k, W_v, W_o, beta_param)[0]

    def _L0_ffn_ref(x, router_w, w13, w2):
        import jax, jax.numpy as jnp
        import numpy as np
        E, H, I, K = (8, 256, 512, 2)
        B, S = (4, 512)
        logits = jnp.einsum('bsh,eh->bse', x, router_w)
        probs = jax.nn.softmax(logits, axis=-1)
        weights, indices = jax.lax.top_k(probs, K)
        weights = weights / (weights.sum(axis=-1, keepdims=True) + 1e-06)
        h13 = jnp.einsum('bsh,ehi->bsei', x, w13)
        gate, up = jnp.split(h13, 2, axis=-1)
        h = jax.nn.silu(gate) * up
        y = jnp.einsum('bsei,eih->bseh', h, w2)
        y_sel = jnp.take_along_axis(y, indices[..., None], axis=2)
        return (y_sel * weights[..., None]).sum(axis=2)
    x = L0_attn_x
    mod = (_silu(L0_c) @ L0_wmod).reshape(L0_c.shape[0], 6, 1, -1)
    sa, ca, ga, sb, cb, gb = (mod[:, 0], mod[:, 1], mod[:, 2], mod[:, 3], mod[:, 4], mod[:, 5])
    ga = (2 * (ga >= 0) - 1) * jnp.maximum(jnp.abs(ga), 0.25)
    gb = (2 * (gb >= 0) - 1) * jnp.maximum(jnp.abs(gb), 0.25)
    h = _layernorm(x, axis=-1) * (1 + ca) + sa
    x = x + ga * _L0_attn_ref(h, L0_attn_W_q, L0_attn_W_k, L0_attn_W_v, L0_attn_W_o, L0_attn_beta_param)
    h = _layernorm(x, axis=-1) * (1 + cb) + sb
    x = x + gb * _L0_ffn_ref(h, L0_ffn_router_w, L0_ffn_w13, L0_ffn_w2)
    return x

_drawn_inputs = setup_inputs


def setup_inputs(seed=0):
    import zlib

    import numpy as np

    out = dict(_drawn_inputs(seed))
    spreads = {'L0_attn_beta_param': (0.0, 0.8)}
    factors = {'L0_ffn_router_w': 8.0, 'L0_ffn_w13': 8.0, 'L0_ffn_w2': 8.0}
    for name, (base, spread) in spreads.items():
        noise = np.random.default_rng([zlib.crc32(name.encode()), seed]).standard_normal(out[name].shape)
        drawn = base * np.exp(spread * noise) if base else spread * noise
        out[name] = jnp.asarray(drawn.astype(out[name].dtype))
    for name, factor in factors.items():
        out[name] = (out[name] * factor).astype(out[name].dtype)
    return out
```

```python
from contextlib import ExitStack

import numpy as np

import concourse.bass as bass
from concourse import mybir

F32 = mybir.dt.float32
F16 = mybir.dt.float16
BF16 = mybir.dt.bfloat16
I32 = mybir.dt.int32
ALU = mybir.AluOpType
ACT = mybir.ActivationFunctionType
X = mybir.AxisListType.X

P = 128
B, T, D = 8, 1024, 256
H, DK, SEG = 16, 16, 64
NJ = B // 2
NS = T // SEG
NT = NJ * NS
G = D // P
HG = P // DK
MW = P + HG
NPAIR = H // 2
VW = 2 * DK + 1
E, I = 8, 512
NSLOT_TILES = (B * T * 2) // P + E - 1
KC = I // P
W_SCALE = 32.0
EPS_LN, EPS_MEM, EPS_TOP = 1e-5, 1e-6, 1e-6
NEG = -1e30
PRE = 4
PARTS = ((0, 0), (0, 1), (1, 0))
OOB = B * T + 4096


def bc(ap, n):
    return ap.unsqueeze(2).to_broadcast([ap.shape[0], ap.shape[1], n])


def bc_mid(ap, n):
    return ap.unsqueeze(1).to_broadcast([ap.shape[0], n, ap.shape[1]])


def apart(e, passed, waits):
    for s, v in waits:
        if not (isinstance(v, int) and v <= 0):
            e.wait_ge(s, v)
    e.sem_inc(passed, 1)


def adaln_block(nc, x, cT, wmod, wqT, wkT, wvT, woT, beta, rwT, w13, w2, ident, head_of_row, mem_mask,
                q_onehot, causal, tri, iotas, tok_a, tok_b, out):
    rows_dram = nc.dram_tensor("moe_rows", [B * T, 2 * D + 2 * D], F16, kind="Internal").ap()
    w8_dram = nc.dram_tensor("top2_weights", [B * T, E], F32, kind="Internal").ap()
    out_rows = out.rearrange("b t d -> (b t) d")

    with ExitStack() as whole:
        def sb(name, shape, dt=F32, ctx=whole):
            return ctx.enter_context(nc.sbuf_tensor(name, shape, dt))

        def sem(name, ctx=whole):
            return ctx.enter_context(nc.semaphore(name))

        passed = sem("passed")
        w13s = sb("w13s", [P, 2, E * G * 2 * I], F16)
        idf = sb("idf", [P, P])
        idh = sb("idh", [P, P], F16)
        logits = sb("logits", [P, E, NT])
        banks = [whole.enter_context(nc.psum_tensor(f"bank{i}", [P, 512], F32)) for i in range(8)]

        with ExitStack() as att:
            attention(nc, att, sb, sem, banks, x, cT, wmod, wqT, wkT, wvT, woT, beta, rwT, w13, ident,
                      head_of_row, mem_mask, q_onehot, causal, out, rows_dram, w13s, idf, idh, logits, passed)
        with ExitStack() as moe:
            experts(nc, moe, sb, sem, banks, tri, iotas, tok_a, tok_b, out_rows, rows_dram, w8_dram,
                    w13s, w2, idh, logits, passed)


def attention(nc, ctx, sb_, sem_, banks, x, cT, wmod, wqT, wkT, wvT, woT, beta, rwT, w13, ident,
              head_of_row, mem_mask, q_onehot, causal, out, rows_dram, w13s, idf, idh, logits, passed):
    def sb(name, shape, dt=F32):
        return sb_(name, shape, dt, ctx)

    def sem(name):
        return sem_(name, ctx)

    wqk = sb("wqk", [P, G, 2 * D])
    wv = sb("wv", [P, G, D])
    wo = sb("wo", [P, G, D])
    rw = sb("rw", [P, G, E])
    hrow = sb("hrow", [P, 4])
    mmask = sb("mmask", [P, MW])
    onehot = sb("onehot", [P, P], BF16)
    cmask = sb("cmask", [P, 8 * SEG], BF16)
    mods = sb("mods", [P, 5, NJ, D])
    sA, sCA, sGA, sB2, sCB, sGB = range(6)
    beta_m = sb("beta_m", [P, H])
    om_beta = sb("om_beta", [P, NPAIR])
    mhalf = sb("mhalf", [P, 1])

    vs = sb("vs", [P, 4, 2, NPAIR, VW], F16)
    vp = sb("vp", [P, 2, G, MW])
    mem = sb("mem", [P, NJ, 2, G, MW])
    hrows = sb("hrows", [P, 4, 4 * D], F16)

    set_up = ExitStack()
    cs = sb_("cs", [P, G, B], F32, set_up)
    crep = sb_("crep", [P, G, B, SEG], F32, set_up)
    btile = sb_("btile", [P, H], F32, set_up)
    wmod_sb = sb_("wmod_sb", [P, G, 6 * D], F32, set_up)
    stage = sb_("stage", [P, 2, 1024], F32, set_up)
    gate_sign = sb_("gate_sign", [P, 512], F32, set_up)

    bkA, bkB, bkC, bkD, bkE, bkF, bkG, bkH = banks

    s_ld, s_w = sem("s_ld"), [sem("s_w0"), sem("s_w1")]
    s_c, s_set, s_mod, s_mev = sem("s_c"), sem("s_set"), sem("s_mod"), sem("s_mev")
    s_hi, s_lo, s_gb = sem("s_hi"), sem("s_lo"), sem("s_gb")

    loads = [(wmod_sb[:, :, :], wmod.rearrange("(c p) n -> p c n", p=P)),
             (cs[:, :, :], cT.rearrange("(c p) b -> p c b", p=P)),
             (idf[:, :], ident), (hrow[:, :], head_of_row), (mmask[:, :], mem_mask),
             (wv[:, :, :], wvT.rearrange("(c p) n -> p c n", p=P)),
             (wo[:, :, :], woT.rearrange("(c p) n -> p c n", p=P)),
             (rw[:, :, :], rwT.rearrange("(c p) n -> p c n", p=P)),
             (wqk[:, :, 0:D], wqT.rearrange("(c p) n -> p c n", p=P)),
             (wqk[:, :, D:2 * D], wkT.rearrange("(c p) n -> p c n", p=P)),
             (btile[:, :], beta.rearrange("(a h) -> a h", a=1).to_broadcast([P, H])),
             (onehot[:, :], q_onehot), (cmask[:, :], causal)]
    chunks = [(w13[e, c * P:(c + 1) * P, :], w13s, (e * G + c) * 1024) for e in range(E) for c in range(G)]

    with nc.Block() as block:
        @block.gpsimd
        def _(e):
            for dst, src in loads:
                e.dma_start(dst, src).then_inc(s_ld, 16)
            e.memset(mem[:, :, :, :, :], 0.0).then_inc(s_c, 1)
            e.memset(mhalf[:, :], -0.5).then_inc(s_c, 1)
            for b_ in range(4):
                e.memset(vs[:, b_, 0, :, 2 * DK:VW], 1.0).then_inc(s_c, 1)
                e.memset(vs[:, b_, 1, :, 2 * DK:VW], 0.0).then_inc(s_c, 1)
            for b_ in range(2):
                e.memset(vp[:, b_, :, P:MW], 1.0).then_inc(s_c, 1)

        @block.sync
        def _(e):
            for n, (src, _, _) in enumerate(chunks):
                if n >= 2:
                    e.wait_ge(s_lo, n - 1)
                e.dma_start(stage[:, n % 2, :], src).then_inc(s_w[n % 2], 16)

        @block.scalar
        def _(e):
            e.wait_ge(s_ld, 16 * len(loads))
            e.activation(cs[:, :, :], cs[:, :, :], ACT.Silu).then_inc(s_set, 1)
            e.activation(btile[:, :], btile[:, :], ACT.Exp, scale=-1.0).then_inc(s_set, 1)
            e.activation(idh[:, :], idf[:, :], ACT.Copy).then_inc(s_set, 1)
            for n, (_, dst, at) in enumerate(chunks):
                e.wait_ge(s_w[n % 2], 16 * (n // 2 + 1))
                e.activation(dst[:, 0, at:at + 1024], stage[:, n % 2, :], ACT.Copy, scale=W_SCALE).then_inc(s_hi, 1)

        @block.vector
        def _(e):
            e.wait_ge(s_set, 3)
            e.tensor_copy(crep[:, :, :, :].rearrange("p c b t -> p (c b) t"),
                          bc(cs[:, :, :].rearrange("p c b -> p (c b)"), SEG)).then_inc(s_gb, 1)
            e.tensor_scalar(btile[:, :], btile[:, :], 1.0, None, ALU.add).then_inc(s_gb, 1)
            e.wait_ge(s_gb, 2)
            e.reciprocal(btile[:, :], btile[:, :]).then_inc(s_gb, 1)
            e.memset(beta_m[SEG:P, :], 1.0)
            e.wait_ge(s_gb, 3)
            e.tensor_copy(beta_m[0:SEG, :], btile[0:SEG, :]).then_inc(s_gb, 1)
            pair = btile[:, :].rearrange("p (n two) -> p two n", two=2)
            for par in range(2):
                rows = slice(par * SEG, (par + 1) * SEG)
                e.tensor_scalar(om_beta[rows, :], pair[rows, par, :], -1.0, 1.0, ALU.mult, ALU.add).then_inc(s_gb, 1)
            link = 6
            for n in range(6 * NJ // 2):
                k, jj = n // 2, n % 2
                bank = banks[n % 2][:, :].rearrange("p (j d) -> p j d", j=2)
                e.wait_ge(s_mod, n + 1)
                if k == sGB:
                    dst = hrows[:, 2 * jj:2 * jj + 2, 2 * D:4 * D].bitcast(F32)
                else:
                    dst = mods[:, k, 2 * jj:2 * jj + 2, :]
                if k in (sCA, sCB):
                    e.tensor_scalar(dst, bank, 1.0, None, ALU.add).then_inc(s_mev, 1)
                elif k in (sGA, sGB):
                    e.wait_ge(s_mev, n)
                    tmp = gate_sign[:, :].rearrange("p (j d) -> p j d", j=2)
                    e.tensor_scalar(tmp, bank, 0.0, None, ALU.is_ge).then_inc(s_gb, 1)
                    e.wait_ge(s_gb, link + 1)
                    e.tensor_scalar(tmp, tmp, 2.0, -1.0, ALU.mult, ALU.add).then_inc(s_gb, 1)
                    e.wait_ge(s_gb, link + 2)
                    e.tensor_tensor(dst, bank, tmp, ALU.mult).then_inc(s_gb, 1)
                    e.wait_ge(s_gb, link + 3)
                    e.scalar_tensor_tensor(out=dst, in0=dst, scalar=0.25, in1=tmp, op0=ALU.max,
                                           op1=ALU.mult).then_inc(s_mev, 1)
                    link += 3
                else:
                    e.tensor_copy(dst, bank).then_inc(s_mev, 1)
            for n, (_, dst, at) in enumerate(chunks):
                e.wait_ge(s_hi, n + 1)
                e.scalar_tensor_tensor(out=dst[:, 1, at:at + 1024], in0=stage[:, n % 2, :], scalar=W_SCALE,
                                       in1=dst[:, 0, at:at + 1024], op0=ALU.mult, op1=ALU.subtract).then_inc(s_lo, 1)

        @block.tensor
        def _(e):
            e.wait_ge(s_gb, 1)
            e.wait_ge(s_ld, 16 * len(loads))
            for n in range(6 * NJ // 2):
                k, jj = n // 2, n % 2
                if n >= 2:
                    e.wait_ge(s_mev, n - 1)
                for q in range(2):
                    j = 2 * jj + q
                    for c in range(G):
                        mm = e.matmul(banks[n % 2][:, q * D:(q + 1) * D],
                                      crep[:, c, 2 * j:2 * j + 2, :].rearrange("p b t -> p (b t)"),
                                      wmod_sb[:, c, k * D:(k + 1) * D], start=(c == 0), stop=(c == G - 1))
                mm.then_inc(s_mod, 1)

    set_up.close()

    xin = sb("xin", [P, 4, D])
    bst = sb("bst", [P, 4, 6])
    mv = sb("mv", [P, 4, 2])
    rstd = sb("rstd", [P, 4, 1])
    h1 = sb("h1", [P, 2, D])
    h1T = sb("h1T", [P, 2, G, P])
    qk = sb("qk", [P, 2, 2, 2 * D], F16)
    qm = sb("qm", [P, 2, 2, 4, 4, SEG], F16)
    ex = sb("ex", [P, 512])
    sig = sb("sig", [P, 2, G, 2, 2, SEG])
    v32 = sb("v32", [P, 2, D])
    mx = sb("mx", [P, 2, 16])
    sc = sb("sc", [P, 2, 16, SEG])
    pT = sb("pT", [P, 2, 2, 8, P], F16)
    rr = sb("rr", [P, 2, 2, NPAIR])
    att_o = sb("att_o", [P, 2, D])
    dd = sb("dd", [P, 2, 2, H])
    memA = sb("memA", [P, 4, D])
    skt = sb("skt", [P, 2, D])
    upd = sb("upd", [P, 2, G, MW])
    aT = sb("aT", [P, 2, G, P])
    xres = sb("xres", [P, 2, D])
    x1 = sb("x1", [P, 4, D])
    bst2 = sb("bst2", [P, 4, 6])
    mv2 = sb("mv2", [P, 4, 2])
    rstd2 = sb("rstd2", [P, 4, 1])
    h2 = sb("h2", [P, 2, D])
    h2T = sb("h2T", [P, 2, G, P])

    names = ("stats aggr eps pow lna lnb T1 h1T pqk pv qkh exq v32 vhi vlo qlo mn sig qm scr mx sub exp "
             "PTr ptA ptB ptl memm den rec bet mA mV vpr skT skt upm umul madd PV rcp rom ado aadd AT aT Wo "
             "gat res st2 ag2 ep2 pw2 l2a l2b hhi hlo h2Tr h2T rtr lg").split()
    S = {n: sem("a_" + n) for n in names}
    s_x = [sem(f"s_x{j}") for j in range(4)]
    s_xr = [sem(f"s_xr{j}") for j in range(4)]
    s_st = [sem(f"s_st{j}") for j in range(4)]

    class Tile:

        def __init__(self, e, s, j):
            self.e, self.s, self.j, self.b = e, s, j, j % 2
            self.t = s * 4 + j

        def when(self, stage, back=0):
            if isinstance(self.s, int):
                of = min(self.t - back, NT - 1)
                return S[stage], max(of, -1) + 1 + PRE
            return S[stage], self.s * 4 + (self.j - back + 1 + PRE)

        def wait(self, stage, back=0):
            if not isinstance(self.s, int) or self.t >= back:
                self.e.wait_ge(*self.when(stage, back))

        def wait_end(self, stage, back):
            if isinstance(self.s, int):
                self.wait(stage, back)

        def wait_apart(self, *stages):
            apart(self.e, passed, [self.when(*w) for w in stages])

        def arrived(self, sems, n=1):
            self.e.wait_ge(sems[self.j], self.s * (16 * n) + 16 * n)

        def stored(self):
            if not isinstance(self.s, int) or self.s > 0:
                self.e.wait_ge(s_st[self.j], self.s * 64)

    def done(ins, stage):
        ins.then_inc(S[stage], 1)

    def load_x(k):
        k.wait("lna", 4)
        k.wait("stats", 4)
        for b2 in range(2):
            k.e.dma_start(xin[b2 * SEG:(b2 + 1) * SEG, k.j, :],
                          x[2 * k.j + b2, bass.ds(k.s * SEG, SEG), :]).then_inc(s_x[k.j], 16)

    def load_res(k):
        k.wait("res", 2)
        for b2 in range(2):
            k.e.dma_start(xres[b2 * SEG:(b2 + 1) * SEG, k.b, :],
                          x[2 * k.j + b2, bass.ds(k.s * SEG, SEG), :]).then_inc(s_xr[k.j], 16)

    def store(k):
        k.wait_apart(("hlo",))
        for b2 in range(2):
            rows = slice(b2 * SEG, (b2 + 1) * SEG)
            k.e.dma_start(out[2 * k.j + b2, bass.ds(k.s * SEG, SEG), :], x1[rows, k.j, :]).then_inc(s_st[k.j], 16)
            k.e.dma_start(rows_dram[bass.ds(k.s * SEG + (2 * k.j + b2) * T, SEG), :],
                          hrows[rows, k.j, :]).then_inc(s_st[k.j], 16)

    def stats(k):
        k.arrived(s_x, 2)
        k.wait("aggr", 4)
        done(k.e.bn_stats(bst[:, k.j, :], xin[:, k.j, :]), "stats")
        k.wait_apart(("stats",), ("lna", 4))
        done(k.e.bn_aggr(mv[:, k.j, :], bst[:, k.j, :]), "aggr")
        k.wait("aggr")
        k.wait("lnb", 4)
        done(k.e.tensor_scalar(rstd[:, k.j, :], mv[:, k.j, 1:2], EPS_LN, None, ALU.add), "eps")

    def pw(k):
        k.wait("eps")
        done(k.e.tensor_tensor(rstd[:, k.j, :], rstd[:, k.j, :], mhalf[:, :], ALU.pow), "pow")

    def ln(k):
        k.wait("T1", 2)
        done(k.e.scalar_tensor_tensor(out=h1[:, k.b, :], in0=xin[:, k.j, :], scalar=mv[:, k.j, 0:1],
                                      in1=mods[:, sCA, k.j, :], op0=ALU.subtract, op1=ALU.mult), "lna")
        k.wait("pow")
        k.wait("lna")
        done(k.e.scalar_tensor_tensor(out=h1[:, k.b, :], in0=h1[:, k.b, :], scalar=rstd[:, k.j, :],
                                      in1=mods[:, sA, k.j, :], op0=ALU.mult, op1=ALU.add), "lnb")

    def t1(k):
        k.wait("lnb")
        k.wait("lg", 9)
        for c in range(G):
            i = k.e.transpose(bkA[:, c * P:(c + 1) * P], h1[:, k.b, c * P:(c + 1) * P], idf[:, :])
        done(i, "T1")

    def h1t(k):
        k.wait("T1")
        k.wait("pv", 2)
        done(k.e.activation(h1T[:, k.b, :, :].rearrange("p c t -> p (c t)"), bkA[:, 0:D], ACT.Copy), "h1T")

    def proj(k):
        k.wait("h1T")
        k.wait("umul", 3)
        for n in range(4):
            for c in range(G):
                i = k.e.matmul(bkB[:, n * P:(n + 1) * P], wqk[:, c, n * P:(n + 1) * P], h1T[:, k.b, c, :],
                               start=(c == 0), stop=(c == G - 1))
        done(i, "pqk")
        for c in range(G):
            i = k.e.matmul(bkC[:, 0:D], h1T[:, k.b, c, :], wv[:, c, :], start=(c == 0), stop=(c == G - 1))
        done(i, "pv")

    def proj_act(k):
        k.wait("pqk")
        k.wait("scr", 2)
        k.wait("qm", 2)
        k.wait("qlo", 2)
        done(k.e.activation(qk[:, k.b, 0, :], bkB[:, :], ACT.Copy), "qkh")
        k.wait("sig", 1)
        done(k.e.activation(ex[:, :], bkB[:, :], ACT.Exp), "exq")
        k.wait("pv")
        k.wait("vpr", 2)
        k.wait("vlo", 2)
        done(k.e.activation(v32[:, k.b, :], bkC[:, 0:D], ACT.Copy), "v32")
        k.wait("PV", 4)
        k.wait("vlo", 4)
        k.wait("v32")
        done(k.e.activation(vs[:, k.j, 0, :, 0:2 * DK], v32[:, k.b, :].rearrange("p (n w) -> p n w", w=2 * DK),
                            ACT.Copy), "vhi")

    def v_rest(k):
        k.wait("vhi")
        k.wait("PV", 4)
        done(k.e.tensor_tensor(vs[:, k.j, 1, :, 0:2 * DK], v32[:, k.b, :].rearrange("p (n w) -> p n w", w=2 * DK),
                               vs[:, k.j, 0, :, 0:2 * DK], ALU.subtract), "vlo")

    def proj_dve(k):
        k.wait("qkh")
        k.wait("exq")
        k.wait("scr", 2)
        done(k.e.tensor_tensor(qk[:, k.b, 1, :], bkB[:, :], qk[:, k.b, 0, :], ALU.subtract), "qlo")
        done(k.e.tensor_scalar(ex[:, :], ex[:, :], 1.0, None, ALU.min), "mn")
        k.wait("mn")
        k.wait("memm", 2)
        k.wait("skT", 2)
        for a in range(2):
            i = k.e.scalar_tensor_tensor(
                out=sig[:, k.b, :, :, a, :].rearrange("p g b t -> p (g b) t"),
                in0=bkB[:, a * D:(a + 1) * D].rearrange("p (n t) -> p n t", t=SEG), scalar=0.0,
                in1=ex[:, a * D:(a + 1) * D].rearrange("p (n t) -> p n t", t=SEG), op0=ALU.max, op1=ALU.add)
        done(i, "sig")

    def q_masks(k):
        k.wait("qlo")
        k.wait("qkh")
        k.wait("scr", 2)
        for m in range(4):
            i = k.e.tensor_scalar(qm[:, k.b, :, :, m, :], qk[:, k.b, :, 0:D].rearrange("p a (n t) -> p a n t", t=SEG),
                                  hrow[:, m:m + 1], None, ALU.mult)
        done(i, "qm")

    def scores(k):
        k.wait("qm")
        k.wait("qlo")
        k.wait("ado", 3)
        for half, bank in enumerate((bkD, bkE)):
            r = slice(half * SEG, (half + 1) * SEG)
            k.e.matmul(bank[:, :], onehot[r, :], cmask[r, :], start=True, stop=False, skip_group_check=True)
            for g in range(G):
                for u in range(2):
                    for b2 in range(2):
                        n = (g * 2 + u) * 2 + b2
                        keys = slice(D + g * P + b2 * SEG, D + g * P + (b2 + 1) * SEG)
                        for a, b_ in PARTS:
                            i = k.e.matmul(bank[:, n * SEG:(n + 1) * SEG],
                                           qm[r, k.b, a, g * 2 + b2, 2 * u:2 * u + 2, :].rearrange("p m t -> p (m t)"),
                                           qk[r, k.b, b_, keys], start=False,
                                           stop=(n == 7 and (a, b_) == PARTS[-1]), skip_group_check=True)
        done(i, "scr")

    def softmax_dve(k):
        k.wait("scr")
        k.wait("sub", 2)
        for half, bank in enumerate((bkD, bkE)):
            i = k.e.tensor_reduce(mx[:, k.b, half * 8:(half + 1) * 8], bank[:, :].rearrange("p (n k) -> p n k", k=SEG),
                                  axis=X, op=ALU.max)
        done(i, "mx")
        k.wait("mx")
        k.wait("PTr", 2)
        k.wait("exp", 2)
        for half, bank in enumerate((bkD, bkE)):
            i = k.e.tensor_tensor(sc[:, k.b, half * 8:(half + 1) * 8, :], bank[:, :].rearrange("p (n k) -> p n k", k=SEG),
                                  bc(mx[:, k.b, half * 8:(half + 1) * 8], SEG), ALU.subtract)
        done(i, "sub")

    def softmax_act(k):
        k.wait("sub")
        flat = sc[:, k.b, :, :].rearrange("p n k -> p (n k)")
        done(k.e.activation(flat, flat, ACT.Exp, scale=DK ** -0.5), "exp")

    def p_trans(k):
        k.wait("exp")
        k.wait("mA", -1)
        k.wait("mV", -1)
        k.wait_end("ptl", 1)
        for n in range(8):
            bank = (bkF, bkG)[n // 4]
            i = k.e.transpose(bank[:, (n % 4) * P:(n % 4 + 1) * P],
                              sc[:, k.b, 2 * n:2 * n + 2, :].rearrange("p n k -> p (n k)"), idf[:, :])
        done(i, "PTr")

    def pt_act(k):
        k.wait("PTr")
        k.wait("PV", 2)
        k.wait("ptl", 2)
        done(k.e.activation(pT[:, k.b, 0, 0:4, :].rearrange("p n t -> p (n t)"), bkF[:, :], ACT.Copy), "ptA")
        done(k.e.activation(pT[:, k.b, 0, 4:8, :].rearrange("p n t -> p (n t)"), bkG[:, :], ACT.Copy), "ptB")

    def pt_dve(k):
        k.wait("PV", 2)
        k.wait("ptA")
        k.e.tensor_tensor(pT[:, k.b, 1, 0:4, :].rearrange("p n t -> p (n t)"), bkF[:, :],
                          pT[:, k.b, 0, 0:4, :].rearrange("p n t -> p (n t)"), ALU.subtract)
        k.wait("ptB")
        done(k.e.tensor_tensor(pT[:, k.b, 1, 4:8, :].rearrange("p n t -> p (n t)"), bkG[:, :],
                               pT[:, k.b, 0, 4:8, :].rearrange("p n t -> p (n t)"), ALU.subtract), "ptl")

    def mem_mm(k):
        k.wait("sig")
        k.wait("madd", 4)
        k.wait("ptl", 2)
        for b2, bank in enumerate((bkF, bkG)):
            for g in range(G):
                i = k.e.matmul(bank[:, g * MW:(g + 1) * MW], sig[:, k.b, g, b2, :, :].rearrange("p a t -> p (a t)"),
                               mem[:, k.j, b2, g, :], start=True, stop=True)
        done(i, "memm")

    def mem_dve(k):
        k.wait("memm")
        k.wait("mA", 2)
        k.wait("mV", 2)
        fg = [bank[:, 0:G * MW].rearrange("p (g w) -> p g w", w=MW) for bank in (bkF, bkG)]
        for b2 in range(2):
            i = k.e.tensor_scalar(dd[:, k.b, b2, :].rearrange("p (g h) -> p g h", g=G), fg[b2][:, :, P:MW],
                                  EPS_MEM, None, ALU.add)
        done(i, "den")
        k.wait("den")
        flat = dd[:, k.b, :, :].rearrange("p b h -> p (b h)")
        done(k.e.reciprocal(flat, flat), "rec")
        k.wait("rec")
        done(k.e.tensor_tensor(dd[:, k.b, :, :], dd[:, k.b, :, :], bc_mid(beta_m[:, :], 2), ALU.mult), "bet")
        k.wait("bet")
        k.wait("upm", 2)
        for b2 in range(2):
            i = k.e.tensor_tensor(
                vp[b2 * SEG:(b2 + 1) * SEG, k.b, :, 0:P].rearrange("p g (h d) -> p g h d", h=HG),
                fg[b2][SEG:P, :, 0:P].rearrange("p g (h d) -> p g h d", d=DK),
                dd[SEG:P, k.b, b2, :].rearrange("p (g h) -> p g h", g=G).unsqueeze(3).to_broadcast([SEG, G, HG, DK]),
                ALU.mult)
        done(i, "mV")
        k.wait("aadd", 4)
        for b2 in range(2):
            i = k.e.tensor_tensor(
                memA[b2 * SEG:(b2 + 1) * SEG, k.j, :].rearrange("p (g h d) -> p g h d", g=G, h=HG),
                fg[b2][0:SEG, :, 0:P].rearrange("p g (h d) -> p g h d", d=DK),
                dd[0:SEG, k.b, b2, :].rearrange("p (g h) -> p g h", g=G).unsqueeze(3).to_broadcast([SEG, G, HG, DK]),
                ALU.mult)
        done(i, "mA")

    def v_new(k):
        k.wait("mV")
        k.wait("v32")
        k.wait("upm", 2)
        done(k.e.tensor_tensor(vp[:, k.b, :, 0:P], v32[:, k.b, :].rearrange("p (g w) -> p g w", g=G),
                               vp[:, k.b, :, 0:P], ALU.subtract), "vpr")

    def sk_trans(k):
        k.wait_apart(("sig",), ("gat", 5))
        for b2 in range(2):
            for g in range(G):
                i = k.e.transpose(bkH[0:SEG, b2 * D + g * P:b2 * D + (g + 1) * P], sig[:, k.b, g, b2, 1, :], idf[:, :])
        done(i, "skT")

    def sk_act(k):
        k.wait("skT")
        k.wait("upm", 2)
        for b2 in range(2):
            i = k.e.activation(skt[b2 * SEG:(b2 + 1) * SEG, k.b, :], bkH[0:SEG, b2 * D:(b2 + 1) * D], ACT.Copy)
        done(i, "skt")

    def update(k):
        k.wait("vpr")
        k.wait("skt")
        k.wait("sig", -2)
        k.wait("v32", -2)
        k.wait_end("umul", 1)
        for b2, bank in enumerate((bkB, bkC)):
            r = slice(b2 * SEG, (b2 + 1) * SEG)
            for g in range(G):
                i = k.e.matmul(bank[:, g * MW:(g + 1) * MW], skt[r, k.b, g * P:(g + 1) * P], vp[r, k.b, g, :],
                               start=True, stop=True)
        done(i, "upm")

    def update_dve(k):
        k.wait("upm")
        k.wait("madd", 1)
        for b2, bank in enumerate((bkB, bkC)):
            i = k.e.tensor_tensor(upd[:, b2, :, :], bank[:, 0:G * MW].rearrange("p (g w) -> p g w", w=MW),
                                  bc_mid(mmask[:, :], G), ALU.mult)
        done(i, "umul")

    def update_add(k):
        k.wait("umul")
        k.wait("memm")
        flat = mem[:, k.j, :, :, :].rearrange("p b g w -> p (b g w)")
        done(k.e.tensor_tensor(flat, flat, upd[:, :, :, :].rearrange("p b g w -> p (b g w)"), ALU.add), "madd")

    def pv(k):
        k.wait("ptl")
        k.wait("vlo")
        k.wait("sub", -2)
        k.wait_end("ado", 1)
        for b2, bank in enumerate((bkD, bkE)):
            r = slice(b2 * SEG, (b2 + 1) * SEG)
            for half in range(2):
                for gu in range(4):
                    pair = (gu // 2) * 4 + half * 2 + gu % 2
                    for a, b_ in PARTS:
                        i = k.e.matmul(bank[:, pair * VW:(pair + 1) * VW], pT[r, k.b, a, half * 4 + gu, :],
                                       vs[r, k.j, b_, pair, :], start=((a, b_) == PARTS[0]),
                                       stop=((a, b_) == PARTS[-1]))
        done(i, "PV")

    def pv_dve(k):
        k.wait("PV")
        k.wait("ado", 2)
        de = [bank[:, 0:NPAIR * VW].rearrange("p (n w) -> p n w", w=VW) for bank in (bkD, bkE)]
        for b2 in range(2):
            i = k.e.reciprocal(rr[:, k.b, b2, :], de[b2][:, :, 2 * DK])
        done(i, "rcp")
        k.wait("rcp")
        done(k.e.tensor_tensor(rr[:, k.b, :, :], rr[:, k.b, :, :], bc_mid(om_beta[:, :], 2), ALU.mult), "rom")
        k.wait("rom")
        k.wait("AT", 2)
        k.wait("aadd", 2)
        for b2 in range(2):
            for par in range(2):
                r = slice(par * SEG, (par + 1) * SEG)
                i = k.e.tensor_tensor(
                    att_o[b2 * SEG:(b2 + 1) * SEG, k.b, :].rearrange("p (n w) -> p n w", w=2 * DK)[:, :, par * DK:(par + 1) * DK],
                    de[b2][r, :, par * DK:(par + 1) * DK], bc(rr[r, k.b, b2, :], DK), ALU.mult)
        done(i, "ado")

    def a_add(k):
        k.wait("ado")
        k.wait("mA")
        done(k.e.tensor_tensor(att_o[:, k.b, :], att_o[:, k.b, :], memA[:, k.j, :], ALU.add), "aadd")

    def a_trans(k):
        k.wait("aadd")
        k.wait("h1T", -5)
        k.wait_end("lg", 4)
        for c in range(G):
            i = k.e.transpose(bkA[:, c * P:(c + 1) * P], att_o[:, k.b, c * P:(c + 1) * P], idf[:, :])
        done(i, "AT")

    def a_act(k):
        k.wait("AT")
        k.wait("Wo", 2)
        done(k.e.activation(aT[:, k.b, :, :].rearrange("p c t -> p (c t)"), bkA[:, 0:D], ACT.Copy), "aT")

    def w_o(k):
        k.wait("aT")
        k.wait("skt", -4)
        k.wait("gat", 1)
        for c in range(G):
            i = k.e.matmul(bkH[:, 0:D], aT[:, k.b, c, :], wo[:, c, :], start=(c == 0), stop=(c == G - 1))
        done(i, "Wo")

    def resid(k):
        k.wait("Wo")
        k.wait("l2a", 4)
        k.stored()
        done(k.e.tensor_tensor(x1[:, k.j, :], bkH[:, 0:D], mods[:, sGA, k.j, :], ALU.mult), "gat")
        k.arrived(s_xr, 2)
        k.wait("gat")
        done(k.e.tensor_tensor(x1[:, k.j, :], x1[:, k.j, :], xres[:, k.b, :], ALU.add), "res")
        k.wait("res")
        done(k.e.bn_stats(bst2[:, k.j, :], x1[:, k.j, :]), "st2")
        k.wait_apart(("st2",), ("l2a", 4))
        done(k.e.bn_aggr(mv2[:, k.j, :], bst2[:, k.j, :]), "ag2")
        k.wait("ag2")
        k.wait("l2b", 4)
        done(k.e.tensor_scalar(rstd2[:, k.j, :], mv2[:, k.j, 1:2], EPS_LN, None, ALU.add), "ep2")

    def pw2(k):
        k.wait("ep2")
        done(k.e.tensor_tensor(rstd2[:, k.j, :], rstd2[:, k.j, :], mhalf[:, :], ALU.pow), "pw2")

    def ln2(k):
        k.wait("h2Tr", 2)
        k.wait("hhi", 2)
        k.wait("hlo", 2)
        done(k.e.scalar_tensor_tensor(out=h2[:, k.b, :], in0=x1[:, k.j, :], scalar=mv2[:, k.j, 0:1],
                                      in1=mods[:, sCB, k.j, :], op0=ALU.subtract, op1=ALU.mult), "l2a")
        k.wait("pw2")
        k.wait("l2a")
        done(k.e.scalar_tensor_tensor(out=h2[:, k.b, :], in0=h2[:, k.b, :], scalar=rstd2[:, k.j, :],
                                      in1=mods[:, sB2, k.j, :], op0=ALU.mult, op1=ALU.add), "l2b")

    def rows_hi(k):
        k.wait("l2b")
        k.stored()
        done(k.e.activation(hrows[:, k.j, 0:D], h2[:, k.b, :], ACT.Copy), "hhi")

    def rows_lo(k):
        k.wait("hhi")
        done(k.e.tensor_tensor(hrows[:, k.j, D:2 * D], h2[:, k.b, :], hrows[:, k.j, 0:D], ALU.subtract), "hlo")

    def h2_trans(k):
        k.wait("l2b")
        k.wait("aT", -3)
        k.wait_end("lg", 1)
        for c in range(G):
            i = k.e.transpose(bkA[:, c * P:(c + 1) * P], h2[:, k.b, c * P:(c + 1) * P], idf[:, :])
        done(i, "h2Tr")

    def h2_act(k):
        k.wait("h2Tr")
        k.wait("rtr", 2)
        done(k.e.activation(h2T[:, k.b, :, :].rearrange("p c t -> p (c t)"), bkA[:, 0:D], ACT.Copy), "h2T")

    def router(k):
        k.wait("h2T")
        for c in range(G):
            i = k.e.matmul(bkA[:, D:D + E], h2T[:, k.b, c, :], rw[:, c, :], start=(c == 0), stop=(c == G - 1))
        done(i, "rtr")

    def logit_copy(k):
        k.wait("rtr")
        done(k.e.activation(logits[:, :, bass.ds(k.t, 1)].rearrange("p e o -> p (e o)"), bkA[:, D:D + E], ACT.Copy), "lg")

    LAST = 9
    program = {
        "sync": [(0, load_x), (6, load_res), (LAST + 2, store)],
        "tensor": [(3, scores), (2, proj), (3, mem_mm), (3, sk_trans), (1, t1), (6, a_trans), (5, pv),
                   (7, w_o), (4, p_trans), (4, update), (9, h2_trans), (9, router)],
        "vector": [(3, softmax_dve), (2, proj_dve), (3, mem_dve), (2, q_masks), (5, pv_dve), (0, stats),
                   (7, resid), (4, pt_dve), (4, update_dve), (0, ln), (8, ln2)],
        "scalar": [(2, proj_act), (3, sk_act), (1, h1t), (3, softmax_act), (6, a_act), (4, pt_act),
                   (8, rows_hi), (9, h2_act), (9, logit_copy)],
        "gpsimd": [(2, v_rest), (3, v_new), (5, a_add), (0, pw), (7, pw2), (4, update_add), (8, rows_lo)],
    }

    def engine_program(name, e):
        stages = program[name]
        deepest = max(lag for lag, _ in stages)
        periods = -(-deepest // 4)

        def slot(s, j):
            for lag, stage_ in stages:
                ds_, jj = (j - lag) // 4, (j - lag) % 4
                if isinstance(s, int) and not (0 <= 4 * (s + ds_) + jj < NT):
                    continue
                stage_(Tile(e, s + ds_, jj))

        for s in range(periods):
            for j in range(4):
                slot(s, j)
        with e.Fori(periods, NS) as s:
            for j in range(4):
                slot(s, j)
        for s in range(NS, NS + periods):
            for j in range(4):
                slot(s, j)

    owner = {n: "vector" for n in names}
    for n in "T1 pqk pv scr PTr memm skT upm PV AT Wo h2Tr rtr".split():
        owner[n] = "tensor"
    for n in "h1T qkh exq v32 vhi exp ptA ptB skt aT hhi h2T lg".split():
        owner[n] = "scalar"
    for n in "pow vlo vpr aadd pw2 madd hlo".split():
        owner[n] = "gpsimd"

    with nc.Block() as block:
        def start(name, e):
            for n in names:
                if owner[n] == name:
                    e.sem_inc(S[n], PRE)
            engine_program(name, e)

        @block.sync
        def _(e):
            start("sync", e)
            for j in range(4):
                e.wait_ge(s_st[j], 64 * NS)

        @block.tensor
        def _(e):
            start("tensor", e)

        @block.vector
        def _(e):
            start("vector", e)

        @block.scalar
        def _(e):
            start("scalar", e)

        @block.gpsimd
        def _(e):
            start("gpsimd", e)


def experts(nc, ctx, sb_, sem_, banks, tri, iotas, tok_a, tok_b, out_rows, rows_dram, w8_dram,
            w13s, w2, idh, logits, passed):
    def sb(name, shape, dt=F32):
        return sb_(name, shape, dt, ctx)

    def sem(name):
        return sem_(name, ctx)

    NW = NSLOT_TILES
    w2s = sb("w2s", [P, 2, E * KC * D], F16)
    w2f = sb("w2f", [P, 2, KC * D])
    trib = sb("trib", [P, 2, P], BF16)
    iota = sb("iota", [P, 4, NW])
    toka = sb("toka", [P, NT])
    tokb = sb("tokb", [P, 1])
    work = [sb(f"work{i}", [P, E, NT]) for i in range(6)]
    oh1, oh2 = sb("oh1", [P, E, NT]), sb("oh2", [P, E, NT])
    chosen = sb("chosen", [P, E, NT], BF16)
    w8 = sb("w8", [P, NT, E])
    col = [sb(f"col{i}", [P, NT]) for i in range(8)]
    small = [sb(f"small{i}", [P, E]) for i in range(6)]
    posi = sb("posi", [P, 4, 2 * NT], I32)
    tile_of, row_of = sb("tile_of", [P, NT, 2]), sb("row_of", [P, NT, 2])
    rsel = sb("rsel", [P, 2, P], F16)
    asel = sb("asel", [P, 2, 2, NW], F16)
    cmpx = sb("cmpx", [P, NW, E])
    ex_of = sb("ex_of", [P, NW])
    ex_i = sb("ex_i", [P, NW], I32)
    oh_tile = sb("oh_tile", [P, NW, E])
    rowf, hasf = sb("rowf", [P, NW]), sb("hasf", [P, NW])
    gidx, sidx = sb("gidx", [P, NW], I32), sb("sidx", [P, NW], I32)

    s_ld, s_v, s_a, s_p, s_w8 = sem("r_ld"), sem("r_v"), sem("r_a"), sem("r_p"), sem("r_w8")
    s_sel, s_use = sem("r_sel"), sem("r_use")
    s_wl, s_wh, s_wr = [sem("r_wl0"), sem("r_wl1")], sem("r_wh"), sem("r_wr")

    with nc.Block() as block:
        n, marks = [0], {}

        @block.sync
        def _(e):
            for dst, src in ((trib[:, :, :], tri), (iota[:, :, :], iotas), (toka[:, :], tok_a), (tokb[:, :], tok_b)):
                e.dma_start(dst, src).then_inc(s_ld, 16)
            for n_ in range(E):
                if n_ >= 2:
                    e.wait_ge(s_wr, n_ - 1)
                e.dma_start(w2f[:, n_ % 2, :].rearrange("p (k n) -> p k n", k=KC),
                            w2[n_].rearrange("(k p) n -> p k n", p=P)).then_inc(s_wl[n_ % 2], 16)

        @block.vector
        def _(e):
            def link(ins):
                n[0] += 1
                ins.then_inc(s_v, 1)
                e.wait_ge(s_v, n[0])

            def by_token(ap):
                return ap.rearrange("p e t -> p t e")

            def first_max(lg, m, oh, a, r):
                link(e.tensor_reduce(m[:, :], by_token(lg[:, :, :]), axis=X, op=ALU.max))
                link(e.tensor_tensor(a[:, :, :], lg[:, :, :], bc_mid(m[:, :], E), ALU.is_equal))
                link(e.tensor_tensor(a[:, :, :], a[:, :, :], bc(iota[:, 2, 0:E], NT), ALU.mult))
                link(e.tensor_reduce(r[:, :], by_token(a[:, :, :]), axis=X, op=ALU.max))
                link(e.tensor_tensor(oh[:, :, :], a[:, :, :], bc_mid(r[:, :], E), ALU.is_equal))

            e.wait_ge(s_ld, 64)
            m1, m2, r, z, e2, w1, w2_ = col[0:7]
            first_max(logits, m1, oh1, work[0], r)
            link(e.scalar_tensor_tensor(out=work[1][:, :, :], in0=oh1[:, :, :], scalar=-3e38, in1=logits[:, :, :],
                                        op0=ALU.mult, op1=ALU.add))
            first_max(work[1], m2, oh2, work[0], r)
            link(e.tensor_tensor(chosen[:, :, :], oh1[:, :, :], oh2[:, :, :], ALU.add))
            at_chosen = n[0]
            link(e.tensor_tensor(work[2][:, :, :], logits[:, :, :], bc_mid(m1[:, :], E), ALU.subtract))
            link(e.tensor_tensor(e2[:, :], m2[:, :], m1[:, :], ALU.subtract))
            at_shift = n[0]
            e.wait_ge(s_a, 2)
            link(e.tensor_reduce(z[:, :], by_token(work[2][:, :, :]), axis=X, op=ALU.add))
            link(e.reciprocal(z[:, :], z[:, :]))
            link(e.tensor_tensor(e2[:, :], e2[:, :], z[:, :], ALU.mult))
            link(e.tensor_tensor(r[:, :], e2[:, :], z[:, :], ALU.add))
            link(e.tensor_scalar(r[:, :], r[:, :], EPS_TOP, None, ALU.add))
            link(e.reciprocal(r[:, :], r[:, :]))
            link(e.tensor_scalar(r[:, :], r[:, :], 1.0 / W_SCALE, None, ALU.mult))
            link(e.tensor_tensor(w1[:, :], z[:, :], r[:, :], ALU.mult))
            link(e.tensor_tensor(w2_[:, :], e2[:, :], r[:, :], ALU.mult))
            link(e.tensor_tensor(work[0][:, :, :], oh1[:, :, :], bc_mid(w1[:, :], E), ALU.mult))
            link(e.tensor_tensor(work[1][:, :, :], oh2[:, :, :], bc_mid(w2_[:, :], E), ALU.mult))
            link(e.tensor_tensor(w8[:, :, :], by_token(work[0][:, :, :]),
                                 by_token(work[1][:, :, :]), ALU.add))
            at_w8 = n[0]
            e.wait_ge(s_p, 2)
            before, tot, cum = work[3], work[4], work[5]
            flat = lambda ap: ap[:, :, :].rearrange("p e t -> p (e t)")
            link(e.tensor_copy(flat(before), banks[0][:, :]))
            link(e.tensor_copy(flat(tot), banks[1][:, :]))
            link(e.memset(flat(work[0]), 1.0))
            link(e.tensor_tensor_scan(flat(cum), flat(work[0]), flat(tot), 0.0, ALU.mult, ALU.add))
            start, cnt, tiles, tend, ones8, base = small
            link(e.memset(start[:, 0:1], 0.0))
            link(e.tensor_copy(start[:, 1:E], cum[:, 0:E - 1, NT - 1]))
            link(e.tensor_tensor(cnt[:, :], cum[:, :, NT - 1], start[:, :], ALU.subtract))
            link(e.tensor_tensor(work[0][:, :, :], bc(cnt[:, :], NT), bc_mid(iota[:, 1, 0:NT], E), ALU.is_gt))
            link(e.tensor_reduce(tiles[:, :], work[0][:, :, :], axis=X, op=ALU.add))
            link(e.memset(ones8[:, :], 1.0))
            link(e.tensor_tensor_scan(tend[:, :], ones8[:, :], tiles[:, :], 0.0, ALU.mult, ALU.add))
            link(e.tensor_tensor(base[:, :], tend[:, :], tiles[:, :], ALU.subtract))
            link(e.scalar_tensor_tensor(out=base[:, :], in0=base[:, :], scalar=float(P), in1=start[:, :],
                                        op0=ALU.mult, op1=ALU.subtract))
            link(e.tensor_tensor(flat(cum), flat(cum), flat(tot), ALU.subtract))
            link(e.tensor_tensor(flat(cum), flat(cum), flat(before), ALU.add))
            link(e.tensor_tensor(cum[:, :, :], cum[:, :, :], bc(base[:, :], NT), ALU.add))
            for q, oh in enumerate((oh1, oh2)):
                link(e.tensor_tensor(work[q][:, :, :], oh[:, :, :], cum[:, :, :], ALU.mult))
                link(e.tensor_reduce(col[q][:, :], by_token(work[q][:, :, :]), axis=X, op=ALU.add))
                link(e.tensor_copy(posi[:, 0, q * NT:(q + 1) * NT], col[q][:, :]))
            link(e.tensor_scalar(posi[:, 1, :], posi[:, 0, :], 7, None, ALU.arith_shift_right))
            link(e.tensor_scalar(posi[:, 2, :], posi[:, 0, :], P - 1, None, ALU.bitwise_and))
            link(e.tensor_copy(tile_of[:, :, :].rearrange("p t q -> p q t"),
                               posi[:, 1, :].rearrange("p (q t) -> p q t", q=2)))
            link(e.tensor_copy(row_of[:, :, :].rearrange("p t q -> p q t"),
                               posi[:, 2, :].rearrange("p (q t) -> p q t", q=2)))
            link(e.tensor_tensor(cmpx[:, :, :], bc(iota[:, 0, :], E), bc_mid(tend[:, :], NW), ALU.is_ge))
            link(e.tensor_reduce(ex_of[:, :], cmpx[:, :, :], axis=X, op=ALU.add))
            link(e.tensor_scalar(ex_of[:, :], ex_of[:, :], float(E - 1), None, ALU.min))
            link(e.tensor_copy(ex_i[:, :], ex_of[:, :]))
            link(e.tensor_tensor(oh_tile[:, :, :], bc(ex_of[:, :], E), bc_mid(iota[:, 3, 0:E], NW), ALU.is_equal))
            with e.Fori(0, NT) as t:
                for q in range(2):
                    e.wait_ge(s_use, t * 2 + (q + 1))
                    e.tensor_scalar(rsel[:, q, :], iota[:, 0, 0:P], row_of[:, bass.ds(t, 1), q], None, ALU.is_equal)
                    e.tensor_scalar(asel[:, q, 0, :], iota[:, 0, :], tile_of[:, bass.ds(t, 1), q],
                                    toka[:, bass.ds(t, 1)], ALU.is_equal, ALU.mult)
                    e.tensor_scalar(asel[:, q, 1, :], iota[:, 0, :], tile_of[:, bass.ds(t, 1), q],
                                    tokb[:, :], ALU.is_equal, ALU.mult).then_inc(s_sel, 1)
            e.wait_ge(s_p, 3)
            link(e.tensor_copy(rowf[:, :], banks[2][:, 0:NW]))
            link(e.tensor_scalar(hasf[:, :], rowf[:, :], 0.5, float(-OOB), ALU.is_le, ALU.mult))
            link(e.scalar_tensor_tensor(out=rowf[:, :], in0=rowf[:, :], scalar=float(SEG), in1=banks[2][:, NW:2 * NW],
                                        op0=ALU.mult, op1=ALU.add))
            link(e.tensor_scalar(rowf[:, :], rowf[:, :], float(-SEG), None, ALU.add))
            link(e.tensor_tensor(hasf[:, :], rowf[:, :], hasf[:, :], ALU.subtract))
            link(e.tensor_copy(sidx[:, :], hasf[:, :]))
            link(e.tensor_scalar(rowf[:, :], rowf[:, :], 0.0, None, ALU.max))
            link(e.tensor_copy(gidx[:, :], rowf[:, :]))
            marks.update(chosen=at_chosen, shift=at_shift, w8=at_w8)

        @block.scalar
        def _(e):
            e.wait_ge(s_v, marks["shift"])
            e.activation(work[2][:, :, :], work[2][:, :, :], ACT.Exp).then_inc(s_a, 1)
            e.activation(col[4][:, :], col[4][:, :], ACT.Exp).then_inc(s_a, 1)
            for n_ in range(E):
                e.wait_ge(s_wl[n_ % 2], 16 * (n_ // 2 + 1))
                f = w2f[:, n_ % 2, :]
                e.activation(w2s[:, 0, n_ * KC * D:(n_ + 1) * KC * D], f, ACT.Copy, scale=W_SCALE).then_inc(s_wh, 1)
                e.activation(f, f, ACT.Copy, scale=W_SCALE).then_inc(s_wh, 1)

        @block.tensor
        def _(e):
            e.wait_ge(s_v, marks["chosen"])
            moving = chosen[:, :, :].rearrange("p e t -> p (e t)")
            for q in range(2):
                e.matmul(banks[q][:, :], trib[:, q, :], moving, start=True, stop=True).then_inc(s_p, 1)
            e.sem_inc(s_use, 2)

            def add(t, q, first, last):
                e.wait_ge(s_sel, t * 2 + (q + 1))
                return e.matmul(banks[2][:, 0:2 * NW], rsel[:, q, :], asel[:, q, :, :].rearrange("p a w -> p (a w)"),
                                start=first, stop=last)

            for q in range(2):
                add(0, q, q == 0, False).then_inc(s_use, 1)
            with e.Fori(1, NT - 1) as t:
                for q in range(2):
                    add(t, q, False, False).then_inc(s_use, 1)
            add(NT - 1, 0, False, False)
            add(NT - 1, 1, False, True).then_inc(s_p, 1)

        @block.gpsimd
        def _(e):
            for n_ in range(E):
                e.wait_ge(s_wh, 2 * n_ + 2)
                at = slice(n_ * KC * D, (n_ + 1) * KC * D)
                e.tensor_tensor(w2s[:, 1, at], w2f[:, n_ % 2, :], w2s[:, 0, at], ALU.subtract).then_inc(s_wr, 1)
            e.wait_ge(s_v, marks["w8"])
            for j in range(NJ):
                for b2 in range(2):
                    dst = w8_dram[(2 * j + b2) * T:(2 * j + b2 + 1) * T, :].rearrange("(s t) e -> t s e", t=SEG)
                    src = w8[b2 * SEG:(b2 + 1) * SEG, :, :].rearrange("p (s j) e -> p j s e", j=NJ)[:, j]
                    e.dma_start(dst, src).then_inc(s_w8, 16)
            e.wait_ge(s_w8, 16 * B)

    U = 5
    gi, si = sb("gi", [P, U, 1], I32), sb("si", [P, U, 1], I32)
    grow = sb("grow", [P, U, 4 * D], F16)
    gw = sb("gw", [P, U, E])
    gwm = sb("gwm", [P, U, E])
    wrow = sb("wrow", [P, U, 1])
    xT = sb("xT", [P, U, 2, G, P], F16)
    sg = sb("sg", [P, U, I])
    hf = sb("hf", [P, U, I])
    hs = sb("hs", [P, U, 2, I], F16)
    hT = sb("hT", [P, U, 2, KC, P], F16)
    yo = sb("yo", [P, U, D])

    names = "cpi xTr xT gu sg hm hhi hlo hTr hT y wm ws yw".split()
    S = {m: sem("f_" + m) for m in names}
    s_g = [sem(f"f_row{i}") for i in range(U)]
    s_gw = [sem(f"f_wt{i}") for i in range(U)]
    s_sc = [sem(f"f_add{i}") for i in range(U)]
    s_init = sem("f_init")
    bGate, bUp, bH, bX, bY = banks[0:5]
    bHh = bH[:, :].bitcast(F16)
    bXh = bX[:, :].bitcast(F16)

    class Slot:
        def __init__(self, e, s, j):
            self.e, self.s, self.j = e, s, j
            self.t = s * U + j

        def when(self, stage, back=0):
            if isinstance(self.s, int):
                of = min(self.t - back, NW - 1)
                return S[stage], max(of, -1) + 1 + PRE
            return S[stage], self.s * U + (self.j - back + 1 + PRE)

        def wait(self, stage, back=0):
            if not isinstance(self.s, int) or self.t >= back:
                self.e.wait_ge(*self.when(stage, back))

        def wait_apart(self, *stages):
            apart(self.e, passed, [self.when(*w) for w in stages])

        def added(self, back):
            s, j = self.s + (self.j - back) // U, (self.j - back) % U
            return s_sc[j], (max(s, -1) if isinstance(s, int) else s) * 16 + 16

        def arrived(self, sems, back=0):
            s, j = self.s + (self.j - back) // U, (self.j - back) % U
            if not isinstance(s, int) or s >= 0:
                self.e.wait_ge(sems[j], s * 16 + 16)

    def done(ins, stage):
        ins.then_inc(S[stage], 1)

    def gather(k):
        k.wait("yw", U)
        k.wait("xTr", U)
        k.arrived(s_g, U)
        k.arrived(s_gw, U)
        k.arrived(s_sc, U)
        k.e.tensor_copy(gi[:, k.j, :], gidx[:, bass.ds(k.t, 1)])
        done(k.e.tensor_copy(si[:, k.j, :], sidx[:, bass.ds(k.t, 1)]), "cpi")
        k.wait_apart(("cpi",))
        at = bass.IndirectOffsetOnAxis(ap=gi[:, k.j, :], axis=0)
        k.e.indirect_dma_start(grow[:, k.j, :], None, rows_dram, at).then_inc(s_g[k.j], 16)
        k.e.indirect_dma_start(gw[:, k.j, :], None, w8_dram, at).then_inc(s_gw[k.j], 16)

    def x_trans(k):
        k.arrived(s_g)
        k.wait("xT", 1)
        for a in range(2):
            for c in range(G):
                i = k.e.transpose(bXh[:, (a * G + c) * P:(a * G + c + 1) * P],
                                  grow[:, k.j, a * D + c * P:a * D + (c + 1) * P], idh[:, :])
        done(i, "xTr")

    def x_copy(k):
        k.wait("xTr")
        k.wait("gu", U)
        done(k.e.tensor_copy(xT[:, k.j, :, :, :].rearrange("p a c t -> p (a c t)"), bXh[:, 0:2 * D]), "xT")

    def gate_up(k):
        k.wait_apart(("xT",), ("hm", 1))
        ex_reg = k.e.value_load(ex_i[0:1, bass.ds(k.t, 1)], min_val=0, max_val=E - 1)
        for c in range(G):
            for a, b_ in PARTS:
                for bank, at in ((bGate, 0), (bUp, I)):
                    i = k.e.matmul(bank[:, :], xT[:, k.j, a, c, :],
                                   w13s[:, b_, bass.ds(ex_reg * (G * 2 * I) + (c * 2 * I + at), I)],
                                   start=(c == 0 and (a, b_) == PARTS[0]),
                                   stop=(c == G - 1 and (a, b_) == PARTS[-1]))
        done(i, "gu")

    def silu(k):
        k.wait("gu")
        k.wait("hm", U)
        done(k.e.activation(sg[:, k.j, :], bGate[:, :], ACT.Silu, scale=1.0 / W_SCALE), "sg")

    def h_mul(k):
        k.wait("sg")
        k.wait("hhi", U)
        k.wait("hlo", U)
        done(k.e.scalar_tensor_tensor(out=hf[:, k.j, :], in0=bUp[:, :], scalar=1.0 / W_SCALE, in1=sg[:, k.j, :],
                                      op0=ALU.mult, op1=ALU.mult), "hm")

    def h_hi(k):
        k.wait("hm")
        k.wait("hTr", U)
        k.wait("hlo", U)
        done(k.e.activation(hs[:, k.j, 0, :], hf[:, k.j, :], ACT.Copy), "hhi")

    def h_lo(k):
        k.wait("hhi")
        k.wait("hTr", U)
        done(k.e.tensor_tensor(hs[:, k.j, 1, :], hf[:, k.j, :], hs[:, k.j, 0, :], ALU.subtract), "hlo")

    def h_trans(k):
        k.wait("hlo")
        k.wait("hT", 1)
        for a in range(2):
            for c in range(KC):
                i = k.e.transpose(bHh[:, (a * KC + c) * P:(a * KC + c + 1) * P],
                                  hs[:, k.j, a, c * P:(c + 1) * P], idh[:, :])
        done(i, "hTr")

    def h_copy(k):
        k.wait("hTr")
        k.wait("y", U)
        done(k.e.tensor_copy(hT[:, k.j, :, :, :].rearrange("p a c t -> p (a c t)"), bHh[:, :]), "hT")

    def down(k):
        k.wait_apart(("hT",), ("yw", 1))
        ex_reg = k.e.value_load(ex_i[0:1, bass.ds(k.t, 1)], min_val=0, max_val=E - 1)
        for c in range(KC):
            for a, b_ in PARTS:
                i = k.e.matmul(bY[:, 0:D], hT[:, k.j, a, c, :], w2s[:, b_, bass.ds(ex_reg * (KC * D) + c * D, D)],
                               start=(c == 0 and (a, b_) == PARTS[0]), stop=(c == KC - 1 and (a, b_) == PARTS[-1]))
        done(i, "y")

    def weigh(k):
        k.arrived(s_gw)
        k.wait("ws", U)
        done(k.e.tensor_tensor(gwm[:, k.j, :], gw[:, k.j, :],
                               oh_tile[:, bass.ds(k.t, 1), :].rearrange("p o e -> p (o e)"), ALU.mult), "wm")
        k.wait("wm")
        k.wait("yw", U)
        done(k.e.tensor_reduce(wrow[:, k.j, :], gwm[:, k.j, :], axis=X, op=ALU.add), "ws")
        k.wait("y")
        k.wait("ws")
        k.arrived(s_g)
        k.arrived(s_sc, U)
        done(k.e.scalar_tensor_tensor(out=yo[:, k.j, :], in0=bY[:, 0:D], scalar=wrow[:, k.j, :],
                                      in1=grow[:, k.j, 2 * D:4 * D].bitcast(F32), op0=ALU.mult, op1=ALU.mult), "yw")

    def scatter(k):
        apart(k.e, passed, [k.when("yw"), k.added(1)])
        k.e.indirect_dma_start(out_rows, bass.IndirectOffsetOnAxis(ap=si[:, k.j, :], axis=0), yo[:, k.j, :], None,
                               bounds_check=B * T - 1, oob_is_err=False, compute_op=ALU.add).then_inc(s_sc[k.j], 16)

    program = {
        "tensor": [(2, gate_up), (3, h_trans), (1, x_trans), (4, down)],
        "vector": [(2, h_mul), (3, h_copy), (1, x_copy), (4, weigh)],
        "scalar": [(2, silu), (2, h_hi)],
        "gpsimd": [(2, h_lo), (0, gather), (4, scatter)],
    }
    owner = {m: "vector" for m in names}
    owner.update({m: "tensor" for m in "xTr gu hTr y".split()})
    owner.update({m: "scalar" for m in "sg hhi".split()})
    owner.update({m: "gpsimd" for m in "cpi hlo".split()})

    with nc.Block() as block:
        def engine_program(name, e):
            for m in names:
                if owner[m] == name:
                    e.sem_inc(S[m], PRE)
            stages = program[name]
            periods = -(-max(lag for lag, _ in stages) // U)

            def slot(s, j):
                for lag, stage_ in stages:
                    back, jj = (j - lag) // U, (j - lag) % U
                    if isinstance(s, int) and not (0 <= U * (s + back) + jj < NW):
                        continue
                    stage_(Slot(e, s + back, jj))

            for s in range(periods):
                for j in range(U):
                    slot(s, j)
            with e.Fori(periods, NW // U) as s:
                for j in range(U):
                    slot(s, j)
            for s in range(NW // U, NW // U + periods):
                for j in range(U):
                    slot(s, j)

        @block.tensor
        def _(e):
            engine_program("tensor", e)

        @block.vector
        def _(e):
            engine_program("vector", e)

        @block.scalar
        def _(e):
            engine_program("scalar", e)

        @block.gpsimd
        def _(e):
            engine_program("gpsimd", e)
            for i in range(U):
                e.wait_ge(s_sc[i], 16 * (NW // U))


def constants():
    bf16 = mybir.dt.to_np(BF16) if hasattr(mybir.dt, "to_np") else np.dtype("bfloat16")
    p = np.arange(P)
    head = p // DK
    block = (head[:, None] == head[None, :]).astype(np.float32)
    onto = (head[:, None] == np.arange(HG)[None, :]).astype(np.float32)
    causal = np.where(np.arange(SEG)[None, :] > (p % SEG)[:, None], np.float32(NEG), np.float32(0))
    n = np.arange(NSLOT_TILES)
    t = np.arange(NT)
    return dict(
        ident=np.eye(P, dtype=np.float32),
        head_of_row=((head % 4)[:, None] == np.arange(4)[None, :]).astype(np.float32),
        mem_mask=np.concatenate([block, onto], 1),
        q_onehot=((p % SEG)[:, None] == (p % SEG)[None, :]).astype(bf16),
        causal=np.tile(causal, (1, 8)).astype(bf16),
        tri=np.stack([(p[:, None] < p[None, :]), np.ones((P, P), bool)], 1).astype(bf16),
        iotas=np.broadcast_to(np.stack([n, P * n, E - n, n]).astype(np.float32), (P, 4, NSLOT_TILES)).copy(),
        tok_a=np.broadcast_to(((2 * (t % NJ)) * (T // SEG) + t // NJ + 1).astype(np.float32), (P, NT)).copy(),
        tok_b=((p // SEG) * T + p % SEG).astype(np.float32)[:, None],
    )


def kernel(**inputs):
    import concourse.bacc as bacc
    from concourse.bass_utils import run_bass_kernel_spmd

    a = {k[3:]: np.asarray(v) for k, v in inputs.items()}
    c = np.ascontiguousarray
    data = dict(
        x=a["attn_x"], cT=c(a["c"].T), wmod=a["wmod"], wqT=c(a["attn_W_q"].T), wkT=c(a["attn_W_k"].T),
        wvT=c(a["attn_W_v"].T), woT=c(a["attn_W_o"].T), beta=a["attn_beta_param"], rwT=c(a["ffn_router_w"].T),
        w13=a["ffn_w13"], w2=a["ffn_w2"], **constants(),
    )
    nc = bacc.Bacc("TRN2", target_bir_lowering=False, num_devices=1)
    arrays, args = {}, {}
    for name, v in data.items():
        arrays[f"in_{name}"] = v
        args[name] = nc.dram_tensor(f"in_{name}", v.shape, mybir.dt.from_np(v.dtype), kind="ExternalInput").ap()
    out = nc.dram_tensor("out", [B, T, D], F32, kind="ExternalOutput").ap()
    adaln_block(nc, out=out, **args)
    r = run_bass_kernel_spmd(nc, [arrays], core_ids=[0])
    return r.results[0]["out"]
```

```python
from contextlib import ExitStack

import numpy as np

import concourse.bass as bass
from concourse import mybir

F32 = mybir.dt.float32
F16 = mybir.dt.float16
BF16 = mybir.dt.bfloat16
I32 = mybir.dt.int32
ALU = mybir.AluOpType
ACT = mybir.ActivationFunctionType
X = mybir.AxisListType.X

P = 128
B, T, D = 8, 1024, 256
H, DK, SEG = 16, 16, 64
NJ = B // 2
NS = T // SEG
NT = NJ * NS
G = D // P
HG = P // DK
MW = P + HG
NPAIR = H // 2
VW = 2 * DK + 1
E, I = 8, 512
NSLOT_TILES = (B * T * 2) // P + E - 1
KC = I // P
W_SCALE = 32.0
EPS_LN, EPS_MEM, EPS_TOP = 1e-5, 1e-6, 1e-6
NEG = -1e30
PRE = 4
PARTS = ((0, 0), (0, 1), (1, 0))
OOB = B * T + 4096


def bc(ap, n):
    return ap.unsqueeze(2).to_broadcast([ap.shape[0], ap.shape[1], n])


def bc_mid(ap, n):
    return ap.unsqueeze(1).to_broadcast([ap.shape[0], n, ap.shape[1]])


def apart(e, passed, waits):
    for s, v in waits:
        if not (isinstance(v, int) and v <= 0):
            e.wait_ge(s, v)
    e.sem_inc(passed, 1)


def adaln_block(nc, x, cT, wmod, wqT, wkT, wvT, woT, beta, rwT, w13, w2, ident, head_of_row, mem_mask,
                q_onehot, causal, tri, iotas, tok_a, tok_b, out):
    rows_dram = nc.dram_tensor("moe_rows", [B * T, 2 * D + 2 * D], F16, kind="Internal").ap()
    w8_dram = nc.dram_tensor("top2_weights", [B * T, E], F32, kind="Internal").ap()
    out_rows = out.rearrange("b t d -> (b t) d")

    with ExitStack() as whole:
        def sb(name, shape, dt=F32, ctx=whole):
            return ctx.enter_context(nc.sbuf_tensor(name, shape, dt))

        def sem(name, ctx=whole):
            return ctx.enter_context(nc.semaphore(name))

        passed = sem("passed")
        w13s = sb("w13s", [P, 2, E * G * 2 * I], F16)
        idf = sb("idf", [P, P])
        idh = sb("idh", [P, P], F16)
        logits = sb("logits", [P, E, NT])
        psum = whole.enter_context(nc.psum_tensor("psum", [P, 8, 512], F32))
        banks = [psum[:, i, :] for i in range(8)]

        with ExitStack() as att:
            attention(nc, att, sb, sem, psum, banks, x, cT, wmod, wqT, wkT, wvT, woT, beta, rwT, w13, ident,
                      head_of_row, mem_mask, q_onehot, causal, out, rows_dram, w13s, idf, idh, logits, passed)
        with ExitStack() as moe:
            experts(nc, moe, sb, sem, banks, tri, iotas, tok_a, tok_b, out_rows, rows_dram, w8_dram,
                    w13s, w2, idh, logits, passed)


def attention(nc, ctx, sb_, sem_, psum, banks, x, cT, wmod, wqT, wkT, wvT, woT, beta, rwT, w13, ident,
              head_of_row, mem_mask, q_onehot, causal, out, rows_dram, w13s, idf, idh, logits, passed):
    def sb(name, shape, dt=F32):
        return sb_(name, shape, dt, ctx)

    def sem(name):
        return sem_(name, ctx)

    wqk = sb("wqk", [P, G, 2 * D])
    wv = sb("wv", [P, G, D])
    wo = sb("wo", [P, G, D])
    rw = sb("rw", [P, G, E])
    rws = sb("rws", [P, 2, G, E], F16)
    hrow = sb("hrow", [P, 4])
    mmask = sb("mmask", [P, MW])
    onehot = sb("onehot", [P, P], BF16)
    cmask = sb("cmask", [P, 8 * SEG], BF16)
    mods = sb("mods", [P, 5, NJ, D])
    sA, sCA, sGA, sB2, sCB, sGB = range(6)
    beta_m = sb("beta_m", [P, H])
    om_beta = sb("om_beta", [P, NPAIR])
    mhalf = sb("mhalf", [P, 1])

    vs = sb("vs", [P, 4, 2, NPAIR, VW], F16)
    vp = sb("vp", [P, 2, G, MW])
    mem = sb("mem", [P, NJ, 2, G, MW])
    hrows = sb("hrows", [P, 4, 4 * D], F16)

    set_up = ExitStack()
    cs = sb_("cs", [P, G, B], F32, set_up)
    crep = sb_("crep", [P, G, B, SEG], F32, set_up)
    btile = sb_("btile", [P, H], F32, set_up)
    wmod_sb = sb_("wmod_sb", [P, G, 6 * D], F32, set_up)
    stage = sb_("stage", [P, 2, 1024], F32, set_up)
    gate_sign = sb_("gate_sign", [P, 512], F32, set_up)

    bkA, bkB, bkC, bkD, bkE, bkF, bkG, bkH = banks
    bkDE = psum[:, 3:5, :]
    bkAh, bkFh, bkGh = (b_.bitcast(F16) for b_ in (bkA, bkF, bkG))

    s_ld, s_w = sem("s_ld"), [sem("s_w0"), sem("s_w1")]
    s_c, s_set, s_mod, s_mev = sem("s_c"), sem("s_set"), sem("s_mod"), sem("s_mev")
    s_hi, s_lo, s_gb = sem("s_hi"), sem("s_lo"), sem("s_gb")

    loads = [(wmod_sb[:, :, :], wmod.rearrange("(c p) n -> p c n", p=P)),
             (cs[:, :, :], cT.rearrange("(c p) b -> p c b", p=P)),
             (idf[:, :], ident), (hrow[:, :], head_of_row), (mmask[:, :], mem_mask),
             (wv[:, :, :], wvT.rearrange("(c p) n -> p c n", p=P)),
             (wo[:, :, :], woT.rearrange("(c p) n -> p c n", p=P)),
             (rw[:, :, :], rwT.rearrange("(c p) n -> p c n", p=P)),
             (wqk[:, :, 0:D], wqT.rearrange("(c p) n -> p c n", p=P)),
             (wqk[:, :, D:2 * D], wkT.rearrange("(c p) n -> p c n", p=P)),
             (btile[:, :], beta.rearrange("(a h) -> a h", a=1).to_broadcast([P, H])),
             (onehot[:, :], q_onehot), (cmask[:, :], causal)]
    chunks = [(w13[e, c * P:(c + 1) * P, :], w13s, (e * G + c) * 1024) for e in range(E) for c in range(G)]

    with nc.Block() as block:
        @block.gpsimd
        def _(e):
            for dst, src in loads:
                e.dma_start(dst, src).then_inc(s_ld, 16)
            e.memset(mem[:, :, :, :, :], 0.0).then_inc(s_c, 1)
            e.memset(mhalf[:, :], -0.5).then_inc(s_c, 1)
            for b_ in range(4):
                e.memset(vs[:, b_, 0, :, 2 * DK:VW], 1.0).then_inc(s_c, 1)
                e.memset(vs[:, b_, 1, :, 2 * DK:VW], 0.0).then_inc(s_c, 1)
            for b_ in range(2):
                e.memset(vp[:, b_, :, P:MW], 1.0).then_inc(s_c, 1)

        @block.sync
        def _(e):
            for n, (src, _, _) in enumerate(chunks):
                if n >= 2:
                    e.wait_ge(s_lo, n - 1)
                e.dma_start(stage[:, n % 2, :], src).then_inc(s_w[n % 2], 16)

        @block.scalar
        def _(e):
            e.wait_ge(s_ld, 16 * len(loads))
            e.activation(cs[:, :, :], cs[:, :, :], ACT.Silu).then_inc(s_set, 1)
            e.activation(btile[:, :], btile[:, :], ACT.Exp, scale=-1.0).then_inc(s_set, 1)
            e.activation(idh[:, :], idf[:, :], ACT.Copy).then_inc(s_set, 1)
            e.activation(rws[:, 0, :, :], rw[:, :, :], ACT.Copy, scale=W_SCALE).then_inc(s_set, 1)
            for n, (_, dst, at) in enumerate(chunks):
                e.wait_ge(s_w[n % 2], 16 * (n // 2 + 1))
                e.activation(dst[:, 0, at:at + 1024], stage[:, n % 2, :], ACT.Copy, scale=W_SCALE).then_inc(s_hi, 1)

        @block.vector
        def _(e):
            e.wait_ge(s_set, 4)
            e.scalar_tensor_tensor(out=rws[:, 1, :, :], in0=rw[:, :, :], scalar=W_SCALE, in1=rws[:, 0, :, :],
                                   op0=ALU.mult, op1=ALU.subtract)
            e.tensor_copy(crep[:, :, :, :].rearrange("p c b t -> p (c b) t"),
                          bc(cs[:, :, :].rearrange("p c b -> p (c b)"), SEG)).then_inc(s_gb, 1)
            e.tensor_scalar(btile[:, :], btile[:, :], 1.0, None, ALU.add).then_inc(s_gb, 1)
            e.wait_ge(s_gb, 2)
            e.reciprocal(btile[:, :], btile[:, :]).then_inc(s_gb, 1)
            e.memset(beta_m[SEG:P, :], 1.0)
            e.wait_ge(s_gb, 3)
            e.tensor_copy(beta_m[0:SEG, :], btile[0:SEG, :]).then_inc(s_gb, 1)
            pair = btile[:, :].rearrange("p (n two) -> p two n", two=2)
            for par in range(2):
                rows = slice(par * SEG, (par + 1) * SEG)
                e.tensor_scalar(om_beta[rows, :], pair[rows, par, :], -1.0, 1.0, ALU.mult, ALU.add).then_inc(s_gb, 1)
            link = 6
            for n in range(6 * NJ // 2):
                k, jj = n // 2, n % 2
                bank = banks[n % 2][:, :].rearrange("p (j d) -> p j d", j=2)
                e.wait_ge(s_mod, n + 1)
                if k == sGB:
                    dst = hrows[:, 2 * jj:2 * jj + 2, 2 * D:4 * D].bitcast(F32)
                else:
                    dst = mods[:, k, 2 * jj:2 * jj + 2, :]
                if k in (sCA, sCB):
                    e.tensor_scalar(dst, bank, 1.0, None, ALU.add).then_inc(s_mev, 1)
                elif k in (sGA, sGB):
                    e.wait_ge(s_mev, n)
                    tmp = gate_sign[:, :].rearrange("p (j d) -> p j d", j=2)
                    e.tensor_scalar(tmp, bank, 0.0, None, ALU.is_ge).then_inc(s_gb, 1)
                    e.wait_ge(s_gb, link + 1)
                    e.tensor_scalar(tmp, tmp, 2.0, -1.0, ALU.mult, ALU.add).then_inc(s_gb, 1)
                    e.wait_ge(s_gb, link + 2)
                    e.tensor_tensor(dst, bank, tmp, ALU.mult).then_inc(s_gb, 1)
                    e.wait_ge(s_gb, link + 3)
                    e.scalar_tensor_tensor(out=dst, in0=dst, scalar=0.25, in1=tmp, op0=ALU.max,
                                           op1=ALU.mult).then_inc(s_mev, 1)
                    link += 3
                else:
                    e.tensor_copy(dst, bank).then_inc(s_mev, 1)
            for n, (_, dst, at) in enumerate(chunks):
                e.wait_ge(s_hi, n + 1)
                e.scalar_tensor_tensor(out=dst[:, 1, at:at + 1024], in0=stage[:, n % 2, :], scalar=W_SCALE,
                                       in1=dst[:, 0, at:at + 1024], op0=ALU.mult, op1=ALU.subtract).then_inc(s_lo, 1)

        @block.tensor
        def _(e):
            e.wait_ge(s_gb, 1)
            e.wait_ge(s_ld, 16 * len(loads))
            for n in range(6 * NJ // 2):
                k, jj = n // 2, n % 2
                if n >= 2:
                    e.wait_ge(s_mev, n - 1)
                for q in range(2):
                    j = 2 * jj + q
                    for c in range(G):
                        mm = e.matmul(banks[n % 2][:, q * D:(q + 1) * D],
                                      crep[:, c, 2 * j:2 * j + 2, :].rearrange("p b t -> p (b t)"),
                                      wmod_sb[:, c, k * D:(k + 1) * D], start=(c == 0), stop=(c == G - 1))
                mm.then_inc(s_mod, 1)

    set_up.close()

    xin = sb("xin", [P, 4, D])
    bst = sb("bst", [P, 4, 6])
    mv = sb("mv", [P, 4, 2])
    rstd, nmr = sb("rstd", [P, 4, 1]), sb("nmr", [P, 4, 1])
    h1 = sb("h1", [P, 2, D])
    h1T = sb("h1T", [P, 2, G, P])
    qk = sb("qk", [P, 2, 2, 2 * D], F16)
    qm = sb("qm", [P, 2, 2, 4, 4, SEG], F16)
    ex = sb("ex", [P, 2, 512])
    rel = sb("rel", [P, 2, 512])
    sig = sb("sig", [P, 2, G, 2, 2, SEG])
    v32 = sb("v32", [P, 2, D])
    mx = sb("mx", [P, 2, 16])
    sc = sb("sc", [P, 2, 16, SEG])
    ph = sb("ph", [P, 2, 2, 16, SEG], F16)
    pT = sb("pT", [P, 2, 2, 8, P], F16)
    rr = sb("rr", [P, 2, 2, NPAIR])
    att_o = sb("att_o", [P, 2, D])
    dd = sb("dd", [P, 2, 2, H])
    memA = sb("memA", [P, 4, D])
    skt = sb("skt", [P, 2, D])
    upd = sb("upd", [P, 2, G, MW])
    aT = sb("aT", [P, 2, G, P])
    xres = sb("xres", [P, 2, D])
    x1 = sb("x1", [P, 4, D])
    bst2 = sb("bst2", [P, 4, 6])
    mv2 = sb("mv2", [P, 4, 2])
    rstd2, nmr2 = sb("rstd2", [P, 4, 1]), sb("nmr2", [P, 4, 1])
    h2 = sb("h2", [P, 2, D])
    h2T = sb("h2T", [P, 2, 2, G, P], F16)

    names = ("stats aggr eps pow nmr xn lna lnb T1 h1T pqk pv qkh exq rel v32 vhi vlo qlo sig qm scr mx sub exp phi plo "
             "PTr ptA ptl memm den rec bet mA mV vpr skT skt upm umul madd PV rcp rom ado aadd AT aT Wo "
             "gat res st2 ag2 ep2 pw2 nm2 xn2 l2a l2b hhi hlo h2Tr h2T rtr lg").split()
    S = {n: sem("a_" + n) for n in names}
    s_x = [sem(f"s_x{j}") for j in range(4)]
    s_xr = [sem(f"s_xr{j}") for j in range(4)]
    s_st = [sem(f"s_st{j}") for j in range(4)]

    BANK_FREE = {
        "pv": ((("sub", -2),),
               (("ado", 1),)),
        "h2_trans": ((("h1T", -8),),
                     (("aT", -3), ("lg", 1), ("h2T", 1))),
        "update": ((("qlo", -1), ("v32", -1), ("rel", -1)),
                   (("umul", 1),)),
        "sk_trans": ((("gat", 5),),
                     (("skt", 1),)),
        "p_trans": ((("mA", -1), ("mV", -1)),
                    (("ptA", 1), ("ptl", 1))),
        "w_o": ((("skt", -4),),
                (("gat", 1),)),
        "scores": ((("ado", 3),),
                   (("sub", 1),)),
        "router": ((("h2T", 0),),
                   (("h1T", -8), ("aT", -3), ("lg", 1))),
        "mem_mm": ((("ptA", 2), ("ptl", 2)),
                   (("mA", 1), ("mV", 1))),
        "a_trans": ((("lg", 4),),
                    (("h2T", 4), ("h1T", -4), ("aT", 1))),
        "proj": ((("umul", 2),),
                 (("qlo", 1), ("v32", 1), ("rel", 1))),
        "t1": ((("aT", 5),),
               (("lg", 9), ("h2T", 9), ("h1T", 1))),
    }

    class Tile:

        def __init__(self, e, s, j):
            self.e, self.s, self.j, self.b = e, s, j, j % 2
            self.t = s * 4 + j

        def when(self, stage, back=0):
            if isinstance(self.s, int):
                of = min(self.t - back, NT - 1)
                return S[stage], max(of, -1) + 1 + PRE
            return S[stage], self.s * 4 + (self.j - back + 1 + PRE)

        def wait(self, stage, back=0):
            if not isinstance(self.s, int) or self.t >= back:
                self.e.wait_ge(*self.when(stage, back))

        def wait_banks(self, name):
            latest, others = BANK_FREE[name]
            for stage, back in latest + (others if isinstance(self.s, int) else ()):
                self.wait(stage, back)

        def wait_apart(self, *stages):
            apart(self.e, passed, [self.when(*w) for w in stages])

        def arrived(self, sems, n=1):
            self.e.wait_ge(sems[self.j], self.s * (16 * n) + 16 * n)

        def stored(self):
            if not isinstance(self.s, int) or self.s > 0:
                self.e.wait_ge(s_st[self.j], self.s * 64)

    def done(ins, stage):
        ins.then_inc(S[stage], 1)

    def load_x(k):
        k.wait("xn", 4)
        for b2 in range(2):
            k.e.dma_start(xin[b2 * SEG:(b2 + 1) * SEG, k.j, :],
                          x[2 * k.j + b2, bass.ds(k.s * SEG, SEG), :]).then_inc(s_x[k.j], 16)

    def load_res(k):
        k.wait("res", 2)
        for b2 in range(2):
            k.e.dma_start(xres[b2 * SEG:(b2 + 1) * SEG, k.b, :],
                          x[2 * k.j + b2, bass.ds(k.s * SEG, SEG), :]).then_inc(s_xr[k.j], 16)

    def store(k):
        k.wait_apart(("hlo",))
        for b2 in range(2):
            rows = slice(b2 * SEG, (b2 + 1) * SEG)
            k.e.dma_start(out[2 * k.j + b2, bass.ds(k.s * SEG, SEG), :], x1[rows, k.j, :]).then_inc(s_st[k.j], 16)
            k.e.dma_start(rows_dram[bass.ds(k.s * SEG + (2 * k.j + b2) * T, SEG), :],
                          hrows[rows, k.j, :]).then_inc(s_st[k.j], 16)

    def stats(k):
        k.arrived(s_x, 2)
        k.wait("aggr", 4)
        done(k.e.bn_stats(bst[:, k.j, :], xin[:, k.j, :]), "stats")
        k.wait_apart(("stats",), ("nmr", 4))
        done(k.e.bn_aggr(mv[:, k.j, :], bst[:, k.j, :]), "aggr")
        k.wait("aggr")
        k.wait("xn", 4)
        done(k.e.tensor_scalar(rstd[:, k.j, :], mv[:, k.j, 1:2], EPS_LN, None, ALU.add), "eps")

    def ln_scale(k):
        k.wait("eps")
        done(k.e.tensor_tensor(rstd[:, k.j, :], rstd[:, k.j, :], mhalf[:, :], ALU.pow), "pow")
        k.wait_apart(("pow",), ("xn", 4))
        done(k.e.tensor_scalar(nmr[:, k.j, :], mv[:, k.j, 0:1], rstd[:, k.j, :], -1.0, ALU.mult, ALU.mult), "nmr")

    def ln_act(k):
        k.wait("nmr")
        k.wait("T1", 2)
        done(k.e.activation(h1[:, k.b, :], xin[:, k.j, :], ACT.Identity, bias=nmr[:, k.j, :],
                            scale=rstd[:, k.j, :]), "xn")

    def ln_mod(k):
        k.wait("xn")
        done(k.e.tensor_tensor(h1[:, k.b, :], h1[:, k.b, :], mods[:, sCA, k.j, :], ALU.mult), "lna")
        k.wait("lna")
        done(k.e.tensor_tensor(h1[:, k.b, :], h1[:, k.b, :], mods[:, sA, k.j, :], ALU.add), "lnb")

    def t1(k):
        k.wait("lnb")
        k.wait_banks("t1")
        for c in range(G):
            i = k.e.transpose(bkA[:, c * P:(c + 1) * P], h1[:, k.b, c * P:(c + 1) * P], idf[:, :])
        done(i, "T1")

    def h1t(k):
        k.wait("T1")
        k.wait("pv", 2)
        done(k.e.activation(h1T[:, k.b, :, :].rearrange("p c t -> p (c t)"), bkA[:, 0:D], ACT.Copy), "h1T")

    def proj(k):
        k.wait("h1T")
        k.wait_banks("proj")
        for n in range(4):
            for c in range(G):
                i = k.e.matmul(bkB[:, n * P:(n + 1) * P], wqk[:, c, n * P:(n + 1) * P], h1T[:, k.b, c, :],
                               start=(c == 0), stop=(c == G - 1))
        done(i, "pqk")
        for c in range(G):
            i = k.e.matmul(bkC[:, 0:D], h1T[:, k.b, c, :], wv[:, c, :], start=(c == 0), stop=(c == G - 1))
        done(i, "pv")

    def proj_act(k):
        k.wait("pqk")
        k.wait("scr", 2)
        k.wait("qm", 2)
        k.wait("qlo", 2)
        done(k.e.activation(qk[:, k.b, 0, :], bkB[:, :], ACT.Copy), "qkh")
        k.wait("sig", 2)
        done(k.e.activation(ex[:, k.b, :], bkB[:, :], ACT.Exp), "exq")
        done(k.e.activation(rel[:, k.b, :], bkB[:, :], ACT.Relu), "rel")
        k.wait("pv")
        k.wait("vpr", 2)
        k.wait("vlo", 2)
        done(k.e.activation(v32[:, k.b, :], bkC[:, 0:D], ACT.Copy), "v32")
        k.wait("PV", 4)
        k.wait("vlo", 4)
        k.wait("v32")
        done(k.e.activation(vs[:, k.j, 0, :, 0:2 * DK], v32[:, k.b, :].rearrange("p (n w) -> p n w", w=2 * DK),
                            ACT.Copy), "vhi")

    def v_rest(k):
        k.wait("vhi")
        k.wait("PV", 4)
        done(k.e.tensor_tensor(vs[:, k.j, 1, :, 0:2 * DK], v32[:, k.b, :].rearrange("p (n w) -> p n w", w=2 * DK),
                               vs[:, k.j, 0, :, 0:2 * DK], ALU.subtract), "vlo")

    def proj_dve(k):
        k.wait("rel")
        k.wait("scr", 2)
        done(k.e.tensor_tensor(qk[:, k.b, 1, :], bkB[:, :], qk[:, k.b, 0, :], ALU.subtract), "qlo")
        k.wait("memm", 2)
        k.wait("skT", 2)
        for a in range(2):
            i = k.e.scalar_tensor_tensor(
                out=sig[:, k.b, :, :, a, :].rearrange("p g b t -> p (g b) t"),
                in0=ex[:, k.b, a * D:(a + 1) * D].rearrange("p (n t) -> p n t", t=SEG), scalar=1.0,
                in1=rel[:, k.b, a * D:(a + 1) * D].rearrange("p (n t) -> p n t", t=SEG), op0=ALU.min, op1=ALU.add)
        done(i, "sig")

    def q_masks(k):
        k.wait("qlo")
        k.wait("qkh")
        k.wait("scr", 2)
        for m in range(4):
            i = k.e.tensor_scalar(qm[:, k.b, :, :, m, :], qk[:, k.b, :, 0:D].rearrange("p a (n t) -> p a n t", t=SEG),
                                  hrow[:, m:m + 1], None, ALU.mult)
        done(i, "qm")

    def scores(k):
        k.wait("qm")
        k.wait("qlo")
        k.wait_banks("scores")
        for half, bank in enumerate((bkD, bkE)):
            r = slice(half * SEG, (half + 1) * SEG)
            k.e.matmul(bank[:, :], onehot[r, :], cmask[r, :], start=True, stop=False, skip_group_check=True)
            for g in range(G):
                for u in range(2):
                    for b2 in range(2):
                        n = (g * 2 + u) * 2 + b2
                        keys = slice(D + g * P + b2 * SEG, D + g * P + (b2 + 1) * SEG)
                        for a, b_ in PARTS:
                            i = k.e.matmul(bank[:, n * SEG:(n + 1) * SEG],
                                           qm[r, k.b, a, g * 2 + b2, 2 * u:2 * u + 2, :].rearrange("p m t -> p (m t)"),
                                           qk[r, k.b, b_, keys], start=False,
                                           stop=(n == 7 and (a, b_) == PARTS[-1]), skip_group_check=True)
        done(i, "scr")

    def softmax_dve(k):
        both = bkDE.rearrange("p h (n k) -> p (h n) k", k=SEG)
        k.wait("scr")
        k.wait("sub", 2)
        done(k.e.tensor_reduce(mx[:, k.b, :], both, axis=X, op=ALU.max), "mx")
        k.wait("mx")
        k.wait("plo", 2)
        k.wait("phi", 2)
        done(k.e.tensor_tensor(sc[:, k.b, :, :], both, bc(mx[:, k.b, :], SEG), ALU.subtract), "sub")

    def softmax_act(k):
        k.wait("sub")
        flat = sc[:, k.b, :, :].rearrange("p n k -> p (n k)")
        done(k.e.activation(flat, flat, ACT.Exp, scale=DK ** -0.5), "exp")
        k.wait("exp")
        k.wait("PTr", 2)
        k.wait("plo", 2)
        done(k.e.activation(ph[:, k.b, 0, :, :].rearrange("p n k -> p (n k)"), flat, ACT.Copy), "phi")

    def p_rest(k):
        k.wait("phi")
        k.wait("PTr", 2)
        done(k.e.tensor_tensor(ph[:, k.b, 1, :, :], sc[:, k.b, :, :], ph[:, k.b, 0, :, :], ALU.subtract), "plo")

    def p_trans(k):
        k.wait("plo")
        k.wait("phi")
        k.wait_banks("p_trans")
        for a, bank in enumerate((bkFh, bkGh)):
            for n in range(8):
                i = k.e.transpose(bank[:, n * P:(n + 1) * P],
                                  ph[:, k.b, a, 2 * n:2 * n + 2, :].rearrange("p n k -> p (n k)"), idh[:, :])
        done(i, "PTr")

    def pt_act(k):
        k.wait("PTr")
        k.wait("PV", 2)
        done(k.e.activation(pT[:, k.b, 0, :, :].rearrange("p n t -> p (n t)"), bkFh, ACT.Copy), "ptA")

    def pt_dve(k):
        k.wait("PTr")
        k.wait("PV", 2)
        done(k.e.tensor_copy(pT[:, k.b, 1, :, :].rearrange("p n t -> p (n t)"), bkGh), "ptl")

    def mem_mm(k):
        k.wait("sig")
        k.wait("madd", 4)
        k.wait_banks("mem_mm")
        for b2, bank in enumerate((bkF, bkG)):
            for g in range(G):
                i = k.e.matmul(bank[:, g * MW:(g + 1) * MW], sig[:, k.b, g, b2, :, :].rearrange("p a t -> p (a t)"),
                               mem[:, k.j, b2, g, :], start=True, stop=True)
        done(i, "memm")

    def mem_dve(k):
        k.wait("memm")
        k.wait("mA", 2)
        k.wait("mV", 2)
        fg = [bank[:, 0:G * MW].rearrange("p (g w) -> p g w", w=MW) for bank in (bkF, bkG)]
        for b2 in range(2):
            i = k.e.tensor_scalar(dd[:, k.b, b2, :].rearrange("p (g h) -> p g h", g=G), fg[b2][:, :, P:MW],
                                  EPS_MEM, None, ALU.add)
        done(i, "den")
        k.wait("den")
        flat = dd[:, k.b, :, :].rearrange("p b h -> p (b h)")
        done(k.e.reciprocal(flat, flat), "rec")
        k.wait("rec")
        done(k.e.tensor_tensor(dd[:, k.b, :, :], dd[:, k.b, :, :], bc_mid(beta_m[:, :], 2), ALU.mult), "bet")
        k.wait("bet")
        k.wait("upm", 2)
        for b2 in range(2):
            i = k.e.tensor_tensor(
                vp[b2 * SEG:(b2 + 1) * SEG, k.b, :, 0:P].rearrange("p g (h d) -> p g h d", h=HG),
                fg[b2][SEG:P, :, 0:P].rearrange("p g (h d) -> p g h d", d=DK),
                dd[SEG:P, k.b, b2, :].rearrange("p (g h) -> p g h", g=G).unsqueeze(3).to_broadcast([SEG, G, HG, DK]),
                ALU.mult)
        done(i, "mV")
        k.wait("aadd", 4)
        for b2 in range(2):
            i = k.e.tensor_tensor(
                memA[b2 * SEG:(b2 + 1) * SEG, k.j, :].rearrange("p (g h d) -> p g h d", g=G, h=HG),
                fg[b2][0:SEG, :, 0:P].rearrange("p g (h d) -> p g h d", d=DK),
                dd[0:SEG, k.b, b2, :].rearrange("p (g h) -> p g h", g=G).unsqueeze(3).to_broadcast([SEG, G, HG, DK]),
                ALU.mult)
        done(i, "mA")

    def v_new(k):
        k.wait("mV")
        k.wait("v32")
        k.wait("upm", 2)
        done(k.e.tensor_tensor(vp[:, k.b, :, 0:P], v32[:, k.b, :].rearrange("p (g w) -> p g w", g=G),
                               vp[:, k.b, :, 0:P], ALU.subtract), "vpr")

    def sk_trans(k):
        k.wait("sig")
        k.wait_banks("sk_trans")
        k.e.sem_inc(passed, 1)
        for b2 in range(2):
            for g in range(G):
                i = k.e.transpose(bkH[0:SEG, b2 * D + g * P:b2 * D + (g + 1) * P], sig[:, k.b, g, b2, 1, :], idf[:, :])
        done(i, "skT")

    def sk_act(k):
        k.wait("skT")
        k.wait("upm", 2)
        for b2 in range(2):
            i = k.e.activation(skt[b2 * SEG:(b2 + 1) * SEG, k.b, :], bkH[0:SEG, b2 * D:(b2 + 1) * D], ACT.Copy)
        done(i, "skt")

    def update(k):
        k.wait("vpr")
        k.wait("skt")
        k.wait_banks("update")
        for b2, bank in enumerate((bkB, bkC)):
            r = slice(b2 * SEG, (b2 + 1) * SEG)
            for g in range(G):
                i = k.e.matmul(bank[:, g * MW:(g + 1) * MW], skt[r, k.b, g * P:(g + 1) * P], vp[r, k.b, g, :],
                               start=True, stop=True)
        done(i, "upm")

    def update_dve(k):
        k.wait("upm")
        k.wait("madd", 1)
        for b2, bank in enumerate((bkB, bkC)):
            i = k.e.tensor_tensor(upd[:, b2, :, :], bank[:, 0:G * MW].rearrange("p (g w) -> p g w", w=MW),
                                  bc_mid(mmask[:, :], G), ALU.mult)
        done(i, "umul")

    def update_add(k):
        k.wait("umul")
        k.wait("memm")
        flat = mem[:, k.j, :, :, :].rearrange("p b g w -> p (b g w)")
        done(k.e.tensor_tensor(flat, flat, upd[:, :, :, :].rearrange("p b g w -> p (b g w)"), ALU.add), "madd")

    def pv(k):
        k.wait("ptl")
        k.wait("ptA")
        k.wait("vlo")
        k.wait_banks("pv")
        for b2, bank in enumerate((bkD, bkE)):
            r = slice(b2 * SEG, (b2 + 1) * SEG)
            for half in range(2):
                for gu in range(4):
                    pair = (gu // 2) * 4 + half * 2 + gu % 2
                    for a, b_ in PARTS:
                        i = k.e.matmul(bank[:, pair * VW:(pair + 1) * VW], pT[r, k.b, a, half * 4 + gu, :],
                                       vs[r, k.j, b_, pair, :], start=((a, b_) == PARTS[0]),
                                       stop=((a, b_) == PARTS[-1]))
        done(i, "PV")

    def pv_dve(k):
        k.wait("PV")
        k.wait("ado", 2)
        de = [bank[:, 0:NPAIR * VW].rearrange("p (n w) -> p n w", w=VW) for bank in (bkD, bkE)]
        for b2 in range(2):
            i = k.e.reciprocal(rr[:, k.b, b2, :], de[b2][:, :, 2 * DK])
        done(i, "rcp")
        k.wait("rcp")
        done(k.e.tensor_tensor(rr[:, k.b, :, :], rr[:, k.b, :, :], bc_mid(om_beta[:, :], 2), ALU.mult), "rom")
        k.wait("rom")
        k.wait("AT", 2)
        k.wait("aadd", 2)
        for b2 in range(2):
            for par in range(2):
                r = slice(par * SEG, (par + 1) * SEG)
                i = k.e.tensor_tensor(
                    att_o[b2 * SEG:(b2 + 1) * SEG, k.b, :].rearrange("p (n w) -> p n w", w=2 * DK)[:, :, par * DK:(par + 1) * DK],
                    de[b2][r, :, par * DK:(par + 1) * DK], bc(rr[r, k.b, b2, :], DK), ALU.mult)
        done(i, "ado")

    def a_add(k):
        k.wait("ado")
        k.wait("mA")
        done(k.e.tensor_tensor(att_o[:, k.b, :], att_o[:, k.b, :], memA[:, k.j, :], ALU.add), "aadd")

    def a_trans(k):
        k.wait("aadd")
        k.wait_banks("a_trans")
        for c in range(G):
            i = k.e.transpose(bkA[:, c * P:(c + 1) * P], att_o[:, k.b, c * P:(c + 1) * P], idf[:, :])
        done(i, "AT")

    def a_act(k):
        k.wait("AT")
        k.wait("Wo", 2)
        done(k.e.activation(aT[:, k.b, :, :].rearrange("p c t -> p (c t)"), bkA[:, 0:D], ACT.Copy), "aT")

    def w_o(k):
        k.wait("aT")
        k.wait_banks("w_o")
        for c in range(G):
            i = k.e.matmul(bkH[:, 0:D], aT[:, k.b, c, :], wo[:, c, :], start=(c == 0), stop=(c == G - 1))
        done(i, "Wo")

    def resid(k):
        k.wait("Wo")
        k.wait("xn2", 4)
        k.stored()
        done(k.e.tensor_tensor(x1[:, k.j, :], bkH[:, 0:D], mods[:, sGA, k.j, :], ALU.mult), "gat")

    def res_add(k):
        k.arrived(s_xr, 2)
        k.wait("gat")
        done(k.e.tensor_tensor(x1[:, k.j, :], x1[:, k.j, :], xres[:, k.b, :], ALU.add), "res")

    def stats2(k):
        k.wait("res")
        done(k.e.bn_stats(bst2[:, k.j, :], x1[:, k.j, :]), "st2")
        k.wait_apart(("st2",), ("nm2", 4))
        done(k.e.bn_aggr(mv2[:, k.j, :], bst2[:, k.j, :]), "ag2")
        k.wait("ag2")
        k.wait("xn2", 4)
        done(k.e.tensor_scalar(rstd2[:, k.j, :], mv2[:, k.j, 1:2], EPS_LN, None, ALU.add), "ep2")

    def ln2_scale(k):
        k.wait("ep2")
        done(k.e.tensor_tensor(rstd2[:, k.j, :], rstd2[:, k.j, :], mhalf[:, :], ALU.pow), "pw2")
        k.wait_apart(("pw2",), ("xn2", 4))
        done(k.e.tensor_scalar(nmr2[:, k.j, :], mv2[:, k.j, 0:1], rstd2[:, k.j, :], -1.0, ALU.mult, ALU.mult), "nm2")

    def ln2_act(k):
        k.wait("nm2")
        k.wait("hhi", 2)
        k.wait("hlo", 2)
        done(k.e.activation(h2[:, k.b, :], x1[:, k.j, :], ACT.Identity, bias=nmr2[:, k.j, :],
                            scale=rstd2[:, k.j, :]), "xn2")

    def ln2_mod(k):
        k.wait("xn2")
        done(k.e.tensor_tensor(h2[:, k.b, :], h2[:, k.b, :], mods[:, sCB, k.j, :], ALU.mult), "l2a")
        k.wait("l2a")
        done(k.e.tensor_tensor(h2[:, k.b, :], h2[:, k.b, :], mods[:, sB2, k.j, :], ALU.add), "l2b")

    def rows_hi(k):
        k.wait("l2b")
        k.stored()
        done(k.e.activation(hrows[:, k.j, 0:D], h2[:, k.b, :], ACT.Copy), "hhi")

    def rows_lo(k):
        k.wait("hhi")
        done(k.e.tensor_tensor(hrows[:, k.j, D:2 * D], h2[:, k.b, :], hrows[:, k.j, 0:D], ALU.subtract), "hlo")

    def h2_trans(k):
        k.wait("hhi")
        k.wait("hlo")
        k.wait_banks("h2_trans")
        for n in range(2 * G):
            i = k.e.transpose(bkAh[:, n * P:(n + 1) * P], hrows[:, k.j, n * P:(n + 1) * P], idh[:, :])
        done(i, "h2Tr")

    def h2_act(k):
        k.wait("h2Tr")
        k.wait("rtr", 2)
        done(k.e.activation(h2T[:, k.b, :, :, :].rearrange("p a c t -> p (a c t)"), bkAh[:, 0:2 * D], ACT.Copy), "h2T")

    def router(k):
        k.wait("h2T")
        k.wait_banks("router")
        for c in range(G):
            for a, b_ in PARTS:
                i = k.e.matmul(bkA[:, D:D + E], h2T[:, k.b, a, c, :], rws[:, b_, c, :],
                               start=(c == 0 and (a, b_) == PARTS[0]), stop=(c == G - 1 and (a, b_) == PARTS[-1]))
        done(i, "rtr")

    def logit_copy(k):
        k.wait("rtr")
        done(k.e.activation(logits[:, :, bass.ds(k.t, 1)].rearrange("p e o -> p (e o)"), bkA[:, D:D + E], ACT.Copy,
                               scale=1.0 / W_SCALE), "lg")

    program = {
        "sync": [(3, load_x), (17, store), (13, load_res)],
        "tensor": [(9, pv), (13, h2_trans), (7, update), (6, sk_trans), (8, p_trans), (10, w_o), (6, scores),
                   (13, router), (6, mem_mm), (9, a_trans), (5, proj), (4, t1)],
        "vector": [(9, pv_dve), (6, q_masks), (7, update_dve), (8, pt_dve), (10, resid), (0, stats),
                   (6, softmax_dve), (6, mem_dve), (10, stats2), (5, proj_dve)],
        "scalar": [(6, sk_act), (13, h2_act), (8, pt_act), (3, ln_act), (7, softmax_act), (13, logit_copy),
                   (9, a_act), (5, proj_act), (4, h1t), (11, rows_hi), (10, ln2_act)],
        "gpsimd": [(3, ln_scale), (9, a_add), (4, ln_mod), (7, update_add), (10, res_add), (11, ln2_mod),
                   (7, p_rest), (6, v_new), (10, ln2_scale), (11, rows_lo), (5, v_rest)],
    }

    def engine_program(name, e):
        stages = program[name]
        deepest = max(lag for lag, _ in stages)
        periods = -(-deepest // 4)

        def slot(s, j):
            for lag, stage_ in stages:
                ds_, jj = (j - lag) // 4, (j - lag) % 4
                if isinstance(s, int) and not (0 <= 4 * (s + ds_) + jj < NT):
                    continue
                stage_(Tile(e, s + ds_, jj))

        for s in range(periods):
            for j in range(4):
                slot(s, j)
        with e.Fori(periods, NS) as s:
            for j in range(4):
                slot(s, j)
        for s in range(NS, NS + periods):
            for j in range(4):
                slot(s, j)

    owner = {n: "vector" for n in names}
    for n in "T1 pqk pv scr PTr memm skT upm PV AT Wo h2Tr rtr".split():
        owner[n] = "tensor"
    for n in "xn h1T qkh exq rel v32 vhi exp phi ptA skt aT xn2 hhi h2T lg".split():
        owner[n] = "scalar"
    for n in "pow nmr lna lnb vlo plo vpr aadd res pw2 nm2 l2a l2b madd hlo".split():
        owner[n] = "gpsimd"

    with nc.Block() as block:
        def start(name, e):
            for n in names:
                if owner[n] == name:
                    e.sem_inc(S[n], PRE)
            engine_program(name, e)

        @block.sync
        def _(e):
            start("sync", e)
            for j in range(4):
                e.wait_ge(s_st[j], 64 * NS)

        @block.tensor
        def _(e):
            start("tensor", e)

        @block.vector
        def _(e):
            start("vector", e)

        @block.scalar
        def _(e):
            start("scalar", e)

        @block.gpsimd
        def _(e):
            start("gpsimd", e)


def experts(nc, ctx, sb_, sem_, banks, tri, iotas, tok_a, tok_b, out_rows, rows_dram, w8_dram,
            w13s, w2, idh, logits, passed):
    def sb(name, shape, dt=F32):
        return sb_(name, shape, dt, ctx)

    def sem(name):
        return sem_(name, ctx)

    NW = NSLOT_TILES
    w2s = sb("w2s", [P, 2, E * KC * D], F16)
    w2f = sb("w2f", [P, 2, KC * D])
    trib = sb("trib", [P, 2, P], BF16)
    iota = sb("iota", [P, 4, NW])
    toka = sb("toka", [P, NT])
    tokb = sb("tokb", [P, 1])
    work = [sb(f"work{i}", [P, E, NT]) for i in range(6)]
    oh1, oh2 = sb("oh1", [P, E, NT]), sb("oh2", [P, E, NT])
    chosen = sb("chosen", [P, E, NT], BF16)
    w8 = sb("w8", [P, NT, E])
    col = [sb(f"col{i}", [P, NT]) for i in range(8)]
    small = [sb(f"small{i}", [P, E]) for i in range(6)]
    posi = sb("posi", [P, 4, 2 * NT], I32)
    tile_of, row_of = sb("tile_of", [P, NT, 2]), sb("row_of", [P, NT, 2])
    rsel = sb("rsel", [P, 2, P], F16)
    asel = sb("asel", [P, 2, 2, NW], F16)
    cmpx = sb("cmpx", [P, NW, E])
    ex_of = sb("ex_of", [P, NW])
    ex_i = sb("ex_i", [P, NW], I32)
    oh_tile = sb("oh_tile", [P, NW, E])
    rowf, hasf = sb("rowf", [P, NW]), sb("hasf", [P, NW])
    gidx, sidx = sb("gidx", [P, NW], I32), sb("sidx", [P, NW], I32)

    s_ld, s_v, s_a, s_p, s_w8 = sem("r_ld"), sem("r_v"), sem("r_a"), sem("r_p"), sem("r_w8")
    s_sel, s_use = sem("r_sel"), sem("r_use")
    s_wl, s_wh, s_wr = [sem("r_wl0"), sem("r_wl1")], sem("r_wh"), sem("r_wr")

    with nc.Block() as block:
        n, marks = [0], {}

        @block.sync
        def _(e):
            for dst, src in ((trib[:, :, :], tri), (iota[:, :, :], iotas), (toka[:, :], tok_a), (tokb[:, :], tok_b)):
                e.dma_start(dst, src).then_inc(s_ld, 16)
            for n_ in range(E):
                if n_ >= 2:
                    e.wait_ge(s_wr, n_ - 1)
                e.dma_start(w2f[:, n_ % 2, :].rearrange("p (k n) -> p k n", k=KC),
                            w2[n_].rearrange("(k p) n -> p k n", p=P)).then_inc(s_wl[n_ % 2], 16)

        @block.vector
        def _(e):
            def link(ins):
                n[0] += 1
                ins.then_inc(s_v, 1)
                e.wait_ge(s_v, n[0])

            def by_token(ap):
                return ap.rearrange("p e t -> p t e")

            def first_max(lg, m, oh, a, r):
                link(e.tensor_reduce(m[:, :], by_token(lg[:, :, :]), axis=X, op=ALU.max))
                link(e.tensor_tensor(a[:, :, :], lg[:, :, :], bc_mid(m[:, :], E), ALU.is_equal))
                link(e.tensor_tensor(a[:, :, :], a[:, :, :], bc(iota[:, 2, 0:E], NT), ALU.mult))
                link(e.tensor_reduce(r[:, :], by_token(a[:, :, :]), axis=X, op=ALU.max))
                link(e.tensor_tensor(oh[:, :, :], a[:, :, :], bc_mid(r[:, :], E), ALU.is_equal))

            e.wait_ge(s_ld, 64)
            m1, m2, r, z, e2, w1, w2_ = col[0:7]
            first_max(logits, m1, oh1, work[0], r)
            link(e.scalar_tensor_tensor(out=work[1][:, :, :], in0=oh1[:, :, :], scalar=-3e38, in1=logits[:, :, :],
                                        op0=ALU.mult, op1=ALU.add))
            first_max(work[1], m2, oh2, work[0], r)
            link(e.tensor_tensor(chosen[:, :, :], oh1[:, :, :], oh2[:, :, :], ALU.add))
            at_chosen = n[0]
            link(e.tensor_tensor(work[2][:, :, :], logits[:, :, :], bc_mid(m1[:, :], E), ALU.subtract))
            link(e.tensor_tensor(e2[:, :], m2[:, :], m1[:, :], ALU.subtract))
            at_shift = n[0]
            e.wait_ge(s_a, 2)
            link(e.tensor_reduce(z[:, :], by_token(work[2][:, :, :]), axis=X, op=ALU.add))
            link(e.reciprocal(z[:, :], z[:, :]))
            link(e.tensor_tensor(e2[:, :], e2[:, :], z[:, :], ALU.mult))
            link(e.tensor_tensor(r[:, :], e2[:, :], z[:, :], ALU.add))
            link(e.tensor_scalar(r[:, :], r[:, :], EPS_TOP, None, ALU.add))
            link(e.reciprocal(r[:, :], r[:, :]))
            link(e.tensor_scalar(r[:, :], r[:, :], 1.0 / W_SCALE, None, ALU.mult))
            link(e.tensor_tensor(w1[:, :], z[:, :], r[:, :], ALU.mult))
            link(e.tensor_tensor(w2_[:, :], e2[:, :], r[:, :], ALU.mult))
            link(e.tensor_tensor(work[0][:, :, :], oh1[:, :, :], bc_mid(w1[:, :], E), ALU.mult))
            link(e.tensor_tensor(work[1][:, :, :], oh2[:, :, :], bc_mid(w2_[:, :], E), ALU.mult))
            link(e.tensor_tensor(w8[:, :, :], by_token(work[0][:, :, :]),
                                 by_token(work[1][:, :, :]), ALU.add))
            at_w8 = n[0]
            e.wait_ge(s_p, 2)
            before, tot, cum = work[3], work[4], work[5]
            flat = lambda ap: ap[:, :, :].rearrange("p e t -> p (e t)")
            link(e.tensor_copy(flat(before), banks[0][:, :]))
            link(e.tensor_copy(flat(tot), banks[1][:, :]))
            link(e.memset(flat(work[0]), 1.0))
            link(e.tensor_tensor_scan(flat(cum), flat(work[0]), flat(tot), 0.0, ALU.mult, ALU.add))
            start, cnt, tiles, tend, ones8, base = small
            link(e.memset(start[:, 0:1], 0.0))
            link(e.tensor_copy(start[:, 1:E], cum[:, 0:E - 1, NT - 1]))
            link(e.tensor_tensor(cnt[:, :], cum[:, :, NT - 1], start[:, :], ALU.subtract))
            link(e.tensor_tensor(work[0][:, :, :], bc(cnt[:, :], NT), bc_mid(iota[:, 1, 0:NT], E), ALU.is_gt))
            link(e.tensor_reduce(tiles[:, :], work[0][:, :, :], axis=X, op=ALU.add))
            link(e.memset(ones8[:, :], 1.0))
            link(e.tensor_tensor_scan(tend[:, :], ones8[:, :], tiles[:, :], 0.0, ALU.mult, ALU.add))
            link(e.tensor_tensor(base[:, :], tend[:, :], tiles[:, :], ALU.subtract))
            link(e.scalar_tensor_tensor(out=base[:, :], in0=base[:, :], scalar=float(P), in1=start[:, :],
                                        op0=ALU.mult, op1=ALU.subtract))
            link(e.tensor_tensor(flat(cum), flat(cum), flat(tot), ALU.subtract))
            link(e.tensor_tensor(flat(cum), flat(cum), flat(before), ALU.add))
            link(e.tensor_tensor(cum[:, :, :], cum[:, :, :], bc(base[:, :], NT), ALU.add))
            for q, oh in enumerate((oh1, oh2)):
                link(e.tensor_tensor(work[q][:, :, :], oh[:, :, :], cum[:, :, :], ALU.mult))
                link(e.tensor_reduce(col[q][:, :], by_token(work[q][:, :, :]), axis=X, op=ALU.add))
                link(e.tensor_copy(posi[:, 0, q * NT:(q + 1) * NT], col[q][:, :]))
            link(e.tensor_scalar(posi[:, 1, :], posi[:, 0, :], 7, None, ALU.arith_shift_right))
            link(e.tensor_scalar(posi[:, 2, :], posi[:, 0, :], P - 1, None, ALU.bitwise_and))
            link(e.tensor_copy(tile_of[:, :, :].rearrange("p t q -> p q t"),
                               posi[:, 1, :].rearrange("p (q t) -> p q t", q=2)))
            link(e.tensor_copy(row_of[:, :, :].rearrange("p t q -> p q t"),
                               posi[:, 2, :].rearrange("p (q t) -> p q t", q=2)))
            link(e.tensor_tensor(cmpx[:, :, :], bc(iota[:, 0, :], E), bc_mid(tend[:, :], NW), ALU.is_ge))
            link(e.tensor_reduce(ex_of[:, :], cmpx[:, :, :], axis=X, op=ALU.add))
            link(e.tensor_scalar(ex_of[:, :], ex_of[:, :], float(E - 1), None, ALU.min))
            link(e.tensor_copy(ex_i[:, :], ex_of[:, :]))
            link(e.tensor_tensor(oh_tile[:, :, :], bc(ex_of[:, :], E), bc_mid(iota[:, 3, 0:E], NW), ALU.is_equal))
            with e.Fori(0, NT) as t:
                for q in range(2):
                    e.wait_ge(s_use, t * 2 + (q + 1))
                    e.tensor_scalar(rsel[:, q, :], iota[:, 0, 0:P], row_of[:, bass.ds(t, 1), q], None, ALU.is_equal)
                    e.tensor_scalar(asel[:, q, 0, :], iota[:, 0, :], tile_of[:, bass.ds(t, 1), q],
                                    toka[:, bass.ds(t, 1)], ALU.is_equal, ALU.mult)
                    e.tensor_scalar(asel[:, q, 1, :], iota[:, 0, :], tile_of[:, bass.ds(t, 1), q],
                                    tokb[:, :], ALU.is_equal, ALU.mult).then_inc(s_sel, 1)
            e.wait_ge(s_p, 3)
            link(e.tensor_copy(rowf[:, :], banks[2][:, 0:NW]))
            link(e.tensor_scalar(hasf[:, :], rowf[:, :], 0.5, float(-OOB), ALU.is_le, ALU.mult))
            link(e.scalar_tensor_tensor(out=rowf[:, :], in0=rowf[:, :], scalar=float(SEG), in1=banks[2][:, NW:2 * NW],
                                        op0=ALU.mult, op1=ALU.add))
            link(e.tensor_scalar(rowf[:, :], rowf[:, :], float(-SEG), None, ALU.add))
            link(e.tensor_tensor(hasf[:, :], rowf[:, :], hasf[:, :], ALU.subtract))
            link(e.tensor_copy(sidx[:, :], hasf[:, :]))
            link(e.tensor_scalar(rowf[:, :], rowf[:, :], 0.0, None, ALU.max))
            link(e.tensor_copy(gidx[:, :], rowf[:, :]))
            marks.update(chosen=at_chosen, shift=at_shift, w8=at_w8)

        @block.scalar
        def _(e):
            e.wait_ge(s_v, marks["shift"])
            e.activation(work[2][:, :, :], work[2][:, :, :], ACT.Exp).then_inc(s_a, 1)
            e.activation(col[4][:, :], col[4][:, :], ACT.Exp).then_inc(s_a, 1)
            for n_ in range(E):
                e.wait_ge(s_wl[n_ % 2], 16 * (n_ // 2 + 1))
                f = w2f[:, n_ % 2, :]
                e.activation(w2s[:, 0, n_ * KC * D:(n_ + 1) * KC * D], f, ACT.Copy, scale=W_SCALE).then_inc(s_wh, 1)
                e.activation(f, f, ACT.Copy, scale=W_SCALE).then_inc(s_wh, 1)

        @block.tensor
        def _(e):
            e.wait_ge(s_v, marks["chosen"])
            moving = chosen[:, :, :].rearrange("p e t -> p (e t)")
            for q in range(2):
                e.matmul(banks[q][:, :], trib[:, q, :], moving, start=True, stop=True).then_inc(s_p, 1)
            e.sem_inc(s_use, 2)

            def add(t, q, first, last):
                e.wait_ge(s_sel, t * 2 + (q + 1))
                return e.matmul(banks[2][:, 0:2 * NW], rsel[:, q, :], asel[:, q, :, :].rearrange("p a w -> p (a w)"),
                                start=first, stop=last)

            for q in range(2):
                add(0, q, q == 0, False).then_inc(s_use, 1)
            with e.Fori(1, NT - 1) as t:
                for q in range(2):
                    add(t, q, False, False).then_inc(s_use, 1)
            add(NT - 1, 0, False, False)
            add(NT - 1, 1, False, True).then_inc(s_p, 1)

        @block.gpsimd
        def _(e):
            for n_ in range(E):
                e.wait_ge(s_wh, 2 * n_ + 2)
                at = slice(n_ * KC * D, (n_ + 1) * KC * D)
                e.tensor_tensor(w2s[:, 1, at], w2f[:, n_ % 2, :], w2s[:, 0, at], ALU.subtract).then_inc(s_wr, 1)
            e.wait_ge(s_v, marks["w8"])
            for j in range(NJ):
                for b2 in range(2):
                    dst = w8_dram[(2 * j + b2) * T:(2 * j + b2 + 1) * T, :].rearrange("(s t) e -> t s e", t=SEG)
                    src = w8[b2 * SEG:(b2 + 1) * SEG, :, :].rearrange("p (s j) e -> p j s e", j=NJ)[:, j]
                    e.dma_start(dst, src).then_inc(s_w8, 16)
            e.wait_ge(s_w8, 16 * B)

    U = 8
    gi, si = sb("gi", [P, U, 1], I32), sb("si", [P, U, 1], I32)
    grow = sb("grow", [P, U, 4 * D], F16)
    gw = sb("gw", [P, U, E])
    gwm = sb("gwm", [P, 2, E])
    wrow = sb("wrow", [P, 2, 1])
    xT = sb("xT", [P, 2, 2, G, P], F16)
    sg = sb("sg", [P, 2, I])
    hf = sb("hf", [P, 2, I])
    hs = sb("hs", [P, 2, 2, I], F16)
    hT = sb("hT", [P, 2, 2, KC, P], F16)
    yo = sb("yo", [P, U, D])

    names = "cpi xTr xT gu sg hm hhi hlo hTr hT y wm ws yw".split()
    S = {m: sem("f_" + m) for m in names}
    s_g = [sem(f"f_row{i}") for i in range(U)]
    s_gw = [sem(f"f_wt{i}") for i in range(U)]
    s_sc = [sem(f"f_add{i}") for i in range(U)]
    s_init = sem("f_init")
    bGate, bUp, bY, bH, bX = banks[0:2], banks[2:4], banks[4:6], banks[6], banks[7]
    bHh = bH[:, :].bitcast(F16)
    bXh = bX[:, :].bitcast(F16)

    class Slot:
        def __init__(self, e, s, j):
            self.e, self.s, self.j, self.b = e, s, j, j % 2
            self.t = s * U + j

        def when(self, stage, back=0):
            if isinstance(self.s, int):
                of = min(self.t - back, NW - 1)
                return S[stage], max(of, -1) + 1 + PRE
            return S[stage], self.s * U + (self.j - back + 1 + PRE)

        def wait(self, stage, back=0):
            if not isinstance(self.s, int) or self.t >= back:
                self.e.wait_ge(*self.when(stage, back))

        def wait_apart(self, *stages):
            apart(self.e, passed, [self.when(*w) for w in stages])

        def added(self, back):
            s, j = self.s + (self.j - back) // U, (self.j - back) % U
            return s_sc[j], (max(s, -1) if isinstance(s, int) else s) * 16 + 16

        def arrived(self, sems, back=0):
            s, j = self.s + (self.j - back) // U, (self.j - back) % U
            if not isinstance(s, int) or s >= 0:
                self.e.wait_ge(sems[j], s * 16 + 16)

    def done(ins, stage):
        ins.then_inc(S[stage], 1)

    def gather(k):
        k.wait_apart(("cpi",), ("yw", U))
        at = bass.IndirectOffsetOnAxis(ap=gi[:, k.j, :], axis=0)
        k.e.indirect_dma_start(grow[:, k.j, :], None, rows_dram, at).then_inc(s_g[k.j], 16)
        k.e.indirect_dma_start(gw[:, k.j, :], None, w8_dram, at).then_inc(s_gw[k.j], 16)

    def indices(k):
        k.arrived(s_g, U)
        k.arrived(s_gw, U)
        k.arrived(s_sc, U)
        k.e.tensor_copy(gi[:, k.j, :], gidx[:, bass.ds(k.t, 1)])
        done(k.e.tensor_copy(si[:, k.j, :], sidx[:, bass.ds(k.t, 1)]), "cpi")

    def x_trans(k):
        k.arrived(s_g)
        k.wait("xT", 1)
        for a in range(2):
            for c in range(G):
                i = k.e.transpose(bXh[:, (a * G + c) * P:(a * G + c + 1) * P],
                                  grow[:, k.j, a * D + c * P:a * D + (c + 1) * P], idh[:, :])
        done(i, "xTr")

    def x_copy(k):
        k.wait("xTr")
        k.wait("gu", 2)
        done(k.e.tensor_copy(xT[:, k.b, :, :, :].rearrange("p a c t -> p (a c t)"), bXh[:, 0:2 * D]), "xT")

    def gate_up(k):
        k.wait_apart(("xT",), ("hm", 2))
        ex_reg = k.e.value_load(ex_i[0:1, bass.ds(k.t, 1)], min_val=0, max_val=E - 1)
        for c in range(G):
            for a, b_ in PARTS:
                for bank, at in ((bGate[k.b], 0), (bUp[k.b], I)):
                    i = k.e.matmul(bank[:, :], xT[:, k.b, a, c, :],
                                   w13s[:, b_, bass.ds(ex_reg * (G * 2 * I) + (c * 2 * I + at), I)],
                                   start=(c == 0 and (a, b_) == PARTS[0]),
                                   stop=(c == G - 1 and (a, b_) == PARTS[-1]))
        done(i, "gu")

    def silu(k):
        k.wait("gu")
        k.wait("hm", 2)
        done(k.e.activation(sg[:, k.b, :], bGate[k.b][:, :], ACT.Silu, scale=1.0 / W_SCALE), "sg")

    def h_mul(k):
        k.wait("sg")
        k.wait("hhi", 2)
        k.wait("hlo", 2)
        done(k.e.scalar_tensor_tensor(out=hf[:, k.b, :], in0=bUp[k.b][:, :], scalar=1.0 / W_SCALE, in1=sg[:, k.b, :],
                                      op0=ALU.mult, op1=ALU.mult), "hm")

    def h_hi(k):
        k.wait("hm")
        k.wait("hTr", 2)
        k.wait("hlo", 2)
        done(k.e.activation(hs[:, k.b, 0, :], hf[:, k.b, :], ACT.Copy), "hhi")

    def h_lo(k):
        k.wait("hhi")
        k.wait("hTr", 2)
        done(k.e.tensor_tensor(hs[:, k.b, 1, :], hf[:, k.b, :], hs[:, k.b, 0, :], ALU.subtract), "hlo")

    def h_trans(k):
        k.wait("hlo")
        k.wait("hT", 1)
        for a in range(2):
            for c in range(KC):
                i = k.e.transpose(bHh[:, (a * KC + c) * P:(a * KC + c + 1) * P],
                                  hs[:, k.b, a, c * P:(c + 1) * P], idh[:, :])
        done(i, "hTr")

    def h_copy(k):
        k.wait("hTr")
        k.wait("y", 2)
        done(k.e.tensor_copy(hT[:, k.b, :, :, :].rearrange("p a c t -> p (a c t)"), bHh[:, :]), "hT")

    def down(k):
        k.wait_apart(("hT",), ("yw", 2))
        ex_reg = k.e.value_load(ex_i[0:1, bass.ds(k.t, 1)], min_val=0, max_val=E - 1)
        for c in range(KC):
            for a, b_ in PARTS:
                i = k.e.matmul(bY[k.b][:, 0:D], hT[:, k.b, a, c, :], w2s[:, b_, bass.ds(ex_reg * (KC * D) + c * D, D)],
                               start=(c == 0 and (a, b_) == PARTS[0]), stop=(c == KC - 1 and (a, b_) == PARTS[-1]))
        done(i, "y")

    def weigh(k):
        k.arrived(s_gw)
        k.wait("ws", 2)
        done(k.e.tensor_tensor(gwm[:, k.b, :], gw[:, k.j, :],
                               oh_tile[:, bass.ds(k.t, 1), :].rearrange("p o e -> p (o e)"), ALU.mult), "wm")
        k.wait("wm")
        k.wait("yw", 2)
        done(k.e.tensor_reduce(wrow[:, k.b, :], gwm[:, k.b, :], axis=X, op=ALU.add), "ws")
        k.wait("y")
        k.wait("ws")
        k.arrived(s_g)
        k.arrived(s_sc, U)
        done(k.e.scalar_tensor_tensor(out=yo[:, k.j, :], in0=bY[k.b][:, 0:D], scalar=wrow[:, k.b, :],
                                      in1=grow[:, k.j, 2 * D:4 * D].bitcast(F32), op0=ALU.mult, op1=ALU.mult), "yw")

    def scatter(k):
        apart(k.e, passed, [k.when("yw"), k.added(1)])
        k.e.indirect_dma_start(out_rows, bass.IndirectOffsetOnAxis(ap=si[:, k.j, :], axis=0), yo[:, k.j, :], None,
                               bounds_check=B * T - 1, oob_is_err=False, compute_op=ALU.add).then_inc(s_sc[k.j], 16)

    program = {
        "tensor": [(2, x_trans), (3, gate_up), (4, h_trans), (5, down)],
        "vector": [(0, indices), (6, weigh), (2, x_copy), (4, h_copy), (3, h_mul), (3, h_lo)],
        "scalar": [(3, silu), (3, h_hi)],
        "gpsimd": [(0, gather), (6, scatter)],
    }
    owner = {m: "vector" for m in names}
    owner.update({m: "tensor" for m in "xTr gu hTr y".split()})
    owner.update({m: "scalar" for m in "sg hhi".split()})

    with nc.Block() as block:
        def engine_program(name, e):
            for m in names:
                if owner[m] == name:
                    e.sem_inc(S[m], PRE)
            stages = program[name]
            periods = -(-max(lag for lag, _ in stages) // U)

            def slot(s, j):
                for lag, stage_ in stages:
                    back, jj = (j - lag) // U, (j - lag) % U
                    if isinstance(s, int) and not (0 <= U * (s + back) + jj < NW):
                        continue
                    stage_(Slot(e, s + back, jj))

            for s in range(periods):
                for j in range(U):
                    slot(s, j)
            with e.Fori(periods, NW // U) as s:
                for j in range(U):
                    slot(s, j)
            for s in range(NW // U, (NW - 1) // U + 1 + periods):
                for j in range(U):
                    slot(s, j)

        @block.tensor
        def _(e):
            engine_program("tensor", e)

        @block.vector
        def _(e):
            engine_program("vector", e)

        @block.scalar
        def _(e):
            engine_program("scalar", e)

        @block.gpsimd
        def _(e):
            engine_program("gpsimd", e)
            for i in range(U):
                e.wait_ge(s_sc[i], 16 * (-(-(NW - i) // U)))


def constants():
    bf16 = mybir.dt.to_np(BF16) if hasattr(mybir.dt, "to_np") else np.dtype("bfloat16")
    p = np.arange(P)
    head = p // DK
    block = (head[:, None] == head[None, :]).astype(np.float32)
    onto = (head[:, None] == np.arange(HG)[None, :]).astype(np.float32)
    causal = np.where(np.arange(SEG)[None, :] > (p % SEG)[:, None], np.float32(NEG), np.float32(0))
    n = np.arange(NSLOT_TILES)
    t = np.arange(NT)
    return dict(
        ident=np.eye(P, dtype=np.float32),
        head_of_row=((head % 4)[:, None] == np.arange(4)[None, :]).astype(np.float32),
        mem_mask=np.concatenate([block, onto], 1),
        q_onehot=((p % SEG)[:, None] == (p % SEG)[None, :]).astype(bf16),
        causal=np.tile(causal, (1, 8)).astype(bf16),
        tri=np.stack([(p[:, None] < p[None, :]), np.ones((P, P), bool)], 1).astype(bf16),
        iotas=np.broadcast_to(np.stack([n, P * n, E - n, n]).astype(np.float32), (P, 4, NSLOT_TILES)).copy(),
        tok_a=np.broadcast_to(((2 * (t % NJ)) * (T // SEG) + t // NJ + 1).astype(np.float32), (P, NT)).copy(),
        tok_b=((p // SEG) * T + p % SEG).astype(np.float32)[:, None],
    )


def kernel(**inputs):
    import concourse.bacc as bacc
    from concourse.bass_utils import run_bass_kernel_spmd

    a = {k[3:]: np.asarray(v) for k, v in inputs.items()}
    c = np.ascontiguousarray
    data = dict(
        x=a["attn_x"], cT=c(a["c"].T), wmod=a["wmod"], wqT=c(a["attn_W_q"].T), wkT=c(a["attn_W_k"].T),
        wvT=c(a["attn_W_v"].T), woT=c(a["attn_W_o"].T), beta=a["attn_beta_param"], rwT=c(a["ffn_router_w"].T),
        w13=a["ffn_w13"], w2=a["ffn_w2"], **constants(),
    )
    nc = bacc.Bacc("TRN2", target_bir_lowering=False, num_devices=1)
    arrays, args = {}, {}
    for name, v in data.items():
        arrays[f"in_{name}"] = v
        args[name] = nc.dram_tensor(f"in_{name}", v.shape, mybir.dt.from_np(v.dtype), kind="ExternalInput").ap()
    out = nc.dram_tensor("out", [B, T, D], F32, kind="ExternalOutput").ap()
    adaln_block(nc, out=out, **args)
    r = run_bass_kernel_spmd(nc, [arrays], core_ids=[0])
    return r.results[0]["out"]
```

```python
from contextlib import ExitStack

import numpy as np

import concourse.bass as bass
from concourse import mybir

F32 = mybir.dt.float32
F16 = mybir.dt.float16
BF16 = mybir.dt.bfloat16
I32 = mybir.dt.int32
ALU = mybir.AluOpType
ACT = mybir.ActivationFunctionType
X = mybir.AxisListType.X

P = 128
B, T, D = 8, 1024, 256
H, DK, SEG = 16, 16, 64
NJ = B // 2
NS = T // SEG
NT = NJ * NS
G = D // P
HG = P // DK
MW = P + HG
NPAIR = H // 2
VW = 2 * DK + 1
E, I = 8, 512
NSLOT_TILES = (B * T * 2) // P + E - 1
KC = I // P
ROW = 2 * D + E
NHOT = 8
W_SCALE = 32.0
EPS_LN, EPS_MEM, EPS_TOP = 1e-5, 1e-6, 1e-6
NEG = -1e30
PRE = 4
FIRST = 16
PARTS = ((0, 0), (0, 1), (1, 0))
OOB = B * T + 4096


def bc(ap, n):
    return ap.unsqueeze(2).to_broadcast([ap.shape[0], ap.shape[1], n])


def bc_mid(ap, n):
    return ap.unsqueeze(1).to_broadcast([ap.shape[0], n, ap.shape[1]])


def apart(e, passed, waits):
    for s, v in waits:
        if not (isinstance(v, int) and v <= 0):
            e.wait_ge(s, v)
    e.sem_inc(passed, 1)


def adaln_block(nc, x, cT, wmod, wqT, wkT, wvT, woT, beta, rwT, w13, w2, ident, head_of_row, mem_mask,
                q_onehot, causal, rows_of_batch, tri, iotas, counting, token_a, token_b, out):
    rows_dram = nc.dram_tensor("moe_rows", [B * T, ROW], F32, kind="Internal").ap()
    out_rows = out.rearrange("b t d -> (b t) d")

    with ExitStack() as whole:
        def sb(name, shape, dt=F32, ctx=whole):
            return ctx.enter_context(nc.sbuf_tensor(name, shape, dt))

        def sem(name, ctx=whole):
            return ctx.enter_context(nc.semaphore(name))

        passed = sem("passed")
        w13s = sb("w13s", [P, 2, E * G * 2 * I], F16)
        idf = sb("idf", [P, P])
        idh = sb("idh", [P, P], F16)
        logits = sb("logits", [P, E, NT])
        trib = sb("trib", [P, 2, P], BF16)
        iota = sb("iota", [P, 4, NSLOT_TILES])
        count = sb("count", [P, NSLOT_TILES, NHOT], F16)
        tok_a = sb("tok_a", [P, 2 * NT], F16)
        tok_b = sb("tok_b", [P, 1])
        psum = whole.enter_context(nc.psum_tensor("psum", [P, 8, 512], F32))
        banks = [psum[:, i, :] for i in range(8)]

        with ExitStack() as att:
            routing_constants = ((trib[:, :, :], tri), (iota[:, :, :], iotas), (count[:, :, :], counting),
                                 (tok_a[:, :], token_a), (tok_b[:, :], token_b))
            attention(nc, att, sb, sem, psum, banks, x, cT, wmod, wqT, wkT, wvT, woT, beta, rwT, ident,
                      head_of_row, mem_mask, q_onehot, causal, rows_of_batch, routing_constants, out, rows_dram,
                      idf, idh, logits, passed)
        with ExitStack() as moe:
            experts(nc, moe, sb, sem, banks, trib, iota, count, tok_a, tok_b, out_rows, rows_dram,
                    w13s, w13, w2, idh, logits, passed)


def attention(nc, ctx, sb_, sem_, psum, banks, x, cT, wmod, wqT, wkT, wvT, woT, beta, rwT, ident,
              head_of_row, mem_mask, q_onehot, causal, rows_of_batch, routing_constants, out, rows_dram,
              idf, idh, logits, passed):
    def sb(name, shape, dt=F32):
        return sb_(name, shape, dt, ctx)

    def sem(name):
        return sem_(name, ctx)

    wqkv = sb("wqkv", [P, 2, G, 3 * D], F16)
    wo = sb("wo", [P, G, D])
    rw = sb("rw", [P, G, E])
    rws = sb("rws", [P, 2, G, E], F16)
    hrow = sb("hrow", [P, 4])
    mmask = sb("mmask", [P, G, MW])
    onehot = sb("onehot", [P, P], BF16)
    cmask = sb("cmask", [P, 8 * SEG], BF16)
    mods = sb("mods", [P, 5, NJ, D])
    sA, sCA, sGA, sB2, sCB, sGB = range(6)
    inv_beta = sb("inv_beta", [P, H])
    om_beta = sb("om_beta", [P, NPAIR])
    mhalf = sb("mhalf", [P, 1])

    vs = sb("vs", [P, 4, 2, NPAIR, VW], F16)
    vp = sb("vp", [P, 2, G, MW])
    mem = sb("mem", [P, NJ, 2, G, MW])
    hrows = sb("hrows", [P, 4, 4 * D], F16)

    set_up = ExitStack()
    cs = sb_("cs", [P, G, B], F32, set_up)
    wq32 = sb_("wq32", [P, G, 3 * D], F32, set_up)
    btile = sb_("btile", [P, H], F32, set_up)
    wmod_sb = sb_("wmod_sb", [P, G, 6 * D], F32, set_up)
    mod8 = sb_("mod8", [B, 6, D], F32, set_up)
    mod8s = sb_("mod8s", [B, 2, 6 * D], F16, set_up)
    gate_sign = sb_("gate_sign", [B, 2, D], F32, set_up)
    batch_rows = sb_("batch_rows", [B, NJ, P], F16, set_up)

    bkA, bkB, bkC, bkD, bkE, bkF, bkG, bkH = banks
    bkBC, bkDE, bkFG = psum[:, 1:3, :], psum[:, 3:5, :], psum[:, 5:7, :]
    bkAh, bkFh, bkGh = (b_.bitcast(F16) for b_ in (bkA, bkF, bkG))

    s_first, s_ld, s_c = sem("s_first"), sem("s_ld"), sem("s_c")
    s_act, s_gb, s_mod, s_m8, s_rep = sem("s_act"), sem("s_gb"), sem("s_mod"), sem("s_m8"), sem("s_rep")
    s_revD, s_revA = sem("s_revD"), sem("s_revA")

    first_loads = [(cs[:, :, :], cT.rearrange("(c p) b -> p c b", p=P)),
                   (wmod_sb[:, :, :], wmod.rearrange("(c p) n -> p c n", p=P)),
                   (batch_rows[:, :, :], rows_of_batch)]
    loads = [(btile[:, :], beta.rearrange("(a h) -> a h", a=1).to_broadcast([P, H])),
             (rw[:, :, :], rwT.rearrange("(c p) n -> p c n", p=P)),
             (idf[:, :], ident), (hrow[:, :], head_of_row), (mmask[:, :, :], mem_mask),
             *((wq32[:, :, n * D:(n + 1) * D], w.rearrange("(c p) n -> p c n", p=P))
               for n, w in enumerate((wqT, wkT, wvT))),
             (wo[:, :, :], woT.rearrange("(c p) n -> p c n", p=P)),
             (onehot[:, :], q_onehot), (cmask[:, :], causal), *routing_constants]

    with nc.Block() as block:
        @block.gpsimd
        def _(e):
            for dst, src in loads:
                e.dma_start(dst, src).then_inc(s_ld, 16)
            e.memset(mem[:, :, :, :, :], 0.0).then_inc(s_c, 1)
            e.memset(mhalf[:, :], -0.5).then_inc(s_c, 1)
            for b_ in range(4):
                e.memset(vs[:, b_, 0, :, 2 * DK:VW], 1.0).then_inc(s_c, 1)
                e.memset(vs[:, b_, 1, :, 2 * DK:VW], 0.0).then_inc(s_c, 1)
            for b_ in range(2):
                e.memset(vp[:, b_, :, P:MW], 1.0).then_inc(s_c, 1)

        @block.sync
        def _(e):
            for dst, src in first_loads:
                e.dma_start(dst, src).then_inc(s_first, 16)

        def replica(j):
            return psum[:, 3 * (j % 2):3 * (j % 2) + 3, :].rearrange("p b (h d) -> p (b h) d", h=2)

        @block.scalar
        def _(e):
            e.wait_ge(s_first, 16 * len(first_loads))
            e.activation(cs[:, :, :], cs[:, :, :], ACT.Silu).then_inc(s_act, 1)
            e.wait_ge(s_m8, 1)
            e.activation(mod8s[:, 0, :], mod8[:, :, :].rearrange("b k d -> b (k d)"), ACT.Copy).then_inc(s_act, 1)
            e.wait_ge(s_ld, 16 * len(loads))
            e.activation(btile[:, :], btile[:, :], ACT.Exp, scale=-1.0).then_inc(s_act, 1)
            e.activation(idh[:, :], idf[:, :], ACT.Copy).then_inc(s_act, 1)
            e.activation(rws[:, 0, :, :], rw[:, :, :], ACT.Copy, scale=W_SCALE).then_inc(s_act, 1)
            e.activation(wqkv[:, 0, :, :], wq32[:, :, :], ACT.Copy, scale=W_SCALE).then_inc(s_act, 1)
            for j in range(NJ):
                e.wait_ge(s_rep, j + 1)
                e.activation(mods[:, sCB, j, :], replica(j)[:, sCB, :], ACT.Copy).then_inc(s_c, 1)
                e.activation(hrows[:, j, 2 * D:4 * D].bitcast(F32), replica(j)[:, sGB, :], ACT.Copy).then_inc(s_revA, 1)

        @block.vector
        def _(e):
            by_kind = psum[0:B, 0:3, :].rearrange("p b (h d) -> p (b h) d", h=2)
            e.wait_ge(s_mod, 1)
            e.tensor_copy(mod8[:, 0::3, :], by_kind[:, 0::3, :])
            e.tensor_scalar(mod8[:, 1::3, :], by_kind[:, 1::3, :], 1.0, None, ALU.add)
            gates = mod8[:, 2::3, :]
            e.tensor_scalar(gate_sign[:, :, :], by_kind[:, 2::3, :], 0.0, None, ALU.is_ge).then_inc(s_gb, 1)
            e.wait_ge(s_gb, 1)
            e.tensor_scalar(gate_sign[:, :, :], gate_sign[:, :, :], 2.0, -1.0, ALU.mult, ALU.add).then_inc(s_gb, 1)
            e.wait_ge(s_gb, 2)
            e.tensor_tensor(gates, by_kind[:, 2::3, :], gate_sign[:, :, :], ALU.mult).then_inc(s_gb, 1)
            e.wait_ge(s_gb, 3)
            e.scalar_tensor_tensor(out=gates, in0=gates, scalar=0.25, in1=gate_sign[:, :, :], op0=ALU.max,
                                   op1=ALU.mult).then_inc(s_m8, 1)
            e.wait_ge(s_act, 2)
            e.wait_ge(s_m8, 1)
            e.tensor_tensor(mod8s[:, 1, :], mod8[:, :, :].rearrange("b k d -> b (k d)"), mod8s[:, 0, :],
                            ALU.subtract).then_inc(s_m8, 1)
            e.wait_ge(s_act, 6)
            e.scalar_tensor_tensor(out=wqkv[:, 1, :, :], in0=wq32[:, :, :], scalar=W_SCALE, in1=wqkv[:, 0, :, :],
                                   op0=ALU.mult, op1=ALU.subtract)
            e.scalar_tensor_tensor(out=rws[:, 1, :, :], in0=rw[:, :, :], scalar=W_SCALE, in1=rws[:, 0, :, :],
                                   op0=ALU.mult, op1=ALU.subtract).then_inc(s_gb, 1)
            e.tensor_scalar(btile[:, :], btile[:, :], 1.0, None, ALU.add).then_inc(s_gb, 1)
            e.memset(inv_beta[SEG:P, :], 1.0)
            e.wait_ge(s_gb, 5)
            e.tensor_copy(inv_beta[0:SEG, :], btile[0:SEG, :]).then_inc(s_gb, 1)
            e.wait_ge(s_gb, 6)
            e.reciprocal(btile[:, :], btile[:, :]).then_inc(s_gb, 1)
            e.wait_ge(s_gb, 7)
            pair = btile[:, :].rearrange("p (n two) -> p two n", two=2)
            for par in range(2):
                rows = slice(par * SEG, (par + 1) * SEG)
                e.tensor_scalar(om_beta[rows, :], pair[rows, par, :], -1.0, 1.0, ALU.mult, ALU.add).then_inc(s_gb, 1)
            for j in range(NJ):
                e.wait_ge(s_rep, j + 1)
                e.tensor_copy(mods[:, 0:4, j, :], replica(j)[:, 0:4, :]).then_inc(s_revD, 1)

        @block.tensor
        def _(e):
            e.wait_ge(s_act, 1)
            for n in range(3):
                for c in range(G):
                    mm = e.matmul(banks[n][0:B, :], cs[:, c, :], wmod_sb[:, c, n * 512:(n + 1) * 512],
                                  start=(c == 0), stop=(c == G - 1))
            mm.then_inc(s_mod, 1)
            e.wait_ge(s_m8, 2)
            for j in range(NJ):
                if j >= 2:
                    e.wait_ge(s_revD, j - 1)
                    e.wait_ge(s_revA, j - 1)
                for n in range(3):
                    for a in range(2):
                        mm = e.matmul(banks[3 * (j % 2) + n][:, :], batch_rows[:, j, :],
                                      mod8s[:, a, n * 512:(n + 1) * 512], start=(a == 0), stop=(a == 1))
                mm.then_inc(s_rep, 1)

    set_up.close()

    xin = sb("xin", [P, 4, D])
    bst = sb("bst", [P, 4, 6])
    mv = sb("mv", [P, 4, 2])
    rstd, nmr = sb("rstd", [P, 4, 1]), sb("nmr", [P, 4, 1])
    h1 = sb("h1", [P, 2, D])
    h1T = sb("h1T", [P, 2, 2, G, P], F16)
    qk = sb("qk", [P, 2, 2, 2 * D], F16)
    qm = sb("qm", [P, 2, 2, 4, 4, SEG], F16)
    ex = sb("ex", [P, 2, 512])
    rel = sb("rel", [P, 2, 512])
    sig = sb("sig", [P, 2, G, 2, 2, SEG])
    v32 = sb("v32", [P, 2, D])
    mx = sb("mx", [P, 2, 16])
    sc = sb("sc", [P, 2, 16, SEG])
    ph = sb("ph", [P, 2, 2, 16, SEG], F16)
    pT = sb("pT", [P, 2, 2, 8, P], F16)
    rr = sb("rr", [P, 2, 2, NPAIR])
    att_o = sb("att_o", [P, 2, D])
    dd = sb("dd", [P, 2, 2, H])
    memA = sb("memA", [P, 4, D])
    skt = sb("skt", [P, 2, D])
    upd = sb("upd", [P, 2, G, MW])
    aT = sb("aT", [P, 2, G, P])
    xres = sb("xres", [P, 2, D])
    x1 = sb("x1", [P, 4, D])
    bst2 = sb("bst2", [P, 4, 6])
    mv2 = sb("mv2", [P, 4, 2])
    rstd2, nmr2 = sb("rstd2", [P, 4, 1]), sb("nmr2", [P, 4, 1])
    h2 = sb("h2", [P, 2, D])
    h2T = sb("h2T", [P, 2, 2, G, P], F16)

    names = ("stats aggr nm eps pow nmr xn lna lnb T1 h1T h1L pqk pv qkh exq rel v32 vhi vlo qlo sig qm scr mx sub "
             "exp phi plo "
             "PTr ptA ptl memm den rec mA mV vpr skT skt upm umul madd PV rcp rom ado aadd AT aT Wo "
             "gat res st2 ag2 nn2 ep2 pw2 nm2 xn2 l2a l2b hhi hlo h2Tr h2T rtr lg").split()
    S = {n: sem("a_" + n) for n in names}
    s_x = [sem(f"s_x{j}") for j in range(4)]
    s_xr = [sem(f"s_xr{j}") for j in range(4)]
    s_st = [sem(f"s_st{j}") for j in range(4)]

    BANK_FREE = {
        "pv": ((("sub", -2),),
               (("ado", 1),)),
        "w_o": ((("skt", -3),),
                (("gat", 1),)),
        "h2_trans": ((("h1L", -8),),
                     (("aT", -3), ("lg", 1), ("h2T", 1))),
        "p_trans": ((("mA", -1), ("mV", -1)),
                    (("ptA", 1), ("ptl", 1))),
        "update": ((("qlo", -1), ("v32", -1)),
                   (("umul", 1),)),
        "router": ((("h2T", 0),),
                   (("h1L", -8), ("aT", -3), ("lg", 1))),
        "scores": ((("ado", 3),),
                   (("sub", 1),)),
        "a_trans": ((("lg", 4),),
                    (("h2T", 4), ("h1L", -4), ("aT", 1))),
        "mem_mm": ((("ptA", 2), ("ptl", 2)),
                   (("mA", 1), ("mV", 1))),
        "sk_trans": ((("gat", 4),),
                     (("skt", 1),)),
        "t1": ((("aT", 5),),
               (("lg", 9), ("h2T", 9), ("h1L", 1))),
        "proj": ((("umul", 2),),
                 (("qlo", 1), ("v32", 1))),
    }

    class Tile:

        def __init__(self, e, s, j):
            self.e, self.s, self.j, self.b = e, s, j, j % 2
            self.t = s * 4 + j

        def when(self, stage, back=0):
            if isinstance(self.s, int):
                of = min(self.t - back, NT - 1)
                return S[stage], max(of, -1) + 1 + PRE
            return S[stage], self.s * 4 + (self.j - back + 1 + PRE)

        def wait(self, stage, back=0):
            if not isinstance(self.s, int) or self.t >= back:
                self.e.wait_ge(*self.when(stage, back))

        def wait_banks(self, name):
            latest, others = BANK_FREE[name]
            for stage, back in latest + (others if isinstance(self.s, int) else ()):
                self.wait(stage, back)

        def wait_apart(self, *stages):
            apart(self.e, passed, [self.when(*w) for w in stages])

        def arrived(self, sems, n=1):
            self.e.wait_ge(sems[self.j], self.s * (16 * n) + 16 * n)

        def stored(self):
            if not isinstance(self.s, int) or self.s > 0:
                self.e.wait_ge(s_st[self.j], self.s * 64 + FIRST)

    def done(ins, stage):
        ins.then_inc(S[stage], 1)

    def load_x(k):
        k.wait("xn", 4)
        for b2 in range(2):
            k.e.dma_start(xin[b2 * SEG:(b2 + 1) * SEG, k.j, :],
                          x[2 * k.j + b2, bass.ds(k.s * SEG, SEG), :]).then_inc(s_x[k.j], 16)

    def load_res(k):
        k.wait("res", 2)
        for b2 in range(2):
            k.e.dma_start(xres[b2 * SEG:(b2 + 1) * SEG, k.b, :],
                          x[2 * k.j + b2, bass.ds(k.s * SEG, SEG), :]).then_inc(s_xr[k.j], 16)

    def store(k):
        k.wait_apart(("hlo",))
        for b2 in range(2):
            rows = slice(b2 * SEG, (b2 + 1) * SEG)
            k.e.dma_start(out[2 * k.j + b2, bass.ds(k.s * SEG, SEG), :], x1[rows, k.j, :]).then_inc(s_st[k.j], 16)
            k.e.dma_start(rows_dram[bass.ds(k.s * SEG + (2 * k.j + b2) * T, SEG), 0:2 * D],
                          hrows[rows, k.j, :].bitcast(F32)).then_inc(s_st[k.j], 16)

    def stats(k):
        k.arrived(s_x, 2)
        k.wait("aggr", 4)
        done(k.e.bn_stats(bst[:, k.j, :], xin[:, k.j, :]), "stats")

    def aggr(k):
        k.wait_apart(("stats",), ("eps", 4))
        done(k.e.bn_aggr(mv[:, k.j, :], bst[:, k.j, :]), "aggr")

    def var_eps(k):
        k.wait("aggr")
        k.wait("xn", 4)
        done(k.e.tensor_scalar(nmr[:, k.j, :], mv[:, k.j, 0:1], -1.0, None, ALU.mult), "nm")
        done(k.e.tensor_scalar(rstd[:, k.j, :], mv[:, k.j, 1:2], EPS_LN, None, ALU.add), "eps")

    def ln_scale(k):
        k.wait("eps")
        done(k.e.tensor_tensor(rstd[:, k.j, :], rstd[:, k.j, :], mhalf[:, :], ALU.pow), "pow")

    def ln_shift(k):
        k.wait("pow")
        k.wait("nm")
        done(k.e.activation(nmr[:, k.j, :], nmr[:, k.j, :], ACT.Copy, scale=rstd[:, k.j, :]), "nmr")

    def ln_act(k):
        k.wait("nmr")
        k.wait("T1", 2)
        done(k.e.activation(h1[:, k.b, :], xin[:, k.j, :], ACT.Identity, bias=nmr[:, k.j, :],
                            scale=rstd[:, k.j, :]), "xn")

    def ln_mult(k):
        k.wait("xn")
        done(k.e.tensor_tensor(h1[:, k.b, :], h1[:, k.b, :], mods[:, sCA, k.j, :], ALU.mult), "lna")

    def ln_add(k):
        k.wait("lna")
        done(k.e.tensor_tensor(h1[:, k.b, :], h1[:, k.b, :], mods[:, sA, k.j, :], ALU.add), "lnb")

    def t1(k):
        k.wait("lnb")
        k.wait_banks("t1")
        for c in range(G):
            i = k.e.transpose(bkA[:, c * P:(c + 1) * P], h1[:, k.b, c * P:(c + 1) * P], idf[:, :])
        done(i, "T1")

    def h1t(k):
        k.wait("T1")
        k.wait("pv", 2)
        k.wait("h1L", 2)
        done(k.e.activation(h1T[:, k.b, 0, :, :].rearrange("p c t -> p (c t)"), bkA[:, 0:D], ACT.Copy), "h1T")

    def h1t_rest(k):
        k.wait("h1T")
        k.wait("pv", 2)
        done(k.e.tensor_tensor(h1T[:, k.b, 1, :, :].rearrange("p c t -> p (c t)"), bkA[:, 0:D],
                               h1T[:, k.b, 0, :, :].rearrange("p c t -> p (c t)"), ALU.subtract), "h1L")

    def proj(k):
        k.wait("h1L")
        k.wait_banks("proj")
        for n in range(4):
            for c in range(G):
                for a, b_ in PARTS:
                    i = k.e.matmul(bkB[:, n * P:(n + 1) * P], wqkv[:, b_, c, n * P:(n + 1) * P], h1T[:, k.b, a, c, :],
                                   start=(c == 0 and (a, b_) == PARTS[0]),
                                   stop=(c == G - 1 and (a, b_) == PARTS[-1]))
        done(i, "pqk")
        for c in range(G):
            for a, b_ in PARTS:
                i = k.e.matmul(bkC[:, 0:D], h1T[:, k.b, a, c, :], wqkv[:, b_, c, 2 * D:3 * D],
                               start=(c == 0 and (a, b_) == PARTS[0]), stop=(c == G - 1 and (a, b_) == PARTS[-1]))
        done(i, "pv")

    def proj_act(k):
        k.wait("pqk")
        k.wait("scr", 2)
        k.wait("qm", 2)
        k.wait("qlo", 2)
        done(k.e.activation(qk[:, k.b, 0, :], bkB[:, :], ACT.Copy, scale=1.0 / W_SCALE), "qkh")
        k.wait("sig", 2)
        done(k.e.activation(ex[:, k.b, :], bkB[:, :], ACT.Exp, scale=1.0 / W_SCALE), "exq")
        done(k.e.activation(rel[:, k.b, :], bkB[:, :], ACT.Relu, scale=1.0 / W_SCALE), "rel")
        k.wait("pv")
        k.wait("vpr", 2)
        k.wait("vlo", 2)
        done(k.e.activation(v32[:, k.b, :], bkC[:, 0:D], ACT.Copy, scale=1.0 / W_SCALE), "v32")
        k.wait("PV", 4)
        k.wait("vlo", 4)
        k.wait("v32")
        done(k.e.activation(vs[:, k.j, 0, :, 0:2 * DK], v32[:, k.b, :].rearrange("p (n w) -> p n w", w=2 * DK),
                            ACT.Copy), "vhi")

    def v_rest(k):
        k.wait("vhi")
        k.wait("PV", 4)
        done(k.e.tensor_tensor(vs[:, k.j, 1, :, 0:2 * DK], v32[:, k.b, :].rearrange("p (n w) -> p n w", w=2 * DK),
                               vs[:, k.j, 0, :, 0:2 * DK], ALU.subtract), "vlo")

    def q_rest(k):
        k.wait("rel")
        k.wait("scr", 2)
        done(k.e.scalar_tensor_tensor(out=qk[:, k.b, 1, :], in0=bkB[:, :], scalar=1.0 / W_SCALE, in1=qk[:, k.b, 0, :],
                                      op0=ALU.mult, op1=ALU.subtract), "qlo")

    def sigma(k):
        k.wait("rel")
        k.wait("memm", 2)
        k.wait("skT", 2)
        for a in range(2):
            i = k.e.scalar_tensor_tensor(
                out=sig[:, k.b, :, :, a, :].rearrange("p g b t -> p (g b) t"),
                in0=ex[:, k.b, a * D:(a + 1) * D].rearrange("p (n t) -> p n t", t=SEG), scalar=1.0,
                in1=rel[:, k.b, a * D:(a + 1) * D].rearrange("p (n t) -> p n t", t=SEG), op0=ALU.min, op1=ALU.add)
        done(i, "sig")

    def q_masks(k):
        k.wait("qlo")
        k.wait("qkh")
        k.wait("scr", 2)
        for m in range(4):
            i = k.e.tensor_scalar(qm[:, k.b, :, :, m, :], qk[:, k.b, :, 0:D].rearrange("p a (n t) -> p a n t", t=SEG),
                                  hrow[:, m:m + 1], None, ALU.mult)
        done(i, "qm")

    def scores(k):
        k.wait("qm")
        k.wait("qlo")
        k.wait_banks("scores")
        for half, bank in enumerate((bkD, bkE)):
            r = slice(half * SEG, (half + 1) * SEG)
            k.e.matmul(bank[:, :], onehot[r, :], cmask[r, :], start=True, stop=False, skip_group_check=True)
            for g in range(G):
                for u in range(2):
                    for b2 in range(2):
                        n = (g * 2 + u) * 2 + b2
                        keys = slice(D + g * P + b2 * SEG, D + g * P + (b2 + 1) * SEG)
                        for a, b_ in PARTS:
                            i = k.e.matmul(bank[:, n * SEG:(n + 1) * SEG],
                                           qm[r, k.b, a, g * 2 + b2, 2 * u:2 * u + 2, :].rearrange("p m t -> p (m t)"),
                                           qk[r, k.b, b_, keys], start=False,
                                           stop=(n == 7 and (a, b_) == PARTS[-1]), skip_group_check=True)
        done(i, "scr")

    def row_max(k):
        k.wait("scr")
        k.wait("sub", 2)
        done(k.e.tensor_reduce(mx[:, k.b, :], bkDE.rearrange("p h (n k) -> p (h n) k", k=SEG), axis=X,
                               op=ALU.max), "mx")

    def row_sub(k):
        k.wait("mx")
        k.wait("plo", 2)
        k.wait("phi", 2)
        done(k.e.tensor_tensor(sc[:, k.b, :, :], bkDE.rearrange("p h (n k) -> p (h n) k", k=SEG),
                               bc(mx[:, k.b, :], SEG), ALU.subtract), "sub")

    def softmax_act(k):
        k.wait("sub")
        flat = sc[:, k.b, :, :].rearrange("p n k -> p (n k)")
        done(k.e.activation(flat, flat, ACT.Exp, scale=DK ** -0.5), "exp")
        k.wait("exp")
        k.wait("PTr", 2)
        k.wait("plo", 2)
        done(k.e.activation(ph[:, k.b, 0, :, :].rearrange("p n k -> p (n k)"), flat, ACT.Copy), "phi")

    def p_rest(k):
        k.wait("phi")
        k.wait("PTr", 2)
        done(k.e.tensor_tensor(ph[:, k.b, 1, :, :], sc[:, k.b, :, :], ph[:, k.b, 0, :, :], ALU.subtract), "plo")

    def p_trans(k):
        k.wait("plo")
        k.wait("phi")
        k.wait_banks("p_trans")
        for a, bank in enumerate((bkFh, bkGh)):
            for n in range(8):
                i = k.e.transpose(bank[:, n * P:(n + 1) * P],
                                  ph[:, k.b, a, 2 * n:2 * n + 2, :].rearrange("p n k -> p (n k)"), idh[:, :])
        done(i, "PTr")

    def pt_act(k):
        k.wait("PTr")
        k.wait("PV", 2)
        done(k.e.activation(pT[:, k.b, 0, :, :].rearrange("p n t -> p (n t)"), bkFh, ACT.Copy), "ptA")

    def pt_rest(k):
        k.wait("PTr")
        k.wait("PV", 2)
        done(k.e.activation(pT[:, k.b, 1, :, :].rearrange("p n t -> p (n t)"), bkGh, ACT.Copy), "ptl")

    def mem_mm(k):
        k.wait("sig")
        k.wait("madd", 4)
        k.wait_banks("mem_mm")
        for b2, bank in enumerate((bkF, bkG)):
            for g in range(G):
                i = k.e.matmul(bank[:, g * MW:(g + 1) * MW], sig[:, k.b, g, b2, :, :].rearrange("p a t -> p (a t)"),
                               mem[:, k.j, b2, g, :], start=True, stop=True)
        done(i, "memm")

    def mem_den(k):
        k.wait("memm")
        k.wait("mA", 2)
        k.wait("mV", 2)
        for b2, bank in enumerate((bkF, bkG)):
            i = k.e.scalar_tensor_tensor(
                out=dd[:, k.b, b2, :].rearrange("p (g h) -> p g h", g=G),
                in0=bank[:, 0:G * MW].rearrange("p (g w) -> p g w", w=MW)[:, :, P:MW], scalar=EPS_MEM,
                in1=inv_beta[:, :].rearrange("p (g h) -> p g h", g=G), op0=ALU.add, op1=ALU.mult)
        done(i, "den")

    def mem_rec(k):
        k.wait("den")
        flat = dd[:, k.b, :, :].rearrange("p b h -> p (b h)")
        done(k.e.reciprocal(flat, flat), "rec")

    def mem_dve(k):
        fg = [bank[:, 0:G * MW].rearrange("p (g w) -> p g w", w=MW) for bank in (bkF, bkG)]
        k.wait("rec")
        k.wait("upm", 2)
        for b2 in range(2):
            i = k.e.tensor_tensor(
                vp[b2 * SEG:(b2 + 1) * SEG, k.b, :, 0:P].rearrange("p g (h d) -> p g h d", h=HG),
                fg[b2][SEG:P, :, 0:P].rearrange("p g (h d) -> p g h d", d=DK),
                dd[SEG:P, k.b, b2, :].rearrange("p (g h) -> p g h", g=G).unsqueeze(3).to_broadcast([SEG, G, HG, DK]),
                ALU.mult)
        done(i, "mV")
        k.wait("aadd", 4)
        for b2 in range(2):
            i = k.e.tensor_tensor(
                memA[b2 * SEG:(b2 + 1) * SEG, k.j, :].rearrange("p (g h d) -> p g h d", g=G, h=HG),
                fg[b2][0:SEG, :, 0:P].rearrange("p g (h d) -> p g h d", d=DK),
                dd[0:SEG, k.b, b2, :].rearrange("p (g h) -> p g h", g=G).unsqueeze(3).to_broadcast([SEG, G, HG, DK]),
                ALU.mult)
        done(i, "mA")

    def v_new(k):
        k.wait("mV")
        k.wait("v32")
        k.wait("upm", 2)
        done(k.e.tensor_tensor(vp[:, k.b, :, 0:P], v32[:, k.b, :].rearrange("p (g w) -> p g w", g=G),
                               vp[:, k.b, :, 0:P], ALU.subtract), "vpr")

    def sk_trans(k):
        k.wait("sig")
        k.wait_banks("sk_trans")
        k.e.sem_inc(passed, 1)
        for b2 in range(2):
            for g in range(G):
                i = k.e.transpose(bkH[0:SEG, b2 * D + g * P:b2 * D + (g + 1) * P], sig[:, k.b, g, b2, 1, :], idf[:, :])
        done(i, "skT")

    def sk_act(k):
        k.wait("skT")
        k.wait("upm", 2)
        for b2 in range(2):
            i = k.e.activation(skt[b2 * SEG:(b2 + 1) * SEG, k.b, :], bkH[0:SEG, b2 * D:(b2 + 1) * D], ACT.Copy)
        done(i, "skt")

    def update(k):
        k.wait("vpr")
        k.wait("skt")
        k.wait_banks("update")
        for b2, bank in enumerate((bkB, bkC)):
            r = slice(b2 * SEG, (b2 + 1) * SEG)
            for g in range(G):
                i = k.e.matmul(bank[:, g * MW:(g + 1) * MW], skt[r, k.b, g * P:(g + 1) * P], vp[r, k.b, g, :],
                               start=True, stop=True)
        done(i, "upm")

    def update_dve(k):
        k.wait("upm")
        k.wait("madd", 1)
        i = k.e.tensor_tensor(upd[:, :, :, :].rearrange("p b g w -> p b (g w)"), bkBC[:, :, 0:G * MW],
                              bc_mid(mmask[:, :, :].rearrange("p g w -> p (g w)"), 2), ALU.mult)
        done(i, "umul")

    def update_add(k):
        k.wait("umul")
        k.wait("memm")
        flat = mem[:, k.j, :, :, :].rearrange("p b g w -> p (b g w)")
        done(k.e.tensor_tensor(flat, flat, upd[:, :, :, :].rearrange("p b g w -> p (b g w)"), ALU.add), "madd")

    def pv(k):
        k.wait("ptl")
        k.wait("ptA")
        k.wait("vlo")
        k.wait_banks("pv")
        for b2, bank in enumerate((bkD, bkE)):
            r = slice(b2 * SEG, (b2 + 1) * SEG)
            for half in range(2):
                for gu in range(4):
                    pair = (gu // 2) * 4 + half * 2 + gu % 2
                    for a, b_ in PARTS:
                        i = k.e.matmul(bank[:, pair * VW:(pair + 1) * VW], pT[r, k.b, a, half * 4 + gu, :],
                                       vs[r, k.j, b_, pair, :], start=((a, b_) == PARTS[0]),
                                       stop=((a, b_) == PARTS[-1]))
        done(i, "PV")

    def pv_scale(k):
        k.wait("PV")
        k.wait("ado", 2)
        done(k.e.reciprocal(rr[:, k.b, :, :],
                            bkDE[:, :, 0:NPAIR * VW].rearrange("p b (n w) -> p b n w", w=VW)[:, :, :, 2 * DK]), "rcp")

    def pv_beta(k):
        k.wait("rcp")
        done(k.e.tensor_tensor(rr[:, k.b, :, :], rr[:, k.b, :, :], bc_mid(om_beta[:, :], 2), ALU.mult), "rom")

    def pv_dve(k):
        de = [bank[:, 0:NPAIR * VW].rearrange("p (n w) -> p n w", w=VW) for bank in (bkD, bkE)]
        k.wait("rom")
        k.wait("AT", 2)
        k.wait("aadd", 2)
        for b2 in range(2):
            for par in range(2):
                r = slice(par * SEG, (par + 1) * SEG)
                i = k.e.tensor_tensor(
                    att_o[b2 * SEG:(b2 + 1) * SEG, k.b, :].rearrange(
                        "p (n w) -> p n w", w=2 * DK)[:, :, par * DK:(par + 1) * DK],
                    de[b2][r, :, par * DK:(par + 1) * DK], bc(rr[r, k.b, b2, :], DK), ALU.mult)
        done(i, "ado")

    def a_add(k):
        k.wait("ado")
        k.wait("mA")
        done(k.e.tensor_tensor(att_o[:, k.b, :], att_o[:, k.b, :], memA[:, k.j, :], ALU.add), "aadd")

    def a_trans(k):
        k.wait("aadd")
        k.wait_banks("a_trans")
        for c in range(G):
            i = k.e.transpose(bkA[:, c * P:(c + 1) * P], att_o[:, k.b, c * P:(c + 1) * P], idf[:, :])
        done(i, "AT")

    def a_act(k):
        k.wait("AT")
        k.wait("Wo", 2)
        done(k.e.activation(aT[:, k.b, :, :].rearrange("p c t -> p (c t)"), bkA[:, 0:D], ACT.Copy), "aT")

    def w_o(k):
        k.wait("aT")
        k.wait_banks("w_o")
        for c in range(G):
            i = k.e.matmul(bkH[:, 0:D], aT[:, k.b, c, :], wo[:, c, :], start=(c == 0), stop=(c == G - 1))
        done(i, "Wo")

    def resid(k):
        k.wait("Wo")
        k.wait("xn2", 4)
        k.stored()
        done(k.e.tensor_tensor(x1[:, k.j, :], bkH[:, 0:D], mods[:, sGA, k.j, :], ALU.mult), "gat")

    def res_add(k):
        k.arrived(s_xr, 2)
        k.wait("gat")
        done(k.e.tensor_tensor(x1[:, k.j, :], x1[:, k.j, :], xres[:, k.b, :], ALU.add), "res")

    def stats2(k):
        k.wait("res")
        done(k.e.bn_stats(bst2[:, k.j, :], x1[:, k.j, :]), "st2")

    def aggr2(k):
        k.wait_apart(("st2",), ("ep2", 4))
        done(k.e.bn_aggr(mv2[:, k.j, :], bst2[:, k.j, :]), "ag2")

    def var_eps2(k):
        k.wait("ag2")
        k.wait("xn2", 4)
        done(k.e.tensor_scalar(nmr2[:, k.j, :], mv2[:, k.j, 0:1], -1.0, None, ALU.mult), "nn2")
        done(k.e.tensor_scalar(rstd2[:, k.j, :], mv2[:, k.j, 1:2], EPS_LN, None, ALU.add), "ep2")

    def ln2_scale(k):
        k.wait("ep2")
        done(k.e.tensor_tensor(rstd2[:, k.j, :], rstd2[:, k.j, :], mhalf[:, :], ALU.pow), "pw2")

    def ln2_shift(k):
        k.wait("pw2")
        k.wait("nn2")
        done(k.e.activation(nmr2[:, k.j, :], nmr2[:, k.j, :], ACT.Copy, scale=rstd2[:, k.j, :]), "nm2")

    def ln2_act(k):
        k.wait("nm2")
        k.wait("hhi", 2)
        k.wait("hlo", 2)
        done(k.e.activation(h2[:, k.b, :], x1[:, k.j, :], ACT.Identity, bias=nmr2[:, k.j, :],
                            scale=rstd2[:, k.j, :]), "xn2")

    def ln2_mult(k):
        k.wait("xn2")
        done(k.e.tensor_tensor(h2[:, k.b, :], h2[:, k.b, :], mods[:, sCB, k.j, :], ALU.mult), "l2a")

    def ln2_add(k):
        k.wait("l2a")
        done(k.e.tensor_tensor(h2[:, k.b, :], h2[:, k.b, :], mods[:, sB2, k.j, :], ALU.add), "l2b")

    def rows_hi(k):
        k.wait("l2b")
        k.stored()
        done(k.e.activation(hrows[:, k.j, 0:D], h2[:, k.b, :], ACT.Copy), "hhi")

    def rows_lo(k):
        k.wait("hhi")
        done(k.e.tensor_tensor(hrows[:, k.j, D:2 * D], h2[:, k.b, :], hrows[:, k.j, 0:D], ALU.subtract), "hlo")

    def h2_trans(k):
        k.wait("hhi")
        k.wait("hlo")
        k.wait_banks("h2_trans")
        for n in range(2 * G):
            i = k.e.transpose(bkAh[:, n * P:(n + 1) * P], hrows[:, k.j, n * P:(n + 1) * P], idh[:, :])
        done(i, "h2Tr")

    def h2_act(k):
        k.wait("h2Tr")
        k.wait("rtr", 2)
        done(k.e.activation(h2T[:, k.b, :, :, :].rearrange("p a c t -> p (a c t)"), bkAh[:, 0:2 * D], ACT.Copy), "h2T")

    def router(k):
        k.wait("h2T")
        k.wait_banks("router")
        for c in range(G):
            for a, b_ in PARTS:
                i = k.e.matmul(bkA[:, D:D + E], h2T[:, k.b, a, c, :], rws[:, b_, c, :],
                               start=(c == 0 and (a, b_) == PARTS[0]), stop=(c == G - 1 and (a, b_) == PARTS[-1]))
        done(i, "rtr")

    def logit_copy(k):
        k.wait("rtr")
        done(k.e.activation(logits[:, :, bass.ds(k.t, 1)].rearrange("p e o -> p (e o)"), bkA[:, D:D + E], ACT.Copy,
                               scale=1.0 / W_SCALE), "lg")

    program = {
        "sync": [(12, store), (9, load_res), (0, load_x)],
        "tensor": [(12, pv), (13, w_o), (16, h2_trans), (11, p_trans), (10, update), (16, router), (9, scores),
                   (12, a_trans), (9, mem_mm), (9, sk_trans), (7, t1), (8, proj)],
        "vector": [(12, pv_beta), (9, q_masks), (12, pv_dve), (13, resid), (5, stats), (9, sigma), (5, aggr),
                   (10, update_dve), (13, stats2), (9, row_max), (9, mem_den), (9, row_sub), (13, aggr2),
                   (5, var_eps), (9, mem_rec), (13, var_eps2), (7, h1t_rest), (9, mem_dve), (6, ln_add), (8, q_rest),
                   (11, pv_scale)],
        "scalar": [(16, h2_act), (11, pt_act), (11, pt_rest), (16, logit_copy), (10, softmax_act), (12, a_act),
                   (7, h1t), (14, rows_hi), (9, sk_act), (8, proj_act), (5, ln_shift), (13, ln2_shift),
                   (13, ln2_act), (5, ln_act)],
        "gpsimd": [(12, a_add), (14, ln2_add), (10, update_add), (6, ln_mult), (10, p_rest), (5, ln_scale),
                   (13, ln2_scale), (9, v_new), (14, rows_lo), (9, v_rest), (13, ln2_mult), (12, res_add)],
    }

    def engine_program(name, e):
        stages = program[name]
        deepest = max(lag for lag, _ in stages)
        periods = -(-deepest // 4)

        def slot(s, j):
            for lag, stage_ in stages:
                ds_, jj = (j - lag) // 4, (j - lag) % 4
                if isinstance(s, int) and not (0 <= 4 * (s + ds_) + jj < NT):
                    continue
                stage_(Tile(e, s + ds_, jj))

        for s in range(periods):
            for j in range(4):
                slot(s, j)
        with e.Fori(periods, NS) as s:
            for j in range(4):
                slot(s, j)
        for s in range(NS, NS + periods):
            for j in range(4):
                slot(s, j)

    owner = {n: "vector" for n in names}
    for n in "T1 pqk pv scr PTr memm skT upm PV AT Wo h2Tr rtr".split():
        owner[n] = "tensor"
    for n in "nmr xn h1T qkh exq rel v32 vhi exp phi ptA ptl skt aT nm2 xn2 hhi h2T lg".split():
        owner[n] = "scalar"
    for n in "pow lna vlo plo vpr aadd res pw2 l2a l2b madd hlo".split():
        owner[n] = "gpsimd"

    with nc.Block() as block:
        def start(name, e):
            for n in names:
                if owner[n] == name:
                    e.sem_inc(S[n], PRE)
            engine_program(name, e)

        @block.sync
        def _(e):
            for j in range(4):
                e.sem_inc(s_st[j], FIRST)
            start("sync", e)
            for j in range(4):
                e.wait_ge(s_st[j], 64 * NS + FIRST)

        @block.tensor
        def _(e):
            start("tensor", e)

        @block.vector
        def _(e):
            start("vector", e)

        @block.scalar
        def _(e):
            start("scalar", e)

        @block.gpsimd
        def _(e):
            start("gpsimd", e)


def experts(nc, ctx, sb_, sem_, banks, trib, iota, count, tok_a, tok_b, out_rows, rows_dram,
            w13s, w13, w2, idh, logits, passed):
    def sb(name, shape, dt=F32):
        return sb_(name, shape, dt, ctx)

    def sem(name):
        return sem_(name, ctx)

    NW = NSLOT_TILES
    w2s = sb("w2s", [P, 2, E * KC * D], F16)
    ex_i = sb("ex_i", [P, NW], I32)
    oh_tile = sb("oh_tile", [P, NW, E])
    gidx, sidx = sb("gidx", [P, NW], I32), sb("sidx", [P, NW], I32)
    routing = ExitStack()

    def scratch(name, shape, dt=F32):
        return sb_(name, shape, dt, routing)

    NSTAGE = 4
    stage = scratch("stage", [P, NSTAGE, 1024])
    work = [scratch(f"work{i}", [P, E, NT]) for i in range(6)]
    oh1, oh2 = scratch("oh1", [P, E, NT]), scratch("oh2", [P, E, NT])
    chosen = scratch("chosen", [P, E, NT], BF16)
    w8 = scratch("w8", [P, NT, E])
    col = [scratch(f"col{i}", [P, NT]) for i in range(8)]
    small = [scratch(f"small{i}", [P, E]) for i in range(6)]
    posi = scratch("posi", [P, 4, 2 * NT], I32)
    tile_of, row_of = scratch("tile_of", [P, NT, 2], F16), scratch("row_of", [P, NT, 2], F16)
    rsel = scratch("rsel", [P, 2, 2, P, NHOT], F16)
    asel = scratch("asel", [P, 2, 2, NW, NHOT], F16)
    cmpx = scratch("cmpx", [P, NW, E])
    ex_of = scratch("ex_of", [P, NW])
    rowf, hasf = scratch("rowf", [P, NW]), scratch("hasf", [P, NW])

    s_v, s_a, s_p, s_w8 = sem("r_v"), sem("r_a"), sem("r_p"), sem("r_w8")
    s_sel, s_use, s_hot = sem("r_sel"), sem("r_use"), sem("r_hot")
    s_wl, s_wh, s_wr = [sem(f"r_wl{i}") for i in range(NSTAGE)], sem("r_wh"), sem("r_wr")
    chunks = [(w13[e_, c * P:(c + 1) * P, :], w13s, (e_ * G + c) * 1024) for e_ in range(E) for c in range(G)]
    chunks += [(w2[e_].rearrange("(k p) n -> p k n", p=P), w2s, e_ * KC * D) for e_ in range(E)]

    with nc.Block() as block:
        n, marks = [0], {}

        @block.sync
        def _(e):
            for i, (src, _, _) in enumerate(chunks):
                if i >= NSTAGE:
                    e.wait_ge(s_wr, i - NSTAGE + 1)
                dst = stage[:, i % NSTAGE, :]
                if len(src.shape) == 3:
                    dst = dst.rearrange("p (k n) -> p k n", k=KC)
                e.dma_start(dst, src).then_inc(s_wl[i % NSTAGE], 16)

        @block.vector
        def _(e):
            def link(ins):
                n[0] += 1
                ins.then_inc(s_v, 1)
                e.wait_ge(s_v, n[0])

            def by_token(ap):
                return ap.rearrange("p e t -> p t e")

            def first_max(lg, m, oh, a, r):
                link(e.tensor_reduce(m[:, :], by_token(lg[:, :, :]), axis=X, op=ALU.max))
                link(e.tensor_tensor(a[:, :, :], lg[:, :, :], bc_mid(m[:, :], E), ALU.is_equal))
                link(e.tensor_tensor(a[:, :, :], a[:, :, :], bc(iota[:, 2, 0:E], NT), ALU.mult))
                link(e.tensor_reduce(r[:, :], by_token(a[:, :, :]), axis=X, op=ALU.max))
                link(e.tensor_tensor(oh[:, :, :], a[:, :, :], bc_mid(r[:, :], E), ALU.is_equal))

            m1, m2, r, z, e2, w1, w2_ = col[0:7]
            first_max(logits, m1, oh1, work[0], r)
            link(e.scalar_tensor_tensor(out=work[1][:, :, :], in0=oh1[:, :, :], scalar=-3e38, in1=logits[:, :, :],
                                        op0=ALU.mult, op1=ALU.add))
            first_max(work[1], m2, oh2, work[0], r)
            link(e.tensor_tensor(chosen[:, :, :], oh1[:, :, :], oh2[:, :, :], ALU.add))
            at_chosen = n[0]
            link(e.tensor_tensor(work[2][:, :, :], logits[:, :, :], bc_mid(m1[:, :], E), ALU.subtract))
            link(e.tensor_tensor(e2[:, :], m2[:, :], m1[:, :], ALU.subtract))
            at_shift = n[0]
            e.wait_ge(s_p, 2)
            before, tot, cum = work[3], work[4], work[5]
            flat = lambda ap: ap[:, :, :].rearrange("p e t -> p (e t)")
            link(e.tensor_copy(flat(before), banks[0][:, :]))
            link(e.tensor_copy(flat(tot), banks[1][:, :]))
            link(e.memset(flat(work[0]), 1.0))
            link(e.tensor_tensor_scan(flat(cum), flat(work[0]), flat(tot), 0.0, ALU.mult, ALU.add))
            start, cnt, tiles, tend, ones8, base = small
            link(e.memset(start[:, 0:1], 0.0))
            link(e.tensor_copy(start[:, 1:E], cum[:, 0:E - 1, NT - 1]))
            link(e.tensor_tensor(cnt[:, :], cum[:, :, NT - 1], start[:, :], ALU.subtract))
            link(e.tensor_tensor(work[0][:, :, :], bc(cnt[:, :], NT), bc_mid(iota[:, 1, 0:NT], E), ALU.is_gt))
            link(e.tensor_reduce(tiles[:, :], work[0][:, :, :], axis=X, op=ALU.add))
            link(e.memset(ones8[:, :], 1.0))
            link(e.tensor_tensor_scan(tend[:, :], ones8[:, :], tiles[:, :], 0.0, ALU.mult, ALU.add))
            link(e.tensor_tensor(base[:, :], tend[:, :], tiles[:, :], ALU.subtract))
            link(e.scalar_tensor_tensor(out=base[:, :], in0=base[:, :], scalar=float(P), in1=start[:, :],
                                        op0=ALU.mult, op1=ALU.subtract))
            link(e.tensor_tensor(flat(cum), flat(cum), flat(tot), ALU.subtract))
            link(e.tensor_tensor(flat(cum), flat(cum), flat(before), ALU.add))
            link(e.tensor_tensor(cum[:, :, :], cum[:, :, :], bc(base[:, :], NT), ALU.add))
            for q, oh in enumerate((oh1, oh2)):
                link(e.tensor_tensor(work[q][:, :, :], oh[:, :, :], cum[:, :, :], ALU.mult))
                link(e.tensor_reduce(col[q][:, :], by_token(work[q][:, :, :]), axis=X, op=ALU.add))
                link(e.tensor_copy(posi[:, 0, q * NT:(q + 1) * NT], col[q][:, :]))
            link(e.tensor_scalar(posi[:, 1, :], posi[:, 0, :], 7, None, ALU.arith_shift_right))
            link(e.tensor_scalar(posi[:, 2, :], posi[:, 0, :], P - 1, None, ALU.bitwise_and))
            link(e.tensor_copy(tile_of[:, :, :].rearrange("p t q -> p q t"),
                               posi[:, 1, :].rearrange("p (q t) -> p q t", q=2)))
            link(e.tensor_copy(row_of[:, :, :].rearrange("p t q -> p q t"),
                               posi[:, 2, :].rearrange("p (q t) -> p q t", q=2)))
            link(e.tensor_tensor(cmpx[:, :, :], bc(iota[:, 0, :], E), bc_mid(tend[:, :], NW), ALU.is_ge))
            link(e.tensor_reduce(ex_of[:, :], cmpx[:, :, :], axis=X, op=ALU.add))
            link(e.tensor_scalar(ex_of[:, :], ex_of[:, :], float(E - 1), None, ALU.min))
            link(e.tensor_copy(ex_i[:, :], ex_of[:, :]))
            link(e.tensor_tensor(oh_tile[:, :, :], bc(ex_of[:, :], E), bc_mid(iota[:, 3, 0:E], NW), ALU.is_equal))
            e.wait_ge(s_a, 2)
            link(e.tensor_reduce(z[:, :], by_token(work[2][:, :, :]), axis=X, op=ALU.add))
            link(e.reciprocal(z[:, :], z[:, :]))
            link(e.tensor_tensor(e2[:, :], e2[:, :], z[:, :], ALU.mult))
            link(e.tensor_tensor(r[:, :], e2[:, :], z[:, :], ALU.add))
            link(e.tensor_scalar(r[:, :], r[:, :], EPS_TOP, None, ALU.add))
            link(e.reciprocal(r[:, :], r[:, :]))
            link(e.tensor_scalar(r[:, :], r[:, :], 1.0 / W_SCALE, None, ALU.mult))
            link(e.tensor_tensor(w1[:, :], z[:, :], r[:, :], ALU.mult))
            link(e.tensor_tensor(w2_[:, :], e2[:, :], r[:, :], ALU.mult))
            link(e.tensor_tensor(work[3][:, :, :], oh1[:, :, :], bc_mid(w1[:, :], E), ALU.mult))
            link(e.tensor_tensor(work[4][:, :, :], oh2[:, :, :], bc_mid(w2_[:, :], E), ALU.mult))
            link(e.tensor_tensor(w8[:, :, :], by_token(work[3][:, :, :]),
                                 by_token(work[4][:, :, :]), ALU.add))
            at_w8 = n[0]
            steps = lambda ap: ap.rearrange("p t q -> p (t q)")
            with e.Fori(0, NT * 2 // NHOT // 2) as i:
                for h in range(2):
                    k = i * 2 + h
                    now = bass.ds(k * NHOT, NHOT)
                    e.wait_ge(s_use, k + 1)
                    e.tensor_tensor(rsel[:, h, 0, :, :], count[:, 0:P, :], bc_mid(steps(row_of[:, :, :])[:, now], P),
                                    ALU.is_equal).then_inc(s_hot, 1)
                    e.tensor_tensor(asel[:, h, 0, :, :], count[:, :, :], bc_mid(steps(tile_of[:, :, :])[:, now], NW),
                                    ALU.is_equal).then_inc(s_hot, 1)
                    e.wait_ge(s_hot, k * 2 + 2)
                    e.tensor_scalar(rsel[:, h, 1, :, :], rsel[:, h, 0, :, :], tok_b[:, :], None, ALU.mult)
                    e.tensor_tensor(asel[:, h, 1, :, :], asel[:, h, 0, :, :], bc_mid(tok_a[:, now], NW),
                                    ALU.mult).then_inc(s_sel, 1)
            e.wait_ge(s_p, 3)
            link(e.tensor_copy(rowf[:, :], banks[2][:, 0:NW]))
            link(e.tensor_scalar(hasf[:, :], rowf[:, :], 0.5, float(-OOB), ALU.is_le, ALU.mult))
            link(e.scalar_tensor_tensor(out=rowf[:, :], in0=rowf[:, :], scalar=float(SEG), in1=banks[3][:, 0:NW],
                                        op0=ALU.mult, op1=ALU.add))
            link(e.tensor_scalar(rowf[:, :], rowf[:, :], float(-SEG), None, ALU.add))
            link(e.tensor_tensor(hasf[:, :], rowf[:, :], hasf[:, :], ALU.subtract))
            link(e.tensor_copy(sidx[:, :], hasf[:, :]))
            link(e.tensor_scalar(rowf[:, :], rowf[:, :], 0.0, None, ALU.max))
            link(e.tensor_copy(gidx[:, :], rowf[:, :]))
            marks.update(chosen=at_chosen, shift=at_shift, w8=at_w8)

        @block.scalar
        def _(e):
            for i, (_, dst, at) in enumerate(chunks):
                if i == 6:
                    e.wait_ge(s_v, marks["shift"])
                    e.activation(work[2][:, :, :], work[2][:, :, :], ACT.Exp).then_inc(s_a, 1)
                    e.activation(col[4][:, :], col[4][:, :], ACT.Exp).then_inc(s_a, 1)
                e.wait_ge(s_wl[i % NSTAGE], 16 * (i // NSTAGE + 1))
                f = stage[:, i % NSTAGE, :]
                e.activation(dst[:, 0, at:at + 1024], f, ACT.Copy, scale=W_SCALE).then_inc(s_wh, 1)
                e.activation(f, f, ACT.Copy, scale=W_SCALE).then_inc(s_wh, 1)

        @block.tensor
        def _(e):
            e.wait_ge(s_v, marks["chosen"])
            moving = chosen[:, :, :].rearrange("p e t -> p (e t)")
            for q in range(2):
                e.matmul(banks[q][:, :], trib[:, q, :], moving, start=True, stop=True).then_inc(s_p, 1)
            e.sem_inc(s_use, 2)

            def add(k, h, first=False, last=False):
                e.wait_ge(s_sel, k + 1)
                for q in range(NHOT):
                    at_end = dict(start=first and q == 0, stop=last and q == NHOT - 1)
                    e.matmul(banks[2][:, 0:NW], rsel[:, h, 0, :, q], asel[:, h, 1, :, q], **at_end)
                    mm = e.matmul(banks[3][:, 0:NW], rsel[:, h, 1, :, q], asel[:, h, 0, :, q], **at_end)
                return mm

            nk = NT * 2 // NHOT
            for k in range(2):
                add(k, k, first=(k == 0)).then_inc(s_use, 1)
            with e.Fori(1, nk // 2 - 1) as i:
                for h in range(2):
                    add(i * 2 + h, h).then_inc(s_use, 1)
            for k in range(2):
                mm = add(nk - 2 + k, k, last=(k == 1))
            mm.then_inc(s_p, 1)

        @block.gpsimd
        def _(e):
            for i, (_, dst, at) in enumerate(chunks):
                e.wait_ge(s_wh, 2 * i + 2)
                e.tensor_tensor(dst[:, 1, at:at + 1024], stage[:, i % NSTAGE, :], dst[:, 0, at:at + 1024],
                                ALU.subtract).then_inc(s_wr, 1)
            e.wait_ge(s_v, marks["w8"])
            for j in range(NJ):
                for b2 in range(2):
                    dst = rows_dram[(2 * j + b2) * T:(2 * j + b2 + 1) * T, 2 * D:ROW].rearrange(
                        "(s t) e -> t s e", t=SEG)
                    src = w8[b2 * SEG:(b2 + 1) * SEG, :, :].rearrange("p (s j) e -> p j s e", j=NJ)[:, j]
                    e.dma_start(dst, src).then_inc(s_w8, 16)
            e.wait_ge(s_w8, 16 * B)

    routing.close()

    U = 8
    gi, si = sb("gi", [P, U, 1], I32), sb("si", [P, U, 1], I32)
    grow = sb("grow", [P, U, ROW])
    gwm = sb("gwm", [P, 2, E])
    wrow = sb("wrow", [P, 2, 1])
    xT = sb("xT", [P, 2, 2, G, P], F16)
    sg = sb("sg", [P, 2, I])
    hf = sb("hf", [P, 2, I])
    hs = sb("hs", [P, 2, 2, I], F16)
    hT = sb("hT", [P, 2, 2, KC, P], F16)
    yo = sb("yo", [P, U, D])

    names = "cpi xTr xT gu sg hm hhi hlo hTr hT y wm ws yw".split()
    S = {m: sem("f_" + m) for m in names}
    s_g = [sem(f"f_row{i}") for i in range(U)]
    s_sc = [sem(f"f_add{i}") for i in range(U)]
    s_init = sem("f_init")
    bGate, bUp, bY, bH, bX = banks[0:2], banks[2:4], banks[4:6], banks[6], banks[7]
    bHh = bH[:, :].bitcast(F16)
    bXh = bX[:, :].bitcast(F16)

    class Slot:
        def __init__(self, e, s, j):
            self.e, self.s, self.j, self.b = e, s, j, j % 2
            self.t = s * U + j

        def when(self, stage, back=0):
            if isinstance(self.s, int):
                of = min(self.t - back, NW - 1)
                return S[stage], max(of, -1) + 1 + PRE
            return S[stage], self.s * U + (self.j - back + 1 + PRE)

        def wait(self, stage, back=0):
            if not isinstance(self.s, int) or self.t >= back:
                self.e.wait_ge(*self.when(stage, back))

        def wait_apart(self, *stages):
            apart(self.e, passed, [self.when(*w) for w in stages])

        def added(self, back):
            s, j = self.s + (self.j - back) // U, (self.j - back) % U
            return s_sc[j], (max(s, -1) if isinstance(s, int) else s) * 16 + 16

        def wait_added(self, back):
            if not isinstance(self.s, int) or self.t >= back:
                self.e.wait_ge(*self.added(back))

        def arrived(self, sems, back=0):
            s, j = self.s + (self.j - back) // U, (self.j - back) % U
            if not isinstance(s, int) or s >= 0:
                self.e.wait_ge(sems[j], s * 16 + 16)

    def done(ins, stage):
        ins.then_inc(S[stage], 1)

    def gather(k):
        k.wait_apart(("cpi",), ("yw", U))
        at = bass.IndirectOffsetOnAxis(ap=gi[:, k.j, :], axis=0)
        k.e.indirect_dma_start(grow[:, k.j, :], None, rows_dram, at).then_inc(s_g[k.j], 16)

    def indices(k):
        k.arrived(s_g, U)
        k.wait_added(U)
        k.e.tensor_copy(gi[:, k.j, :], gidx[:, bass.ds(k.t, 1)])
        done(k.e.tensor_copy(si[:, k.j, :], sidx[:, bass.ds(k.t, 1)]), "cpi")

    def x_trans(k):
        k.arrived(s_g)
        k.wait("xT", 1)
        halves = grow[:, k.j, 0:D].bitcast(F16)
        for a in range(2):
            for c in range(G):
                i = k.e.transpose(bXh[:, (a * G + c) * P:(a * G + c + 1) * P],
                                  halves[:, (a * G + c) * P:(a * G + c + 1) * P], idh[:, :])
        done(i, "xTr")

    def x_copy(k):
        k.wait("xTr")
        k.wait("gu", 2)
        done(k.e.tensor_copy(xT[:, k.b, :, :, :].rearrange("p a c t -> p (a c t)"), bXh[:, 0:2 * D]), "xT")

    def gate_up(k):
        k.wait_apart(("xT",), ("hm", 2))
        ex_reg = k.e.value_load(ex_i[0:1, bass.ds(k.t, 1)], min_val=0, max_val=E - 1)
        for c in range(G):
            for a, b_ in PARTS:
                for bank, at in ((bGate[k.b], 0), (bUp[k.b], I)):
                    i = k.e.matmul(bank[:, :], xT[:, k.b, a, c, :],
                                   w13s[:, b_, bass.ds(ex_reg * (G * 2 * I) + (c * 2 * I + at), I)],
                                   start=(c == 0 and (a, b_) == PARTS[0]),
                                   stop=(c == G - 1 and (a, b_) == PARTS[-1]))
        done(i, "gu")

    def silu(k):
        k.wait("gu")
        k.wait("hm", 2)
        done(k.e.activation(sg[:, k.b, :], bGate[k.b][:, :], ACT.Silu, scale=1.0 / W_SCALE), "sg")

    def h_mul(k):
        k.wait("sg")
        k.wait("hhi", 2)
        k.wait("hlo", 2)
        done(k.e.scalar_tensor_tensor(out=hf[:, k.b, :], in0=bUp[k.b][:, :], scalar=1.0 / W_SCALE, in1=sg[:, k.b, :],
                                      op0=ALU.mult, op1=ALU.mult), "hm")

    def h_hi(k):
        k.wait("hm")
        k.wait("hTr", 2)
        k.wait("hlo", 2)
        done(k.e.activation(hs[:, k.b, 0, :], hf[:, k.b, :], ACT.Copy), "hhi")

    def h_lo(k):
        k.wait("hhi")
        k.wait("hTr", 2)
        done(k.e.tensor_tensor(hs[:, k.b, 1, :], hf[:, k.b, :], hs[:, k.b, 0, :], ALU.subtract), "hlo")

    def h_trans(k):
        k.wait("hlo")
        k.wait("hT", 1)
        for a in range(2):
            for c in range(KC):
                i = k.e.transpose(bHh[:, (a * KC + c) * P:(a * KC + c + 1) * P],
                                  hs[:, k.b, a, c * P:(c + 1) * P], idh[:, :])
        done(i, "hTr")

    def h_copy(k):
        k.wait("hTr")
        k.wait("y", 2)
        done(k.e.tensor_copy(hT[:, k.b, :, :, :].rearrange("p a c t -> p (a c t)"), bHh[:, :]), "hT")

    def down(k):
        k.wait_apart(("hT",), ("yw", 2))
        ex_reg = k.e.value_load(ex_i[0:1, bass.ds(k.t, 1)], min_val=0, max_val=E - 1)
        for c in range(KC):
            for a, b_ in PARTS:
                i = k.e.matmul(bY[k.b][:, 0:D], hT[:, k.b, a, c, :], w2s[:, b_, bass.ds(ex_reg * (KC * D) + c * D, D)],
                               start=(c == 0 and (a, b_) == PARTS[0]), stop=(c == KC - 1 and (a, b_) == PARTS[-1]))
        done(i, "y")

    def weigh(k):
        k.arrived(s_g)
        k.wait("ws", 2)
        done(k.e.tensor_tensor(gwm[:, k.b, :], grow[:, k.j, 2 * D:ROW],
                               oh_tile[:, bass.ds(k.t, 1), :].rearrange("p o e -> p (o e)"), ALU.mult), "wm")
        k.wait("wm")
        k.wait("yw", 2)
        done(k.e.tensor_reduce(wrow[:, k.b, :], gwm[:, k.b, :], axis=X, op=ALU.add), "ws")
        k.wait("y")
        k.wait("ws")
        k.arrived(s_g)
        k.wait_added(U)
        done(k.e.scalar_tensor_tensor(out=yo[:, k.j, :], in0=bY[k.b][:, 0:D], scalar=wrow[:, k.b, :],
                                      in1=grow[:, k.j, D:2 * D], op0=ALU.mult, op1=ALU.mult), "yw")

    def scatter(k):
        apart(k.e, passed, [k.when("yw"), k.added(1)])
        k.e.indirect_dma_start(out_rows, bass.IndirectOffsetOnAxis(ap=si[:, k.j, :], axis=0), yo[:, k.j, :], None,
                               bounds_check=B * T - 1, oob_is_err=False, compute_op=ALU.add).then_inc(s_sc[k.j], 16)

    program = {
        "tensor": [(2, x_trans), (3, gate_up), (4, h_trans), (5, down)],
        "vector": [(0, indices), (6, weigh), (2, x_copy), (4, h_copy), (3, h_mul), (3, h_lo)],
        "scalar": [(3, silu), (3, h_hi)],
        "gpsimd": [(0, gather), (6, scatter)],
    }
    owner = {m: "vector" for m in names}
    owner.update({m: "tensor" for m in "xTr gu hTr y".split()})
    owner.update({m: "scalar" for m in "sg hhi".split()})

    with nc.Block() as block:
        def engine_program(name, e):
            for m in names:
                if owner[m] == name:
                    e.sem_inc(S[m], PRE)
            stages = program[name]
            periods = -(-max(lag for lag, _ in stages) // U) + 1

            def slot(s, j):
                for lag, stage_ in stages:
                    back, jj = (j - lag) // U, (j - lag) % U
                    if isinstance(s, int) and not (0 <= U * (s + back) + jj < NW):
                        continue
                    stage_(Slot(e, s + back, jj))

            for s in range(periods):
                for j in range(U):
                    slot(s, j)
            with e.Fori(periods, NW // U) as s:
                for j in range(U):
                    slot(s, j)
            for s in range(NW // U, (NW - 1) // U + 1 + periods):
                for j in range(U):
                    slot(s, j)

        @block.tensor
        def _(e):
            engine_program("tensor", e)

        @block.vector
        def _(e):
            engine_program("vector", e)

        @block.scalar
        def _(e):
            engine_program("scalar", e)

        @block.gpsimd
        def _(e):
            engine_program("gpsimd", e)
            for i in range(U):
                e.wait_ge(s_sc[i], 16 * (-(-(NW - i) // U)))


def constants():
    bf16 = mybir.dt.to_np(BF16) if hasattr(mybir.dt, "to_np") else np.dtype("bfloat16")
    p = np.arange(P)
    head = p // DK
    block = (head[:, None] == head[None, :]).astype(np.float32)
    onto = (head[:, None] == np.arange(HG)[None, :]).astype(np.float32)
    causal = np.where(np.arange(SEG)[None, :] > (p % SEG)[:, None], np.float32(NEG), np.float32(0))
    n = np.arange(NSLOT_TILES)
    t = np.arange(NT)
    return dict(
        ident=np.eye(P, dtype=np.float32),
        head_of_row=((head % 4)[:, None] == np.arange(4)[None, :]).astype(np.float32),
        mem_mask=np.tile(np.concatenate([block, onto], 1)[:, None], (1, G, 1)),
        q_onehot=((p % SEG)[:, None] == (p % SEG)[None, :]).astype(bf16),
        causal=np.tile(causal, (1, 8)).astype(bf16),
        tri=np.stack([(p[:, None] < p[None, :]), np.ones((P, P), bool)], 1).astype(bf16),
        iotas=np.broadcast_to(np.stack([n, P * n, E - n, n]).astype(np.float32), (P, 4, NSLOT_TILES)).copy(),
        counting=np.broadcast_to(n.astype(np.float16)[:, None], (P, NSLOT_TILES, NHOT)).copy(),
        token_a=np.broadcast_to(((2 * (t % NJ)) * (T // SEG) + t // NJ + 1).astype(np.float16)[:, None],
                                (P, NT, 2)).reshape(P, 2 * NT).copy(),
        token_b=((p // SEG) * T + p % SEG).astype(np.float32)[:, None],
        rows_of_batch=(np.arange(B)[:, None, None] == 2 * np.arange(NJ)[:, None] + p // SEG).astype(np.float16),
    )


def kernel(**inputs):
    import concourse.bacc as bacc
    from concourse.bass_utils import run_bass_kernel_spmd

    a = {k[3:]: np.asarray(v) for k, v in inputs.items()}
    c = np.ascontiguousarray
    data = dict(
        x=a["attn_x"], cT=c(a["c"].T), wmod=a["wmod"], wqT=c(a["attn_W_q"].T), wkT=c(a["attn_W_k"].T),
        wvT=c(a["attn_W_v"].T), woT=c(a["attn_W_o"].T), beta=a["attn_beta_param"], rwT=c(a["ffn_router_w"].T),
        w13=a["ffn_w13"], w2=a["ffn_w2"], **constants(),
    )
    nc = bacc.Bacc("TRN2", target_bir_lowering=False, num_devices=1)
    arrays, args = {}, {}
    for name, v in data.items():
        arrays[f"in_{name}"] = v
        args[name] = nc.dram_tensor(f"in_{name}", v.shape, mybir.dt.from_np(v.dtype), kind="ExternalInput").ap()
    out = nc.dram_tensor("out", [B, T, D], F32, kind="ExternalOutput").ap()
    adaln_block(nc, out=out, **args)
    r = run_bass_kernel_spmd(nc, [arrays], core_ids=[0])
    return r.results[0]["out"]
```
